# Optimizing a Trainium2 kernel written in Bass

```python
import numpy as np
import jax
import jax.numpy as jnp

def _softmax(x, axis=-1):
    return jax.nn.softmax(x, axis=axis)

def _gelu(x):
    return jax.nn.gelu(x, approximate=True)

def _silu(x):
    return jax.nn.silu(x)

def _sigmoid(x):
    return jax.nn.sigmoid(x)

def _layernorm(x, axis=-1, eps=1e-05):
    m = jnp.mean(x, axis=axis, keepdims=True)
    v = jnp.var(x, axis=axis, keepdims=True)
    return (x - m) / jnp.sqrt(v + eps)

def _scatter_add(tgt, idx, src, axis=0):
    return tgt.at[idx].add(src)

def _segment_sum(src, seg, n):
    return jax.ops.segment_sum(src, seg, n)
kernel_name = 'mk_sandwich_d2_jaxref_r8_11ab31'

def setup_inputs(seed: int=0):
    np.random.seed(seed)
    _w = jnp.asarray

    def _L0_attn_setup():
        import math
        import jax, jax.numpy as jnp
        import numpy as np
        D_MODEL = 512
        N_HEADS = 32
        N_KV_HEADS = 8
        D_HEAD = D_MODEL // N_HEADS
        GROUP = N_HEADS // N_KV_HEADS
        ROPE = dict(rope_theta=500000.0, factor=32.0, hi_freq_factor=4.0, lo_freq_factor=1.0, original_context_length=1024)

        def _rope_cos_sin(head_dim, pos, dtype):
            idx = jnp.arange(0, head_dim, 2, dtype=jnp.float32) / head_dim
            freq = 1.0 / (2.0 * math.pi) * ROPE['rope_theta'] ** (-idx)
            factor, lo, hi = (ROPE['factor'], ROPE['lo_freq_factor'], ROPE['hi_freq_factor'])
            L0 = ROPE['original_context_length']
            freq_low, freq_high = (lo / L0, hi / L0)
            freq_scaled = jnp.where(freq < freq_low, freq / factor, freq)
            smooth = jnp.clip((L0 * freq - lo) / (hi - lo), 0.0, 1.0)
            freq_smooth = (1.0 - smooth) * (freq / factor) + smooth * freq
            is_mid = (freq >= freq_low) & (freq <= freq_high)
            freq = jnp.where(is_mid, freq_smooth, freq_scaled)
            phase = 2.0 * math.pi * pos.astype(jnp.float32)[:, None] * freq[None, :]
            emb = jnp.concatenate([phase, phase], axis=-1)
            return (jnp.cos(emb).astype(dtype), jnp.sin(emb).astype(dtype))

        def _rotate_half(x):
            h = x.shape[-1] // 2
            return jnp.concatenate([-x[..., h:], x[..., :h]], axis=-1)
        key = jax.random.key(seed)
        ks = jax.random.split(key, 5)
        B, T = (1, 256)
        s = 0.02
        return {'resid': jax.random.normal(ks[0], (B, T, D_MODEL), jnp.float32), 'Wq': jax.random.normal(ks[1], (D_MODEL, D_MODEL), jnp.float32) * s, 'Wk': jax.random.normal(ks[2], (D_MODEL, N_KV_HEADS * D_HEAD), jnp.float32) * s, 'Wv': jax.random.normal(ks[3], (D_MODEL, N_KV_HEADS * D_HEAD), jnp.float32) * s, 'Wo': jax.random.normal(ks[4], (D_MODEL, D_MODEL), jnp.float32) * s}
    _L0_attn_in = _L0_attn_setup()

    def _L0_ffn_setup():
        import jax, jax.numpy as jnp
        import numpy as np
        HIDDEN = 512
        INTER = 1376
        GROUP = 128
        B, S = (4, 256)
        NIB = jnp.uint32(15)

        def _pack_rows(nib):
            r = nib.reshape(-1, 8, nib.shape[-1])
            shifts = (jnp.arange(8, dtype=jnp.uint32) * 4)[None, :, None]
            return jnp.sum(r << shifts, axis=1, dtype=jnp.uint32)

        def _pack_cols(nib):
            r = nib.reshape(nib.shape[0], -1, 8)
            shifts = (jnp.arange(8, dtype=jnp.uint32) * 4)[None, None, :]
            return jnp.sum(r << shifts, axis=2, dtype=jnp.uint32)

        def _dequant(qw, qz, sc, g_idx):
            shifts = jnp.arange(8, dtype=jnp.uint32) * 4
            wq = qw[:, None, :] >> shifts[None, :, None] & NIB
            wq = wq.reshape(-1, qw.shape[1]).astype(jnp.float32)
            zq = qz[:, :, None] >> shifts[None, None, :] & NIB
            zq = zq.reshape(qz.shape[0], -1).astype(jnp.float32) + 1.0
            return sc[g_idx] * (wq - zq[g_idx])
        key = jax.random.key(seed)
        ks = jax.random.split(key, 7)
        n_groups = HIDDEN // GROUP
        n_groups_d = INTER // GROUP
        x = jax.random.normal(ks[0], (B, S, HIDDEN), jnp.float32)
        nib_w_gu = jax.random.randint(ks[1], (HIDDEN, 2 * INTER), 0, 16).astype(jnp.uint32)
        nib_z_gu = jax.random.randint(ks[2], (n_groups, 2 * INTER), 0, 15).astype(jnp.uint32)
        qweight_gu = _pack_rows(nib_w_gu)
        qzeros_gu = _pack_cols(nib_z_gu)
        scales_gu = jax.random.uniform(ks[3], (n_groups, 2 * INTER), jnp.float32, 0.005, 0.02)
        g_idx_gu = jnp.arange(HIDDEN, dtype=jnp.int32) // GROUP
        nib_w_d = jax.random.randint(ks[4], (INTER, HIDDEN), 0, 16).astype(jnp.uint32)
        nib_z_d = jax.random.randint(ks[5], (n_groups_d, HIDDEN), 0, 15).astype(jnp.uint32)
        qweight_down = _pack_rows(nib_w_d)
        qzeros_down = _pack_cols(nib_z_d)
        scales_down = jax.random.uniform(ks[6], (n_groups_d, HIDDEN), jnp.float32, 0.005, 0.02)
        g_idx_down = jnp.arange(INTER, dtype=jnp.int32) // GROUP
        return {'x': x, 'qweight_gu': qweight_gu, 'qzeros_gu': qzeros_gu, 'scales_gu': scales_gu, 'g_idx_gu': g_idx_gu, 'qweight_down': qweight_down, 'qzeros_down': qzeros_down, 'scales_down': scales_down, 'g_idx_down': g_idx_down}
    _L0_ffn_in = _L0_ffn_setup()

    def _L1_attn_setup():
        import jax, jax.numpy as jnp
        import numpy as np
        NUM_HEADS = 32
        NUM_KV_HEADS = 8
        HEAD_DIM = 128
        key = jax.random.key(seed)
        ks = jax.random.split(key, 5)
        B, S, H = (2, 256, 512)
        Dq = NUM_HEADS * HEAD_DIM
        Dkv = NUM_KV_HEADS * HEAD_DIM
        return {'hidden_states': jax.random.normal(ks[0], (B, S, H), jnp.float32), 'w_q': jax.random.normal(ks[1], (H, Dq), jnp.float32) * 0.02, 'w_k': jax.random.normal(ks[2], (H, Dkv), jnp.float32) * 0.02, 'w_v': jax.random.normal(ks[3], (H, Dkv), jnp.float32) * 0.02, 'w_o': jax.random.normal(ks[4], (Dq, H), jnp.float32) * 0.02}
    _L1_attn_in = _L1_attn_setup()

    def _L1_ffn_setup():
        import jax, jax.numpy as jnp
        import numpy as np
        B, S, D, O, E, R = (2, 512, 512, 512, 8, 16)
        TOP_K = 2
        SCALING = 32.0 / 16.0
        key = jax.random.key(seed)
        k = jax.random.split(key, 6)
        x = jax.random.normal(k[0], (B, S, D), dtype=jnp.float32)
        W_base = jax.random.normal(k[1], (O, D), dtype=jnp.float32) * 0.02
        b_base = jax.random.normal(k[2], (O,), dtype=jnp.float32) * 0.02
        W_router = jax.random.normal(k[3], (E, D), dtype=jnp.float32) * 0.01
        lora_A = jax.random.normal(k[4], (E, R, D), dtype=jnp.float32) * (1.0 / np.sqrt(D))
        lora_B = jax.random.normal(k[5], (E, O, R), dtype=jnp.float32) * 0.02
        return {'x': x, 'W_base': W_base, 'b_base': b_base, 'W_router': W_router, 'lora_A': lora_A, 'lora_B': lora_B}
    _L1_ffn_in = _L1_ffn_setup()
    _d = {'L0_attn_resid': _L0_attn_in['resid'], 'L0_attn_Wq': _L0_attn_in['Wq'], 'L0_attn_Wk': _L0_attn_in['Wk'], 'L0_attn_Wv': _L0_attn_in['Wv'], 'L0_attn_Wo': _L0_attn_in['Wo'], 'L0_ffn_qweight_gu': _L0_ffn_in['qweight_gu'], 'L0_ffn_qzeros_gu': _L0_ffn_in['qzeros_gu'], 'L0_ffn_scales_gu': _L0_ffn_in['scales_gu'], 'L0_ffn_g_idx_gu': _L0_ffn_in['g_idx_gu'], 'L0_ffn_qweight_down': _L0_ffn_in['qweight_down'], 'L0_ffn_qzeros_down': _L0_ffn_in['qzeros_down'], 'L0_ffn_scales_down': _L0_ffn_in['scales_down'], 'L0_ffn_g_idx_down': _L0_ffn_in['g_idx_down'], 'L1_attn_w_q': _L1_attn_in['w_q'], 'L1_attn_w_k': _L1_attn_in['w_k'], 'L1_attn_w_v': _L1_attn_in['w_v'], 'L1_attn_w_o': _L1_attn_in['w_o'], 'L1_ffn_W_base': _L1_ffn_in['W_base'], 'L1_ffn_b_base': _L1_ffn_in['b_base'], 'L1_ffn_W_router': _L1_ffn_in['W_router'], 'L1_ffn_lora_A': _L1_ffn_in['lora_A'], 'L1_ffn_lora_B': _L1_ffn_in['lora_B']}
    _x0 = _d['L0_attn_resid']
    _d['L0_attn_resid'] = jax.random.normal(jax.random.fold_in(jax.random.key(seed), 1), (1, 1024, 512), dtype=_x0.dtype)
    del _x0
    return _d

def reference(L0_attn_resid, L0_attn_Wq, L0_attn_Wk, L0_attn_Wv, L0_attn_Wo, L0_ffn_qweight_gu, L0_ffn_qzeros_gu, L0_ffn_scales_gu, L0_ffn_g_idx_gu, L0_ffn_qweight_down, L0_ffn_qzeros_down, L0_ffn_scales_down, L0_ffn_g_idx_down, L1_attn_w_q, L1_attn_w_k, L1_attn_w_v, L1_attn_w_o, L1_ffn_W_base, L1_ffn_b_base, L1_ffn_W_router, L1_ffn_lora_A, L1_ffn_lora_B):

    def _L0_attn_ref(resid, Wq, Wk, Wv, Wo):
        import math
        import jax, jax.numpy as jnp
        import numpy as np
        D_MODEL = 512
        N_HEADS = 32
        N_KV_HEADS = 8
        D_HEAD = D_MODEL // N_HEADS
        GROUP = N_HEADS // N_KV_HEADS
        ROPE = dict(rope_theta=500000.0, factor=32.0, hi_freq_factor=4.0, lo_freq_factor=1.0, original_context_length=1024)

        def _rope_cos_sin(head_dim, pos, dtype):
            idx = jnp.arange(0, head_dim, 2, dtype=jnp.float32) / head_dim
            freq = 1.0 / (2.0 * math.pi) * ROPE['rope_theta'] ** (-idx)
            factor, lo, hi = (ROPE['factor'], ROPE['lo_freq_factor'], ROPE['hi_freq_factor'])
            L0 = ROPE['original_context_length']
            freq_low, freq_high = (lo / L0, hi / L0)
            freq_scaled = jnp.where(freq < freq_low, freq / factor, freq)
            smooth = jnp.clip((L0 * freq - lo) / (hi - lo), 0.0, 1.0)
            freq_smooth = (1.0 - smooth) * (freq / factor) + smooth * freq
            is_mid = (freq >= freq_low) & (freq <= freq_high)
            freq = jnp.where(is_mid, freq_smooth, freq_scaled)
            phase = 2.0 * math.pi * pos.astype(jnp.float32)[:, None] * freq[None, :]
            emb = jnp.concatenate([phase, phase], axis=-1)
            return (jnp.cos(emb).astype(dtype), jnp.sin(emb).astype(dtype))

        def _rotate_half(x):
            h = x.shape[-1] // 2
            return jnp.concatenate([-x[..., h:], x[..., :h]], axis=-1)
        B, T, _ = resid.shape
        q = (resid @ Wq).reshape(B, T, N_HEADS, D_HEAD).transpose(0, 2, 1, 3)
        k = (resid @ Wk).reshape(B, T, N_KV_HEADS, D_HEAD).transpose(0, 2, 1, 3)
        v = (resid @ Wv).reshape(B, T, N_KV_HEADS, D_HEAD).transpose(0, 2, 1, 3)
        cos, sin = _rope_cos_sin(D_HEAD, jnp.arange(T), resid.dtype)
        cos = cos[None, None]
        sin = sin[None, None]
        q = q * cos + _rotate_half(q) * sin
        k = k * cos + _rotate_half(k) * sin
        qg = q.reshape(B, N_KV_HEADS, GROUP, T, D_HEAD)
        att = jnp.einsum('bhgqd,bhkd->bhgqk', qg.astype(jnp.float32), k.astype(jnp.float32)) / math.sqrt(D_HEAD)
        causal = jnp.tril(jnp.ones((T, T), dtype=bool))
        att = jnp.where(causal[None, None, None], att, -jnp.inf)
        probs = jax.nn.softmax(att, axis=-1).astype(resid.dtype)
        ctx = jnp.einsum('bhgqk,bhkd->bhgqd', probs, v)
        out = ctx.reshape(B, N_HEADS, T, D_HEAD).transpose(0, 2, 1, 3).reshape(B, T, D_MODEL)
        return out @ Wo

    def _L0_ffn_ref(x, qweight_gu, qzeros_gu, scales_gu, g_idx_gu, qweight_down, qzeros_down, scales_down, g_idx_down):
        import jax, jax.numpy as jnp
        import numpy as np
        HIDDEN = 512
        INTER = 1376
        GROUP = 128
        B, S = (4, 256)
        NIB = jnp.uint32(15)

        def _pack_rows(nib):
            r = nib.reshape(-1, 8, nib.shape[-1])
            shifts = (jnp.arange(8, dtype=jnp.uint32) * 4)[None, :, None]
            return jnp.sum(r << shifts, axis=1, dtype=jnp.uint32)

        def _pack_cols(nib):
            r = nib.reshape(nib.shape[0], -1, 8)
            shifts = (jnp.arange(8, dtype=jnp.uint32) * 4)[None, None, :]
            return jnp.sum(r << shifts, axis=2, dtype=jnp.uint32)

        def _dequant(qw, qz, sc, g_idx):
            shifts = jnp.arange(8, dtype=jnp.uint32) * 4
            wq = qw[:, None, :] >> shifts[None, :, None] & NIB
            wq = wq.reshape(-1, qw.shape[1]).astype(jnp.float32)
            zq = qz[:, :, None] >> shifts[None, None, :] & NIB
            zq = zq.reshape(qz.shape[0], -1).astype(jnp.float32) + 1.0
            return sc[g_idx] * (wq - zq[g_idx])
        w_gu = _dequant(qweight_gu, qzeros_gu, scales_gu, g_idx_gu)
        inter = jnp.einsum('bsh,hf->bsf', x, w_gu)
        gate, up = (inter[..., :INTER], inter[..., INTER:])
        h = jax.nn.silu(gate) * up
        w_d = _dequant(qweight_down, qzeros_down, scales_down, g_idx_down)
        return jnp.einsum('bsf,fh->bsh', h, w_d)

    def _L1_attn_ref(hidden_states, w_q, w_k, w_v, w_o):
        import jax, jax.numpy as jnp
        import numpy as np
        NUM_HEADS = 32
        NUM_KV_HEADS = 8
        HEAD_DIM = 128
        B, S, _ = hidden_states.shape
        Hq, Hkv, D = (NUM_HEADS, NUM_KV_HEADS, HEAD_DIM)
        g = Hq // Hkv
        scale = D ** (-0.5)
        q = (hidden_states @ w_q).reshape(B, S, Hkv, g, D)
        k = (hidden_states @ w_k).reshape(B, S, Hkv, D)
        v = (hidden_states @ w_v).reshape(B, S, Hkv, D)
        scores = jnp.einsum('bqhgd,bkhd->bhgqk', q, k) * scale
        causal = jnp.tril(jnp.ones((S, S), dtype=bool))
        scores = jnp.where(causal, scores, -jnp.inf)
        probs = jax.nn.softmax(scores.astype(jnp.float32), axis=-1).astype(q.dtype)
        attn = jnp.einsum('bhgqk,bkhd->bqhgd', probs, v)
        attn = attn.reshape(B, S, Hq * D)
        return attn @ w_o

    def _L1_ffn_ref(x, W_base, b_base, W_router, lora_A, lora_B):
        import jax, jax.numpy as jnp
        import numpy as np
        B, S, D, O, E, R = (2, 512, 512, 512, 8, 16)
        TOP_K = 2
        SCALING = 32.0 / 16.0
        d = x.shape[-1]
        n_experts = W_router.shape[0]
        xf = x.reshape(-1, d)
        logits = xf @ W_router.T
        probs = jax.nn.softmax(logits, axis=-1)
        topk_p, topk_i = jax.lax.top_k(probs, TOP_K)
        topk_p = topk_p / jnp.sum(topk_p, axis=-1, keepdims=True)
        w = jnp.sum(jax.nn.one_hot(topk_i, n_experts, dtype=xf.dtype) * topk_p[..., None], axis=1)
        h = jnp.einsum('td,erd->ter', xf, lora_A)
        lora_out = jnp.einsum('ter,eor,te->to', h, lora_B, w) * SCALING
        base = x @ W_base.T + b_base
        return base + lora_out.reshape(x.shape[:-1] + (W_base.shape[0],))
    x = L0_attn_resid
    x = x + _layernorm(_L0_attn_ref(_layernorm(x, axis=-1), L0_attn_Wq, L0_attn_Wk, L0_attn_Wv, L0_attn_Wo), axis=-1)
    x = x + _layernorm(_L0_ffn_ref(_layernorm(x, axis=-1), L0_ffn_qweight_gu, L0_ffn_qzeros_gu, L0_ffn_scales_gu, L0_ffn_g_idx_gu, L0_ffn_qweight_down, L0_ffn_qzeros_down, L0_ffn_scales_down, L0_ffn_g_idx_down), axis=-1)
    x = x + _layernorm(_L1_attn_ref(_layernorm(x, axis=-1), L1_attn_w_q, L1_attn_w_k, L1_attn_w_v, L1_attn_w_o), axis=-1)
    x = x + _layernorm(_L1_ffn_ref(_layernorm(x, axis=-1), L1_ffn_W_base, L1_ffn_b_base, L1_ffn_W_router, L1_ffn_lora_A, L1_ffn_lora_B), axis=-1)
    return x

_drawn_inputs = setup_inputs


def setup_inputs(seed=0):
    import zlib

    import numpy as np

    out = dict(_drawn_inputs(seed))
    spreads = {}
    factors = {'L1_ffn_b_base': 3.123}
    for name, (base, spread) in spreads.items():
        noise = np.random.default_rng([zlib.crc32(name.encode()), seed]).standard_normal(out[name].shape)
        drawn = base * np.exp(spread * noise) if base else spread * noise
        out[name] = jnp.asarray(drawn.astype(out[name].dtype))
    for name, factor in factors.items():
        out[name] = (out[name] * factor).astype(out[name].dtype)
    return out
```

```python
from contextlib import ExitStack, contextmanager

import concourse.bass as bass
import concourse.mybir as mybir

F32 = mybir.dt.float32
F32R = mybir.dt.float32r
I32 = mybir.dt.int32
U32 = mybir.dt.uint32
ALU = mybir.AluOpType
ACT = mybir.ActivationFunctionType
AX = mybir.AxisListType

P = 128
T = 1024
D = 512
KT = D // P
TB = T // P
HALF = 512
EPS = 1e-5
MASKED = 1e30

HEADS = 32
KV = 8
GH = HEADS // KV
DH0 = D // HEADS
DH1 = 128

INTER = 1376
NIBBLES = 8
GU_GROUPS = 4
DN_GROUPS = INTER // 128
FT = -(-INTER // P)
F_LAST = INTER - (FT - 1) * P

EXPERTS = 8
RANK = 16
LORA_SCALE = 2.0


class Core:

    def __init__(self, nc, ctx):
        self.nc, self.own = nc, []
        self.banks = [ctx.enter_context(nc.psum_tensor(f"bank{i}", [P, HALF], F32)) for i in range(4)]
        self.slots = [ctx.enter_context(nc.psum_tensor(f"slot{i}", [P, 2 * HALF], F32)) for i in range(2)]

    def sem(self, name):
        handle = self.nc.alloc_semaphore(name=name)
        self.own.append(handle)
        return handle

    @contextmanager
    def stage(self, name):
        before, self.own = self.own, []
        with ExitStack() as ctx:
            yield lambda n, shape, dt=F32: ctx.enter_context(self.nc.sbuf_tensor(f"{name}_{n}", shape, dt))
            self.nc.clear_and_free_semaphores(self.own)
            self.nc.all_engine_barrier()
        self.own = before


def constants(core, tensors, ident_d, mask_d):
    nc = core.nc
    ident, mask, eps, ones = tensors
    loaded = core.sem("const_loaded")
    set_ = core.sem("const_set")
    with nc.Block() as block:

        @block.sync
        def _(sp):
            sp.dma_start(ident[:, :], ident_d).then_inc(loaded, 16)
            sp.dma_start(mask[:, :], mask_d).then_inc(loaded, 16)
            sp.wait_ge(loaded, 32)

        @block.vector
        def _(dve):
            dve.memset(eps[:, :], EPS).then_inc(set_, 1)
            dve.memset(ones[:, :], 1.0).then_inc(set_, 1)
            dve.wait_ge(set_, 2)


def seam(core, name, consts, acc, xh, xl, x_src, x_dst, residual, last):
    nc = core.nc
    ident, mask, eps, ones = consts
    src = x_src.rearrange("(b p) d -> p b d", p=P)
    dst = x_dst.rearrange("(b p) d -> p b d", p=P) if x_dst is not None else None
    with core.stage(name) as sb:
        x_in = sb("x_in", [P, TB, D]) if residual else acc
        xn = sb("xn", [P, TB, D])
        stats = [sb(f"stats{i}", [P, TB, 6]) for i in range(2)]
        mv = [sb(f"mv{i}", [P, TB, 2]) for i in range(2)]
        std = [sb(f"std{i}", [P, TB]) for i in range(2)]
        rstd = [sb(f"rstd{i}", [P, TB]) for i in range(2)]
        x_loaded = [core.sem(f"{name}_x_loaded{h}") for h in range(2)]
        stored = core.sem(f"{name}_stored")
        stat = core.sem(f"{name}_stat")
        std_ready = core.sem(f"{name}_std_ready")
        scaled = core.sem(f"{name}_scaled")
        x_new = core.sem(f"{name}_x_new")
        xn_ready = core.sem(f"{name}_xn_ready")
        turned = core.sem(f"{name}_turned")
        hi_ready = core.sem(f"{name}_hi_ready")
        lo_ready = core.sem(f"{name}_lo_ready")
        hb = TB // 2
        with nc.Block() as block:

            @block.sync
            def _(sp):
                for h in range(2):
                    sp.dma_start(x_in[:, h * hb:(h + 1) * hb, :], src[:, h * hb:(h + 1) * hb, :]).then_inc(x_loaded[h], 16)
                if dst is not None:
                    for h in range(2):
                        sp.wait_ge(x_new, (h + 1) * hb)
                        sp.dma_start(dst[:, h * hb:(h + 1) * hb, :], acc[:, h * hb:(h + 1) * hb, :]).then_inc(stored, 16)
                    sp.wait_ge(stored, 32)

            @block.scalar
            def _(act):
                for n in range((2 if residual else 0) + (0 if last else 2)):
                    i, h = (n // 2 if residual else 1), n % 2
                    act.wait_ge(stat, n * (2 * hb + 1) + 2 * hb)
                    act.activation(std[i][:, h * hb:(h + 1) * hb], mv[i][:, h * hb:(h + 1) * hb, 1], ACT.Sqrt,
                                   bias=eps[:, 0:1]).then_inc(std_ready, 1)
                if not last:
                    for n in range(2 * KT):
                        act.wait_ge(turned, n + 1)
                        k, h = n % KT, n // KT
                        act.activation(xh[:, k, h * HALF:(h + 1) * HALF], core.banks[n % 4][:, :],
                                       ACT.Copy).then_inc(hi_ready, 1)

            @block.vector
            def _(dve):
                count = [0]

                def statistics(i, h, ready):
                    blocks = range(h * hb, (h + 1) * hb)
                    for b in blocks:
                        ready(b)
                        dve.bn_stats(stats[i][:, b, :], acc[:, b, :]).then_inc(stat, 1)
                    for n, b in enumerate(blocks):
                        dve.wait_ge(stat, count[0] + n + 1)
                        dve.bn_aggr(mv[i][:, b, :], stats[i][:, b, :]).then_inc(stat, 1)
                    count[0] += 2 * hb

                def root(i, h, n):
                    dve.wait_ge(std_ready, n)
                    dve.reciprocal(rstd[i][:, h * hb:(h + 1) * hb], std[i][:, h * hb:(h + 1) * hb]).then_inc(stat, 1)
                    count[0] += 1
                    dve.wait_ge(stat, count[0])

                done = 0
                if residual:
                    for h in range(2):
                        statistics(0, h, lambda b: None)
                        done += 1
                        root(0, h, done)
                        for b in range(h * hb, (h + 1) * hb):
                            dve.tensor_scalar(acc[:, b, :], acc[:, b, :], mv[0][:, b, 0:1], rstd[0][:, b:b + 1],
                                              ALU.subtract, ALU.mult).then_inc(scaled, 1)
                        dve.wait_ge(x_loaded[h], 16)
                        for b in range(h * hb, (h + 1) * hb):
                            dve.wait_ge(scaled, b + 1)
                            dve.tensor_tensor(acc[:, b, :], acc[:, b, :], x_in[:, b, :], ALU.add).then_inc(x_new, 1)
                else:
                    for h in range(2):
                        dve.wait_ge(x_loaded[h], 16)
                if last:
                    return
                for h in range(2):
                    statistics(1, h, (lambda b: dve.wait_ge(x_new, b + 1)) if residual else (lambda b: None))
                    done += 1
                    root(1, h, done)
                    for b in range(h * hb, (h + 1) * hb):
                        dve.tensor_scalar(xn[:, b, :], acc[:, b, :], mv[1][:, b, 0:1], rstd[1][:, b:b + 1],
                                          ALU.subtract, ALU.mult).then_inc(xn_ready, 1)
                for n in range(2 * KT):
                    dve.wait_ge(hi_ready, n + 1)
                    k, h = n % KT, n // KT
                    cols = slice(h * HALF, (h + 1) * HALF)
                    dve.tensor_tensor(xl[:, k, cols], core.banks[n % 4][:, :], xh[:, k, cols].bitcast(F32),
                                      ALU.subtract).then_inc(lo_ready, 1)

            @block.tensor
            def _(pe):
                if last:
                    return
                for n in range(2 * KT):
                    k, h = n % KT, n // KT
                    if n >= 4:
                        pe.wait_ge(lo_ready, n - 3)
                    for b in range(hb):
                        pe.wait_ge(xn_ready, h * hb + b + 1)
                        t = pe.transpose(core.banks[n % 4][:, b * P:(b + 1) * P], xn[:, h * hb + b, k * P:(k + 1) * P],
                                         ident[:, :])
                    t.then_inc(turned, 1)


def products(pe, out, pairs, start=True, stop=True):
    for n, (w, m) in enumerate(pairs):
        mm = pe.matmul(out, w, m, start=start and n == 0, stop=stop and n == len(pairs) - 1)
    return mm


def three(wh, wl, mh, ml):
    return [(wh, mh), (wh, ml), (wl, mh)]


def project_layer0(core, consts, xh, xl, wq_d, wk_d, wv_d, cos_d, sin_d, q_scr, k_scr, v0, v0l):
    nc = core.nc
    NW = 2 * D + 3 * P
    SW = D + 2 * P
    QK = D // P + 1
    with core.stage("p0") as sb:
        raw = sb("raw", [P, KT, SW])
        wh = sb("wh", [P, KT, NW], F32R)
        wl = sb("wl", [P, KT, NW], F32R)
        cos, sin = sb("cos", [P, T]), sb("sin", [P, T])
        direct = sb("direct", [P, 2, HALF])
        swapped = sb("swapped", [P, 2, HALF])
        rot = sb("rot", [P, 2, HALF])
        rh = sb("rh", [P, 2, HALF], F32R)
        rl = sb("rl", [P, 2, HALF], F32R)
        w_loaded, tables = core.sem("p0_w_loaded"), core.sem("p0_tables")
        w_split = core.sem("p0_w_split")
        w_hi = core.sem("p0_w_hi")
        w_swap = core.sem("p0_w_swap")
        proj = core.sem("p0_proj")
        prod = core.sem("p0_prod")
        rotated = core.sem("p0_rotated")
        rh_ready, rl_ready = core.sem("p0_rh_ready"), core.sem("p0_rl_ready")
        sent = [core.sem(f"p0_sent{i}") for i in range(2)]
        v_proj, v_hi, v_lo = core.sem("p0_v_proj"), core.sem("p0_v_hi"), core.sem("p0_v_lo")
        CH = 2 * QK

        def swap_view(t, a, b):
            return t[:, :, a:b].rearrange("p k (h s i) -> p k h s i", s=2, i=DH0 // 2)

        with nc.Block() as block:

            @block.sync
            def _(sp):
                for w, a, b in ((wq_d, 0, D), (wk_d, D, D + P), (wv_d, D + P, SW)):
                    sp.dma_start(raw[:, :, a:b], w.rearrange("(k p) n -> p k n", p=P)).then_inc(w_loaded, 16)
                sp.dma_start(cos[:, :], cos_d).then_inc(tables, 16)
                sp.dma_start(sin[:, :], sin_d).then_inc(tables, 16)
                for n in range(CH):
                    m, h = n // 2, n % 2
                    sp.wait_ge(rl_ready, n + 1)
                    for part, r in ((0, rh), (1, rl)):
                        out = (q_scr[part, m * P:(m + 1) * P, h * HALF:(h + 1) * HALF] if m < QK - 1
                               else k_scr[part, :, h * HALF:(h + 1) * HALF])
                        sp.dma_start(out, r[:, n % 2, :].bitcast(F32)).then_inc(sent[n % 2], 16)
                for i in range(2):
                    sp.wait_ge(sent[i], 32 * (CH // 2))

            @block.scalar
            def _(act):
                act.wait_ge(w_loaded, 48)
                act.activation(wh[:, :, 0:SW], raw[:, :, :], ACT.Copy).then_inc(w_hi, 1)
                for n in range(CH):
                    act.wait_ge(rotated, n + 1)
                    if n >= 2:
                        act.wait_ge(sent[n % 2], 32 * (n // 2))
                    act.activation(rh[:, n % 2, :], rot[:, n % 2, :], ACT.Copy,
                                   scale=(-DH0 ** -0.5 if n // 2 < QK - 1 else 1.0)).then_inc(rh_ready, 1)
                act.wait_ge(v_proj, 1)
                for b in range(2):
                    act.activation(v0[:, 4 * b:4 * b + 4, :], core.banks[b][:, :].rearrange("p (b n) -> p b n", n=P),
                                   ACT.Copy).then_inc(v_hi, 1)

            @block.gpsimd
            def _(pool):
                pool.wait_ge(w_split, 1)
                for t in (wh, wl):
                    for a, b, o in ((0, D, SW), (D, D + P, SW + D)):
                        for s in range(2):
                            pool.tensor_copy(swap_view(t, o, o + b - a)[:, :, :, s, :],
                                             swap_view(t, a, b)[:, :, :, 1 - s, :]).then_inc(w_swap, 1)

            @block.vector
            def _(dve):
                dve.wait_ge(w_hi, 1)
                dve.tensor_tensor(wl[:, :, 0:SW], raw[:, :, :], wh[:, :, 0:SW].bitcast(F32),
                                  ALU.subtract).then_inc(w_split, 1)
                dve.wait_ge(tables, 32)
                for n in range(CH):
                    m, h = n // 2, n % 2
                    cols = slice(h * HALF, (h + 1) * HALF)
                    scale = -DH0 ** -0.5 if m < QK - 1 else 1.0
                    dve.wait_ge(proj, n + 1)
                    dve.tensor_tensor(direct[:, n % 2, :], core.slots[n % 2][:, 0:HALF], cos[:, cols],
                                      ALU.mult).then_inc(prod, 1)
                    dve.tensor_tensor(swapped[:, n % 2, :], core.slots[n % 2][:, HALF:2 * HALF], sin[:, cols],
                                      ALU.mult).then_inc(prod, 1)
                    dve.wait_ge(prod, 2 * n + 2)
                    dve.tensor_tensor(rot[:, n % 2, :], direct[:, n % 2, :], swapped[:, n % 2, :],
                                      ALU.add).then_inc(rotated, 1)
                    dve.wait_ge(rh_ready, n + 1)
                    dve.scalar_tensor_tensor(rl[:, n % 2, :], rot[:, n % 2, :], scale, rh[:, n % 2, :].bitcast(F32),
                                             ALU.mult, ALU.subtract).then_inc(rl_ready, 1)
                for b in range(2):
                    dve.wait_ge(v_hi, b + 1)
                    dve.tensor_tensor(v0l[:, 4 * b:4 * b + 4, :], core.banks[b][:, :].rearrange("p (b n) -> p b n", n=P),
                                      v0[:, 4 * b:4 * b + 4, :].bitcast(F32), ALU.subtract).then_inc(v_lo, 1)

            @block.tensor
            def _(pe):
                pe.wait_ge(w_split, 1)
                for b in range(TB):
                    toks = slice(b * P, (b + 1) * P)
                    vc = slice(D + P, SW)
                    pairs = [pr for k in range(KT)
                             for pr in three(xh[:, k, toks], xl[:, k, toks], wh[:, k, vc], wl[:, k, vc])]
                    mm = products(pe, core.banks[b // 4][:, (b % 4) * P:(b % 4 + 1) * P], pairs)
                mm.then_inc(v_proj, 1)
                pe.wait_ge(w_swap, 8)
                for n in range(CH):
                    m, h = n // 2, n % 2
                    cols = slice(h * HALF, (h + 1) * HALF)
                    if n >= 2:
                        pe.wait_ge(prod, 2 * (n - 1))
                    for s, base in ((0, 0), (1, SW)):
                        wc = slice(base + m * P, base + (m + 1) * P)
                        pairs = [pr for k in range(KT)
                                 for pr in three(wh[:, k, wc], wl[:, k, wc], xh[:, k, cols], xl[:, k, cols])]
                        mm = products(pe, core.slots[n % 2][:, s * HALF:(s + 1) * HALF], pairs)
                    mm.then_inc(proj, 1)


def attention(core, name, layer, consts, acc, xh, xl, io):
    nc = core.nc
    ident, mask, eps, ones = consts
    one = layer == 1
    UNITS = 2 * GH
    KBS = [4, 8]
    TURN = GH * sum(KBS)
    LAG = 2
    first_tile = [sum(KBS[v % 2] for v in range(u)) for u in range(UNITS + 1)]

    items = [("K", 0), ("V", 0), ("Q", 0)] if one else []
    items += [("S", 0, b) for b in range(4)]
    for u in range(UNITS):
        if u + 1 < UNITS:
            items += [("S", u + 1, b) for b in range(4)]
        if one and u % 2 == 0 and u // 2 + 1 < GH:
            items += [("Q", u // 2 + 1)]
    items += [("W", c) for c in range(4)]
    N = len(items)
    assert N % 2 == 0
    at = {it: n for n, it in enumerate(items)}

    with core.stage(name) as sb:
        probs = [sb("probs_a", [P, 4, HALF]), sb("probs_b", [P, 4, T])]
        pt_h = sb("pt_h", [P, 4, HALF], F32R)
        pt_l = sb("pt_l", [P, 4, HALF], F32R)
        low = sb("low", [P, 2, 4])
        sums = sb("sums", [P, 2, 4])
        rinv = sb("rinv", [P, 2, 4])
        AJ = GH if one else 1
        at_h = sb("at_h", [P, AJ, T], F32R)
        at_l = sb("at_l", [P, AJ, T], F32R)
        wo_h = sb("wo_h", [P, AJ, D], F32R)
        wo_l = sb("wo_l", [P, AJ, D], F32R)
        wo_raw = sb("wo_raw", [P, 2, D])
        if one:
            qh, ql = sb("qh", [P, 2, T], F32R), sb("ql", [P, 2, T], F32R)
            kh, kl = sb("kh", [P, T], F32R), sb("kl", [P, T], F32R)
            vh, vl = sb("vh", [P, TB, P], F32R), sb("vl", [P, TB, P], F32R)
            wq_raw, wkv_raw = sb("wq_raw", [P, 2, KT, P]), sb("wkv_raw", [P, KT, 2 * P])
            wqh, wql = sb("wqh", [P, 2, KT, P], F32R), sb("wql", [P, 2, KT, P], F32R)
            wkvh, wkvl = sb("wkvh", [P, KT, 2 * P], F32R), sb("wkvl", [P, KT, 2 * P], F32R)
        else:
            DQ = 4 * DH0
            q_stack = sb("q_stack", [DQ, GH, T], F32R)
            k_stack = sb("k_stack", [DQ, KV, T], F32R)
            v_pad = sb("v_pad", [P, TB, GH, P], F32R)
        tbank, obank = core.banks[0:2], core.banks[2:4]

        kv_loaded = core.sem(f"{name}_kv_loaded")
        q_loaded = [core.sem(f"{name}_q_loaded{i}") for i in range(2 if one else GH)]
        wo_loaded = [core.sem(f"{name}_wo_loaded{i}") for i in range(2)]
        kv_split = core.sem(f"{name}_kv_split")
        q_split = core.sem(f"{name}_q_split")
        wo_split = core.sem(f"{name}_wo_split")
        w_hi = core.sem(f"{name}_w_hi")
        slot_full = core.sem(f"{name}_slot_full")
        hi_done = core.sem(f"{name}_hi_done")
        slot_free = core.sem(f"{name}_slot_free")
        exp_done = core.sem(f"{name}_exp_done")
        inv_done = core.sem(f"{name}_inv_done")
        norm_done = core.sem(f"{name}_norm_done")
        turned = core.sem(f"{name}_turned")
        pt_hi = core.sem(f"{name}_pt_hi")
        pt_lo = core.sem(f"{name}_pt_lo")
        pv_done = core.sem(f"{name}_pv_done")
        out_hi = core.sem(f"{name}_out_hi")
        out_lo = core.sem(f"{name}_out_lo")
        acc_zero = core.sem(f"{name}_acc_zero")
        own_pe, own_dve, own_pool = (core.sem(f"{name}_own_{e}") for e in ("pe", "dve", "pool"))
        pad_zero = core.sem(f"{name}_pad_zero")
        OUTS = UNITS if one else 2
        QS = GH
        WOS = GH if one else 1
        HIS = 2 + GH

        WEIGHTS = [("kv", 0), ("q", 0), ("q", 1), ("wo", 0), ("q", 2), ("wo", 1), ("q", 3), ("wo", 2), ("wo", 3)]

        def out_index(u):
            return u if one else ({UNITS - 2: 0, UNITS - 1: 1}.get(u))

        def widths(u, b):
            return (4 * (u % 2) + b + 1) * P

        def tile_cols(u, kb):
            return max(0, kb - 4 * (u % 2)) * P

        with nc.Block() as block:

            @block.sync
            def _(sp):
                if not one:
                    for part, rows in ((0, 0), (0, 1), (1, 2), (1, 3)):
                        sp.dma_start(k_stack[rows * DH0:(rows + 1) * DH0, :, :].bitcast(F32),
                                     io["k"][part].rearrange("(g i) t -> i g t", i=DH0)).then_inc(kv_loaded, 16)
                with sp.Fori(0, KV) as g:
                    if one:
                        for what, j in WEIGHTS:
                            if what == "kv":
                                sp.wait_ge(kv_split, g + 1)
                                for s, w in enumerate((io["wk"], io["wv"])):
                                    sp.dma_start(wkv_raw[:, :, s * P:(s + 1) * P],
                                                 w.rearrange("(k p) n -> p k n", p=P)[:, :, bass.ds(g * P, P)]).then_inc(kv_loaded, 16)
                            elif what == "q":
                                sp.wait_ge(q_split, g * GH + j + 1)
                                sp.dma_start(wq_raw[:, j % 2, :, :], io["wq"].rearrange("(k p) n -> p k n", p=P)
                                             [:, :, bass.ds(g * (GH * P) + j * P, P)]).then_inc(q_loaded[j % 2], 16)
                            else:
                                sp.wait_ge(wo_split, g * GH + j + 1)
                                sp.dma_start(wo_raw[:, j % 2, :],
                                             io["wo"][bass.ds(g * (GH * P) + j * P, P), :]).then_inc(wo_loaded[j % 2], 16)
                    else:
                        for j in range(GH):
                            sp.wait_ge(slot_full, g * N + at[("S", 2 * j + 1, 3)] + 1)
                            for rows in range(4):
                                sp.dma_start(q_stack[rows * DH0:(rows + 1) * DH0, j, :].bitcast(F32),
                                             io["q"][rows % 2][bass.ds(g * (GH * DH0) + j * DH0, DH0), :]).then_inc(q_loaded[j], 16)
                            if j == 0:
                                sp.wait_ge(wo_split, g + 1)
                                for s in range(2):
                                    sp.dma_start(wo_raw[s * 64:(s + 1) * 64, 0, :],
                                                 io["wo"][bass.ds(g * 64, 64), :]).then_inc(wo_loaded[0], 16)

            @block.gpsimd
            def _(pool):
                pool.sem_inc(kv_split, 1)
                pool.sem_inc(q_split, 2)
                pool.sem_inc(wo_split, 2 if one else 1)

                def split(raw, hi, lo, count, done):
                    pool.sem_inc(own_pool, 1)
                    pool.tensor_copy(hi, raw).then_inc(w_hi, 1)
                    pool.wait_ge(w_hi, count)
                    pool.tensor_tensor(lo, raw, hi.bitcast(F32), ALU.subtract).then_inc(done, 1)

                if not one:
                    pool.memset(v_pad[:, :, :, :].bitcast(F32), 0.0).then_inc(pad_zero, 1)
                    pool.wait_ge(pad_zero, 1)
                with pool.Fori(0, KV) as g:
                    if one:
                        W = 1 + 2 * GH
                        for n, (what, j) in enumerate(WEIGHTS):
                            if what == "kv":
                                pool.wait_ge(kv_loaded, g * 32 + 32)
                                pool.wait_ge(slot_full, g * N + at[("V", 0)] + 1)
                                split(wkv_raw[:, :, :], wkvh[:, :, :], wkvl[:, :, :], g * W + n + 1, kv_split)
                            elif what == "q":
                                pool.wait_ge(q_loaded[j % 2], g * 32 + (j // 2) * 16 + 16)
                                used = at[("Q", j - 2)] + N if j >= 2 else at[("Q", j + 2)]
                                pool.wait_ge(slot_full, g * N + used + 1)
                                split(wq_raw[:, j % 2, :, :], wqh[:, j % 2, :, :], wql[:, j % 2, :, :], g * W + n + 1, q_split)
                            else:
                                pool.wait_ge(wo_loaded[j % 2], g * 32 + (j // 2) * 16 + 16)
                                pool.wait_ge(slot_full, g * N + N)
                                split(wo_raw[:, j % 2, :], wo_h[:, j, :], wo_l[:, j, :], g * W + n + 1, wo_split)
                    else:
                        pool.wait_ge(pv_done, g * TURN + 4)
                        pool.sem_inc(own_pool, 1)
                        for part, t in ((0, io["v0"]), (1, io["v0l"])):
                            for j in range(GH):
                                c = part * 64 + j * DH0
                                pool.tensor_copy(v_pad[:, :, j, c:c + DH0],
                                                 t[:, :, bass.ds(g * DH0, DH0)]).then_inc(kv_split, 1)
                        pool.wait_ge(wo_loaded[0], g * 32 + 32)
                        pool.wait_ge(slot_full, g * N + N)
                        split(wo_raw[:, 0, :], wo_h[:, 0, :], wo_l[:, 0, :], g + 1, wo_split)

            @block.scalar
            def _(act):
                with act.Fori(0, KV) as g:
                    def high(item, n, dst, scale):
                        act.wait_ge(slot_full, (g + 1) * N + at[item] + 1)
                        act.activation(dst, core.slots[at[item] % 2][:, :], ACT.Copy, scale=scale).then_inc(hi_done, 1)

                    def exps(u):
                        s = u % 2
                        for b in range(4):
                            w = widths(u, b)
                            act.wait_ge(slot_free, g * N + at[("S", u, b)] + 1 + 2)
                            act.activation(probs[s][:, b, 0:w], probs[s][:, b, 0:w], ACT.Exp, bias=low[:, s, b:b + 1],
                                           scale=-1.0, accum_out=sums[:, s, b:b + 1]).then_inc(exp_done, 1)

                    def tile_high(u, kb):
                        n, c = first_tile[u] + kb, tile_cols(u, kb)
                        act.wait_ge(turned, g * TURN + n + 1)
                        act.wait_ge(pv_done, g * TURN + n + 1)
                        act.activation(pt_h[:, n % 4, c:HALF], tbank[n % 2][:, c:HALF], ACT.Copy).then_inc(pt_hi, 1)

                    def out_high(u):
                        e = out_index(u)
                        act.wait_ge(pv_done, g * TURN + first_tile[u + 1] + 4)
                        act.activation(at_h[:, u // 2 if one else 0, (u % 2) * HALF:(u % 2 + 1) * HALF],
                                       obank[u % 2][:, :], ACT.Copy).then_inc(out_hi, 1)

                    if one:
                        high(("K", 0), 0, kh[:, :], 1.0)
                        high(("V", 0), 1, vh[:, :, :].rearrange("p b n -> p (b n)"), 1.0)
                        high(("Q", 0), 2, qh[:, 0, :], -DH1 ** -0.5)
                    exps(0)
                    for u in range(UNITS):
                        if u + 1 < UNITS:
                            exps(u + 1)
                        if ("Q", u // 2 + 1) in at and u % 2 == 0:
                            high(("Q", u // 2 + 1), 3 + u // 2, qh[:, (u // 2 + 1) % 2, :], -DH1 ** -0.5)
                        for kb in range(KBS[u % 2]):
                            tile_high(u, kb)
                        if out_index(u) is not None:
                            out_high(u)

            @block.vector
            def _(dve):
                dve.sem_inc(slot_free, 2)
                dve.sem_inc(pt_lo, 2)
                dve.sem_inc(out_lo, 2)
                dve.memset(acc[:, :, :], 0.0).then_inc(acc_zero, 1)
                dve.wait_ge(acc_zero, 1)
                with dve.Fori(0, KV) as g:
                    def low_part(item, n, hi, lo, scale):
                        dve.wait_ge(hi_done, g * HIS + n + 1)
                        slot = core.slots[at[item] % 2][:, :]
                        dve.scalar_tensor_tensor(lo, slot, scale, hi.bitcast(F32), ALU.mult,
                                                 ALU.subtract).then_inc(slot_free, 1)

                    def minima(u):
                        s = u % 2
                        for b in range(4):
                            n, w = at[("S", u, b)], widths(u, b)
                            dve.wait_ge(slot_full, (g + 1) * N + n + 1)
                            dve.sem_inc(own_dve, 1)
                            dve.tensor_tensor_reduce(probs[s][:, b, 0:w], core.slots[n % 2][:, 0:w],
                                                     mask[:, T - w:T], 1.0, 3e38, ALU.add, ALU.min,
                                                     low[:, s, b:b + 1]).then_inc(slot_free, 1)

                    def normalise(u):
                        s = u % 2
                        dve.wait_ge(exp_done, g * 4 * UNITS + 4 * (u + 1))
                        dve.reciprocal(rinv[:, s, :], sums[:, s, :]).then_inc(inv_done, 1)
                        dve.wait_ge(inv_done, g * UNITS + u + 1)
                        for b in range(4):
                            w = widths(u, b)
                            dve.tensor_scalar(probs[s][:, b, 0:w], probs[s][:, b, 0:w], rinv[:, s, b:b + 1], None,
                                              ALU.mult).then_inc(norm_done, 1)

                    def tile_low(u, kb):
                        n, c = first_tile[u] + kb, tile_cols(u, kb)
                        dve.wait_ge(pt_hi, g * TURN + n + 1)
                        dve.tensor_tensor(pt_l[:, n % 4, c:HALF], tbank[n % 2][:, c:HALF],
                                          pt_h[:, n % 4, c:HALF].bitcast(F32), ALU.subtract).then_inc(pt_lo, 1)

                    def out_low(u):
                        e = out_index(u)
                        dve.wait_ge(out_hi, g * OUTS + e + 1)
                        j, cols = (u // 2 if one else 0), slice((u % 2) * HALF, (u % 2 + 1) * HALF)
                        dve.tensor_tensor(at_l[:, j, cols], obank[u % 2][:, :], at_h[:, j, cols].bitcast(F32),
                                          ALU.subtract).then_inc(out_lo, 1)

                    if one:
                        low_part(("K", 0), 0, kh[:, :], kl[:, :], 1.0)
                        low_part(("V", 0), 1, vh[:, :, :].rearrange("p b n -> p (b n)"),
                                 vl[:, :, :].rearrange("p b n -> p (b n)"), 1.0)
                        low_part(("Q", 0), 2, qh[:, 0, :], ql[:, 0, :], -DH1 ** -0.5)
                    minima(0)
                    for u in range(UNITS):
                        normalise(u)
                        if u + 1 < UNITS:
                            minima(u + 1)
                        j = u // 2 + 1
                        if ("Q", j) in at and u % 2 == 0:
                            low_part(("Q", j), 2 + j, qh[:, j % 2, :], ql[:, j % 2, :], -DH1 ** -0.5)
                        for kb in range(KBS[u % 2]):
                            tile_low(u, kb)
                        if out_index(u) is not None:
                            out_low(u)
                    for c in range(4):
                        n = at[("W", c)]
                        dve.wait_ge(slot_full, (g + 1) * N + n + 1)
                        part = acc[:, 2 * c:2 * c + 2, :].rearrange("p b n -> p (b n)")
                        dve.tensor_tensor(part, part, core.slots[n % 2][:, :], ALU.add).then_inc(slot_free, 1)

            @block.tensor
            def _(pe):
                pe.sem_inc(pv_done, 4)
                pe.sem_inc(slot_full, N)
                with pe.Fori(0, KV) as g:
                    def slot(item):
                        n = at[item]
                        pe.wait_ge(slot_free, g * N + n + 1)
                        return core.slots[n % 2]

                    def project(item, hi, lo, weights_ready, value):
                        out = slot(item)
                        pe.wait_ge(weights_ready, value)
                        for h in range(2):
                            cols = slice(h * HALF, (h + 1) * HALF)
                            pairs = [pr for k in range(KT) for pr in three(hi(k), lo(k), xh[:, k, cols], xl[:, k, cols])]
                            mm = products(pe, out[:, cols], pairs)
                        mm.then_inc(slot_full, 1)

                    def project_q(j):
                        project(("Q", j), lambda k: wqh[:, j % 2, k, :], lambda k: wql[:, j % 2, k, :],
                                q_split, g * GH + j + 1 + 2)

                    def scores(u):
                        j, s = u // 2, u % 2
                        for b in range(4):
                            out = slot(("S", u, b))
                            if b == 0 and one and s == 0:
                                pe.wait_ge(slot_free, g * N + at[("Q", j)] + 1 + 2)
                            if b == 0 and not one and s == 0:
                                pe.wait_ge(q_loaded[j], g * 64 + 64)
                            w = widths(u, b)
                            qc = slice(w - P, w)
                            for c0 in range(0, w, HALF):
                                c1 = min(c0 + HALF, w)
                                if not one and c0 == 0:
                                    pe.sem_inc(own_pe, 1)
                                if one:
                                    pairs = three(qh[:, j % 2, qc], ql[:, j % 2, qc], kh[:, c0:c1], kl[:, c0:c1])
                                else:
                                    pairs = [(q_stack[:, j, qc], k_stack[:, bass.ds(g, 1), c0:c1]
                                              .rearrange("p g t -> p (g t)"))]
                                mm = products(pe, out[:, c0:c1], pairs)
                            mm.then_inc(slot_full, 1)

                    def transpose_tile(u, kb):
                        n, s, c = first_tile[u] + kb, u % 2, tile_cols(u, kb)
                        if kb == 0:
                            pe.wait_ge(norm_done, g * 4 * UNITS + 4 * (u + 1))
                        pe.wait_ge(pt_lo, g * TURN + n + 1)
                        for b in range(c // P, 4):
                            t = pe.transpose(tbank[n % 2][:, b * P:(b + 1) * P], probs[s][:, b, kb * P:(kb + 1) * P],
                                             ident[:, :])
                        t.then_inc(turned, 1)

                    def times_v(u, kb):
                        n, j, s, c = first_tile[u] + kb, u // 2, u % 2, tile_cols(u, kb)
                        pe.wait_ge(pt_lo, g * TURN + n + 1 + 2)
                        if kb == 0 and one:
                            pe.wait_ge(out_lo, g * OUTS + u + 1)
                        if kb == 0 and not one and j == 0:
                            pe.wait_ge(out_lo, g * OUTS + s + 1)
                            pe.wait_ge(kv_split, g * 8 + 8 + 1)
                        ph, pl = pt_h[:, n % 4, c:HALF], pt_l[:, n % 4, c:HALF]
                        if one:
                            pairs = three(vh[:, kb, :], vl[:, kb, :], ph, pl)
                        else:
                            pairs = [(v_pad[:, kb, j, :], ph), (v_pad[:, kb, j, :], pl)]
                        first = kb == 0 and (one or j == 0)
                        final = kb == KBS[s] - 1 and (one or j == GH - 1)
                        products(pe, obank[s][:, c:HALF], pairs, first, final).then_inc(pv_done, 1)

                    if one:
                        project(("K", 0), lambda k: wkvh[:, k, 0:P], lambda k: wkvl[:, k, 0:P], kv_split, g + 1 + 1)
                        out = slot(("V", 0))
                        for b in range(TB):
                            toks = slice(b * P, (b + 1) * P)
                            pairs = [pr for k in range(KT) for pr in three(xh[:, k, toks], xl[:, k, toks],
                                                                           wkvh[:, k, P:2 * P], wkvl[:, k, P:2 * P])]
                            mm = products(pe, out[:, toks], pairs)
                        mm.then_inc(slot_full, 1)
                        project_q(0)
                    else:
                        pe.wait_ge(kv_loaded, 64)
                    scores(0)
                    for u in range(UNITS):
                        if u + 1 < UNITS:
                            scores(u + 1)
                        if ("Q", u // 2 + 1) in at and u % 2 == 0:
                            project_q(u // 2 + 1)
                        kbs = KBS[u % 2]
                        for kb in range(kbs + LAG):
                            if kb < kbs:
                                t = transpose_tile(u, kb)
                            if kb >= LAG:
                                times_v(u, kb - LAG)
                    pe.wait_ge(wo_split, (g + 1) * WOS + (2 if one else 1))
                    for c in range(4):
                        out = slot(("W", c))
                        if c == 0:
                            pe.wait_ge(out_lo, (g + 1) * OUTS + 2)
                        for b in (2 * c, 2 * c + 1):
                            toks = slice(b * P, (b + 1) * P)
                            pairs = [pr for j in range(AJ) for pr in three(at_h[:, j, toks], at_l[:, j, toks],
                                                                           wo_h[:, j, :], wo_l[:, j, :])]
                            mm = products(pe, out[:, (b % 2) * HALF:(b % 2 + 1) * HALF], pairs)
                        mm.then_inc(slot_full, 1)


def swiglu(core, consts, acc, xh, xl, io):
    nc = core.nc
    with core.stage("f0") as sb:
        w_gu = sb("w_gu", [P, KT, 2 * INTER])
        w_dn = sb("w_dn", [P, FT, D])
        shift = sb("shift", [P, 1], U32)
        loads = core.sem("f0_loads")
        idx_done = core.sem("f0_idx")
        gathered = core.sem("f0_gathered")
        raw_loaded = [core.sem(f"f0_raw{i}") for i in range(2)]
        raw_free = core.sem("f0_raw_free")
        nib, zeros_ready, diff, ready = (core.sem(f"f0_{n}") for n in ("nib", "zeros", "diff", "ready"))

        with ExitStack() as ctx2:
            sb2 = lambda n, shape, dt=F32: ctx2.enter_context(nc.sbuf_tensor(f"f0_{n}", shape, dt))
            idx = sb2("idx", [P, KT + FT], I32)
            wrap = sb2("wrap", [P, KT + FT], I32)
            z_gu = sb2("z_gu", [P, KT, 2 * INTER // NIBBLES], U32)
            z_dn = sb2("z_dn", [P, FT, D // NIBBLES], U32)
            WIDE = 2 * INTER
            raw = sb2("raw", [P, 2, WIDE], U32)
            wi = sb2("wi", [P, WIDE], U32)
            zi = sb2("zi", [P, WIDE], U32)
            parts = [(P, io["qgu"], 16 * k, WIDE, k, z_gu[:, k, :], w_gu[:, k, :], 1) for k in range(KT)]
            parts += [(P, io["qdn"], 16 * k, D * 5, KT + k, z_dn[:, k:k + 5, :], w_dn[:, k:k + 5, :], 5) for k in (0, 5)]
            parts += [(F_LAST, io["qdn"], 160, D, KT + 10, z_dn[:, 10, :], w_dn[:, 10, :], 1)]
            with nc.Block() as block:

                @block.sync
                def _(sp):
                    sp.dma_start(idx[:, 0:KT], io["ggu"].rearrange("(k p) -> p k", p=P), allow_slow_non_contiguous=True).then_inc(loads, 16)
                    sp.dma_start(idx[:, KT:KT + FT - 1], io["gdn"][0:(FT - 1) * P].rearrange("(k p) -> p k", p=P), allow_slow_non_contiguous=True).then_inc(loads, 16)
                    sp.dma_start(idx[0:F_LAST, KT + FT - 1:KT + FT], io["gdn"][(FT - 1) * P:INTER].rearrange("(p a) -> p a", a=1), allow_slow_non_contiguous=True).then_inc(loads, 16)
                    sp.dma_start(shift[:, :], io["shift"]).then_inc(loads, 16)
                    for n, (rows, src, r0, width, _, _, _, tiles) in enumerate(parts):
                        if n >= 2:
                            sp.wait_ge(raw_free, n - 1)
                        for s in range(NIBBLES):
                            if tiles == 1:
                                out = raw[s:rows:NIBBLES, n % 2, 0:width]
                                sp.dma_start(out, src[r0:r0 + rows // NIBBLES, :]).then_inc(raw_loaded[n % 2], 16)
                            else:
                                out = raw[s:rows:NIBBLES, n % 2, 0:width].rearrange("r (k n) -> r k n", n=D)
                                sp.dma_start(out, src[r0:r0 + tiles * 16, :].rearrange("(k r) n -> r k n", r=16)).then_inc(raw_loaded[n % 2], 16)

                @block.gpsimd
                def _(pool):
                    pool.wait_ge(idx_done, 7)
                    for k in range(KT + FT):
                        rows = F_LAST if k == KT + FT - 1 else P
                        at = bass.IndirectOffsetOnAxis(ap=idx[0:rows, k:k + 1].bitcast(U32), axis=0)
                        if k < KT:
                            pairs = ((z_gu[:, k, :], io["zgu"]), (w_gu[:, k, :], io["sgu"]))
                        else:
                            pairs = ((z_dn[0:rows, k - KT, :], io["zdn"]), (w_dn[0:rows, k - KT, :], io["sdn"]))
                        for out, src in pairs:
                            pool.indirect_dma_start(out=out, out_offset=None, in_=src[:, :], in_offset=at).then_inc(gathered, 16)
                    pool.wait_ge(gathered, 32 * (KT + FT))

                @block.vector
                def _(dve):
                    dve.wait_ge(loads, 64)
                    dve.memset(wrap[:, :], 0.0).then_inc(idx_done, 1)
                    dve.wait_ge(idx_done, 1)
                    views = ((slice(0, KT), P, GU_GROUPS), (slice(KT, KT + FT - 1), P, DN_GROUPS),
                             (slice(KT + FT - 1, KT + FT), F_LAST, DN_GROUPS))
                    for c, rows, groups in views:
                        dve.tensor_scalar(wrap[0:rows, c], idx[0:rows, c], 0, groups, ALU.is_lt, ALU.mult).then_inc(idx_done, 1)
                    dve.wait_ge(idx_done, 4)
                    for c, rows, groups in views:
                        dve.tensor_tensor(wrap[0:rows, c], idx[0:rows, c], wrap[0:rows, c], ALU.add).then_inc(nib, 1)
                    dve.wait_ge(nib, 3)
                    for c, rows, groups in views:
                        dve.tensor_scalar(idx[0:rows, c], wrap[0:rows, c], 0, groups - 1, ALU.max, ALU.min).then_inc(idx_done, 1)
                    dve.wait_ge(gathered, 32 * (KT + FT))
                    for n, (rows, _, _, width, _, z, w, tiles) in enumerate(parts):
                        z, w = z[0:rows], w[0:rows]
                        if n:
                            dve.wait_ge(ready, n)
                        zo = zi[0:rows, 0:width]
                        if tiles > 1:
                            zo = zo.rearrange("p (k c s) -> p k c s", k=tiles, s=NIBBLES)
                            w = w.rearrange("p k n -> p (k n)")
                        else:
                            zo = zo.rearrange("p (c s) -> p c s", s=NIBBLES)
                        for s in range(NIBBLES):
                            o = zo[:, :, :, s] if tiles > 1 else zo[:, :, s]
                            dve.tensor_scalar(o, z, 4 * s, 15, ALU.logical_shift_right, ALU.bitwise_and).then_inc(zeros_ready, 1)
                        dve.wait_ge(raw_loaded[n % 2], 16 * NIBBLES * (n // 2 + 1))
                        dve.tensor_scalar(wi[0:rows, 0:width], raw[0:rows, n % 2, 0:width], shift[0:rows, 0:1], 15,
                                          ALU.logical_shift_right, ALU.bitwise_and).then_inc(raw_free, 1)
                        dve.wait_ge(raw_free, n + 1)
                        dve.wait_ge(zeros_ready, NIBBLES * (n + 1))
                        d = raw[0:rows, n % 2, 0:width].bitcast(F32) if False else wf_view(zi, rows, width)
                        dve.scalar_tensor_tensor(d, wi[0:rows, 0:width], -1.0, zi[0:rows, 0:width], ALU.add,
                                                 ALU.subtract).then_inc(diff, 1)
                        dve.wait_ge(diff, n + 1)
                        dve.tensor_tensor(w, w, d, ALU.mult).then_inc(ready, 1)
                    dve.wait_ge(ready, len(parts))

        silu_sets(core, acc, xh, xl, w_gu, w_dn)


def wf_view(zi, rows, width):
    return zi[0:rows, 0:width].bitcast(F32)


def silu_sets(core, acc, xh, xl, w_gu, w_dn):
    nc = core.nc
    with core.stage("f1") as sb:
        wh, wl = sb("wh", [P, KT, 2, P], F32R), sb("wl", [P, KT, 2, P], F32R)
        dh, dl = sb("dh", [P, D], F32R), sb("dl", [P, D], F32R)
        gate = sb("gate", [P, 2, HALF])
        hid = sb("hid", [P, 2, HALF])
        hh, hl = sb("hh", [P, T], F32R), sb("hl", [P, T], F32R)
        S = {n: core.sem(f"f1_{n}") for n in
             ("acc_zero", "wh", "wl", "dh", "dl", "gu", "gate", "hid", "hh", "hl", "dn", "added", "own_pool")}
        gu_bank = [core.slots[0], core.slots[1]]

        def turns(eng, body, lag_last=None):
            with eng.Fori(0, FT - 1) as f:
                body(f, f * P, P)
            body(FT - 1, (FT - 1) * P, F_LAST)

        with nc.Block() as block:

            @block.gpsimd
            def _(pool):
                pool.memset(acc[:, :, :], 0.0).then_inc(S["acc_zero"], 1)

                def body(f, c0, F):
                    pool.wait_ge(S["gu"], f * 2 + 2)
                    pool.sem_inc(S["own_pool"], 1)
                    for s in range(2):
                        cols = bass.ds(c0 + s * INTER, F)
                        pool.tensor_copy(wh[:, :, s, 0:F], w_gu[:, :, cols]).then_inc(S["wh"], 1)
                    for s in range(2):
                        cols = bass.ds(c0 + s * INTER, F)
                        pool.wait_ge(S["wh"], f * 2 + s + 1)
                        pool.sem_inc(S["own_pool"], 1)
                        pool.tensor_tensor(wl[:, :, s, 0:F], w_gu[:, :, cols], wh[:, :, s, 0:F].bitcast(F32),
                                           ALU.subtract).then_inc(S["wl"], 1)
                    row = (w_dn[0:F, bass.ds(f, 1), :]).rearrange("p a n -> p (a n)")
                    pool.wait_ge(S["dn"], f * 8 + 8)
                    pool.sem_inc(S["own_pool"], 1)
                    pool.tensor_copy(dh[0:F, :], row).then_inc(S["dh"], 1)
                    pool.wait_ge(S["dh"], f + 1)
                    pool.sem_inc(S["own_pool"], 1)
                    pool.tensor_tensor(dl[0:F, :], row, dh[0:F, :].bitcast(F32), ALU.subtract).then_inc(S["dl"], 1)

                turns(pool, body)

            @block.scalar
            def _(act):
                def body(f, c0, F):
                    for h in range(2):
                        act.wait_ge(S["gu"], f * 2 + h + 1 + 2)
                        act.activation(gate[0:F, h, :], gu_bank[h][0:F, 0:HALF], ACT.Silu).then_inc(S["gate"], 1)
                        act.wait_ge(S["hid"], f * 2 + h + 1)
                        act.wait_ge(S["dn"], f * 8 + 4 * h + 4)
                        act.activation(hh[0:F, h * HALF:(h + 1) * HALF], hid[0:F, h, :], ACT.Copy).then_inc(S["hh"], 1)

                turns(act, body)

            @block.vector
            def _(dve):
                dve.wait_ge(S["acc_zero"], 1)

                def add(f, half):
                    for b in range(4 * half, 4 * half + 4):
                        dve.wait_ge(S["dn"], f * 8 + b + 1 + 8)
                        dve.wait_ge(S["hl"], f * 2 + half + 1)
                        dve.tensor_tensor(acc[:, b, :], acc[:, b, :], core.banks[b % 4][:, :], ALU.add).then_inc(S["added"], 1)

                def hidden(f, h, F):
                    cols = slice(h * HALF, (h + 1) * HALF)
                    dve.wait_ge(S["gate"], f * 2 + h + 1)
                    dve.tensor_tensor(hid[0:F, h, :], gate[0:F, h, :], gu_bank[h][0:F, HALF:2 * HALF],
                                      ALU.mult).then_inc(S["hid"], 1)
                    dve.wait_ge(S["hh"], f * 2 + h + 1)
                    dve.tensor_tensor(hl[0:F, cols], hid[0:F, h, :], hh[0:F, cols].bitcast(F32),
                                      ALU.subtract).then_inc(S["hl"], 1)

                def body(f, c0, F):
                    hidden(f, 0, F)
                    hidden(f, 1, F)
                    add(f, 0)
                    add(f, 1)

                turns(dve, body)

            @block.tensor
            def _(pe):
                pe.sem_inc(S["gu"], 2)
                pe.sem_inc(S["dn"], 8)

                def body(f, c0, F):
                    for h in range(2):
                        if h == 0:
                            pe.wait_ge(S["wl"], f * 2 + 2)
                        cols = slice(h * HALF, (h + 1) * HALF)
                        for s in range(2):
                            pairs = [pr for k in range(KT) for pr in three(wh[:, k, s, 0:F], wl[:, k, s, 0:F],
                                                                           xh[:, k, cols], xl[:, k, cols])]
                            mm = products(pe, gu_bank[h][0:F, s * HALF:(s + 1) * HALF], pairs)
                        mm.then_inc(S["gu"], 1)
                    pe.wait_ge(S["dl"], f + 1)
                    for b in range(TB):
                        if b % 4 == 0:
                            pe.wait_ge(S["hl"], f * 2 + b // 4 + 1)
                        toks = slice(b * P, (b + 1) * P)
                        if b >= 4:
                            pe.wait_ge(S["added"], f * 8 + b - 3)
                        mm = products(pe, core.banks[b % 4][:, :], three(hh[0:F, toks], hl[0:F, toks], dh[0:F, :], dl[0:F, :]))
                        mm.then_inc(S["dn"], 1)

                turns(pe, body)


def lora_mixture(core, consts, acc, xh, xl, io):
    nc = core.nc
    ident, mask, eps, ones = consts
    ER = EXPERTS * RANK
    with core.stage("m") as sb:
        wb = sb("wb", [P, KT, D])
        la = sb("la", [ER, D])
        wr = sb("wr", [EXPERTS, D])
        lb = sb("lb", [P, KT, EXPERTS, RANK])
        bias = sb("bias", [1, D])
        NW = D + ER + EXPERTS
        wth, wtl = sb("wth", [P, KT, NW], F32R), sb("wtl", [P, KT, NW], F32R)
        bth, btl = sb("bth", [ER, D], F32R), sb("btl", [ER, D], F32R)
        prob = sb("prob", [P, TB, EXPERTS])
        top = sb("top", [P, TB])
        tot = sb("tot", [P, TB])
        gt = sb("gt", [P, TB, EXPERTS, EXPERTS])
        eq = sb("eq", [P, TB, EXPERTS, EXPERTS])
        before = sb("before", [P, EXPERTS, EXPERTS])
        rank_of = sb("rank_of", [P, TB, EXPERTS])
        gated = sb("gated", [P, TB, EXPERTS])
        h = sb("h", [P, TB, EXPERTS, RANK])
        hth, htl = sb("hth", [ER, T], F32R), sb("htl", [ER, T], F32R)
        loaded = core.sem("m_loaded")
        turned, hi, lo = core.sem("m_turned"), core.sem("m_hi"), core.sem("m_lo")
        route, r = core.sem("m_route"), core.sem("m_r")
        expd, weighted = core.sem("m_expd"), core.sem("m_weighted")
        ht, hth_ready, htl_ready = core.sem("m_ht"), core.sem("m_hth"), core.sem("m_htl")
        outs, copied = core.sem("m_outs"), core.sem("m_copied")
        with nc.Block() as block:

            @block.sync
            def _(sp):
                sp.dma_start(wb[:, :, :], io["wb"].rearrange("(k p) d -> p k d", p=P)).then_inc(loaded, 16)
                sp.dma_start(la[:, :], io["la"].rearrange("e r d -> (e r) d")).then_inc(loaded, 16)
                sp.dma_start(wr[:, :], io["wr"]).then_inc(loaded, 16)
                sp.dma_start(bias[:, :], io["bb"].rearrange("(a n) -> a n", a=1)).then_inc(loaded, 16)
                for k in range(KT):
                    sp.dma_start(lb[:, k, :, :], io["lb"][:, k * P:(k + 1) * P, :].rearrange("e p r -> p e r")).then_inc(loaded, 16)
                sp.dma_start(before[:, :, :], io["before"]).then_inc(loaded, 16)

            pieces = [(k, slice(0, D), wth[:, k, 0:D], wtl[:, k, 0:D]) for k in range(KT)]
            pieces += [(KT, slice(0, HALF), wth[:, :, D:D + ER], wtl[:, :, D:D + ER])]
            pieces += [(KT + 1, slice(0, KT * EXPERTS), wth[:, :, D + ER:NW], wtl[:, :, D + ER:NW])]
            pieces += [(KT + 2, slice(0, D), bth[:, :], btl[:, :])]

            def bank_view(n, cols):
                v = core.banks[n % 4][:, cols]
                if n == KT:
                    return v.rearrange("p (k c) -> p k c", k=KT)
                if n == KT + 1:
                    return v.rearrange("p (k c) -> p k c", k=KT)
                return v

            @block.scalar
            def _(act):
                for n, cols, h_, l_ in pieces:
                    act.wait_ge(turned, n + 1)
                    act.activation(h_, bank_view(n, cols), ACT.Copy).then_inc(hi, 1)
                act.wait_ge(r, 2)
                act.activation(prob[:, :, :], prob[:, :, :], ACT.Exp).then_inc(expd, 1)
                for n in range(2):
                    act.wait_ge(ht, n + 1)
                    act.activation(hth[:, n * HALF:(n + 1) * HALF], core.banks[n][:, :], ACT.Copy).then_inc(hth_ready, 1)
                for b in range(TB):
                    act.wait_ge(outs, b + 1)
                    if b % 2:
                        act.activation(acc[:, b, :], core.banks[b % 4][:, :], ACT.Copy).then_inc(copied, 1)
                    else:
                        act.activation(acc[:, b, :], core.banks[b % 4][:, :], ACT.Copy).then_inc(copied, 1)

            @block.vector
            def _(dve):
                for n, cols, h_, l_ in pieces:
                    dve.wait_ge(hi, n + 1)
                    dve.tensor_tensor(l_, bank_view(n, cols), h_.bitcast(F32), ALU.subtract).then_inc(lo, 1)
                steps = [0]

                def step(ins):
                    steps[0] += 1
                    ins.then_inc(r, 1)
                    dve.wait_ge(r, steps[0])

                wide = lambda t: t[:, :, :].unsqueeze(3).to_broadcast([P, TB, EXPERTS, EXPERTS])
                across = lambda t: t[:, :, :].unsqueeze(2).to_broadcast([P, TB, EXPERTS, EXPERTS])
                dve.wait_ge(route, 1)
                step(dve.tensor_reduce(top[:, :], core.slots[1][:, 0:TB * EXPERTS].rearrange("p (b e) -> p b e", b=TB), AX.X, ALU.max))
                step(dve.tensor_tensor(prob[:, :, :], core.slots[1][:, 0:TB * EXPERTS].rearrange("p (b e) -> p b e", b=TB),
                                       top[:, :].unsqueeze(2).to_broadcast([P, TB, EXPERTS]), ALU.subtract))
                dve.wait_ge(expd, 1)
                step(dve.tensor_reduce(tot[:, :], prob[:, :, :], AX.X, ALU.add))
                step(dve.reciprocal(tot[:, :], tot[:, :]))
                step(dve.tensor_tensor(prob[:, :, :], prob[:, :, :], tot[:, :].unsqueeze(2).to_broadcast([P, TB, EXPERTS]), ALU.mult))
                step(dve.tensor_tensor(gt[:, :, :, :], across(prob), wide(prob), ALU.is_gt))
                step(dve.tensor_tensor(eq[:, :, :, :], across(prob), wide(prob), ALU.is_equal))
                step(dve.tensor_tensor(eq[:, :, :, :], eq[:, :, :, :],
                                       before[:, :, :].unsqueeze(1).to_broadcast([P, TB, EXPERTS, EXPERTS]), ALU.mult))
                step(dve.tensor_tensor(gt[:, :, :, :], gt[:, :, :, :], eq[:, :, :, :], ALU.add))
                step(dve.tensor_reduce(rank_of[:, :, :], gt[:, :, :, :], AX.X, ALU.add))
                step(dve.scalar_tensor_tensor(gated[:, :, :], rank_of[:, :, :], 2.0, prob[:, :, :], ALU.is_lt, ALU.mult))
                step(dve.tensor_reduce(tot[:, :], gated[:, :, :], AX.X, ALU.add))
                step(dve.reciprocal(tot[:, :], tot[:, :]))
                step(dve.scalar_tensor_tensor(gated[:, :, :], gated[:, :, :], LORA_SCALE,
                                              tot[:, :].unsqueeze(2).to_broadcast([P, TB, EXPERTS]), ALU.mult, ALU.mult))
                dve.tensor_tensor(h[:, :, :, :], core.slots[0][:, :].rearrange("p (b e r) -> p b e r", b=TB, r=RANK),
                                  gated[:, :, :].unsqueeze(3).to_broadcast([P, TB, EXPERTS, RANK]), ALU.mult).then_inc(weighted, 1)
                for n in range(2):
                    dve.wait_ge(hth_ready, n + 1)
                    cols = slice(n * HALF, (n + 1) * HALF)
                    dve.tensor_tensor(htl[:, cols], core.banks[n][:, :], hth[:, cols].bitcast(F32), ALU.subtract).then_inc(htl_ready, 1)

            @block.tensor
            def _(pe):
                pe.wait_ge(loaded, 16 * (5 + KT))
                for n in range(KT + 3):
                    if n >= 4:
                        pe.wait_ge(lo, n - 3)
                    bank = core.banks[n % 4]
                    for k in range(KT):
                        if n < KT:
                            t = pe.transpose(bank[:, k * P:(k + 1) * P], wb[:, k, n * P:(n + 1) * P], ident[:, :])
                        elif n == KT:
                            t = pe.transpose(bank[:, k * P:(k + 1) * P], la[:, k * P:(k + 1) * P], ident[:, :])
                        elif n == KT + 1:
                            t = pe.transpose(bank[:, k * EXPERTS:(k + 1) * EXPERTS], wr[:, k * P:(k + 1) * P],
                                             ident[0:EXPERTS, 0:EXPERTS])
                        else:
                            t = pe.transpose(bank[:, k * P:(k + 1) * P],
                                             lb[:, k, :, :].rearrange("p e r -> p (e r)"), ident[:, :])
                    t.then_inc(turned, 1)
                pe.wait_ge(lo, KT + 3)
                for b in range(TB):
                    toks = slice(b * P, (b + 1) * P)
                    for out, c0, c1 in ((core.slots[1][:, b * EXPERTS:(b + 1) * EXPERTS], D + ER, NW),
                                        (core.slots[0][:, b * ER:(b + 1) * ER], D, D + ER)):
                        pairs = [pr for k in range(KT) for pr in three(xh[:, k, toks], xl[:, k, toks],
                                                                       wth[:, k, c0:c1], wtl[:, k, c0:c1])]
                        mm = products(pe, out, pairs)
                mm.then_inc(route, 1)
                pe.wait_ge(weighted, 1)
                for n in range(2):
                    for b in range(4):
                        t = pe.transpose(core.banks[n][:, b * P:(b + 1) * P],
                                         h[:, 4 * n + b, :, :].rearrange("p e r -> p (e r)"), ident[:, :])
                    t.then_inc(ht, 1)
                for b in range(TB):
                    toks = slice(b * P, (b + 1) * P)
                    pe.wait_ge(htl_ready, 2)
                    if b >= 4:
                        pe.wait_ge(copied, b - 3)
                    pairs = [pr for k in range(KT) for pr in three(xh[:, k, toks], xl[:, k, toks],
                                                                   wth[:, k, 0:D], wtl[:, k, 0:D])]
                    pairs += three(hth[:, toks], htl[:, toks], bth[:, :], btl[:, :])
                    products(pe, core.banks[b % 4][:, :], pairs, True, False)
                    mm = pe.matmul(core.banks[b % 4][:, :], ones[0:1, :], bias[0:1, :], start=False, stop=True)
                    mm.then_inc(outs, 1)


def program(nc, io, out):
    with ExitStack() as ctx:
        core = Core(nc, ctx)
        sb = lambda n, shape, dt=F32: ctx.enter_context(nc.sbuf_tensor(n, shape, dt))
        ident, mask, eps, ones = sb("ident", [P, P]), sb("mask", [P, T]), sb("eps", [P, 1]), sb("ones", [P, P])
        consts = (ident, mask, eps, ones)
        acc = sb("acc", [P, TB, D])
        xh, xl = sb("xh", [P, KT, T], F32R), sb("xl", [P, KT, T], F32R)
        x_scr = [nc.dram_tensor(f"x_after_{i}", (T, D), F32).ap() for i in range(3)]
        q_scr = nc.dram_tensor("q_parts", (2, D, T), F32).ap()
        k_scr = nc.dram_tensor("k_parts", (2, P, T), F32).ap()
        constants(core, consts, io["ident"], io["mask"])
        resid = io["L0_attn_resid"].rearrange("b t d -> (b t) d")
        seam(core, "s0", consts, acc, xh, xl, resid, None, False, False)
        with nc.sbuf_tensor("v0", [P, TB, P], F32R) as v0, nc.sbuf_tensor("v0l", [P, TB, P], F32R) as v0l:
            project_layer0(core, consts, xh, xl, io["L0_attn_Wq"], io["L0_attn_Wk"], io["L0_attn_Wv"],
                           io["cos"], io["sin"], q_scr, k_scr, v0, v0l)
            attention(core, "a0", 0, consts, acc, xh, xl,
                      {"q": q_scr, "k": k_scr, "v0": v0, "v0l": v0l, "wo": io["L0_attn_Wo"]})
        seam(core, "s1", consts, acc, xh, xl, resid, x_scr[0], True, False)
        swiglu(core, consts, acc, xh, xl,
               {"qgu": io["L0_ffn_qweight_gu"], "zgu": io["L0_ffn_qzeros_gu"], "sgu": io["L0_ffn_scales_gu"],
                "ggu": io["L0_ffn_g_idx_gu"], "qdn": io["L0_ffn_qweight_down"], "zdn": io["L0_ffn_qzeros_down"],
                "sdn": io["L0_ffn_scales_down"], "gdn": io["L0_ffn_g_idx_down"], "shift": io["shift"]})
        seam(core, "s2", consts, acc, xh, xl, x_scr[0], x_scr[1], True, False)
        attention(core, "a1", 1, consts, acc, xh, xl,
                  {"wq": io["L1_attn_w_q"], "wk": io["L1_attn_w_k"], "wv": io["L1_attn_w_v"], "wo": io["L1_attn_w_o"]})
        seam(core, "s3", consts, acc, xh, xl, x_scr[1], x_scr[2], True, False)
        lora_mixture(core, consts, acc, xh, xl,
                     {"wb": io["L1_ffn_W_base"], "bb": io["L1_ffn_b_base"], "wr": io["L1_ffn_W_router"],
                      "la": io["L1_ffn_lora_A"], "lb": io["L1_ffn_lora_B"], "before": io["before"]})
        seam(core, "s4", consts, acc, xh, xl, x_scr[2], out.rearrange("b t d -> (b t) d"), True, True)


def shape_constants():
    import math

    import numpy as np

    f32 = np.float32
    i = np.arange(0, DH0, 2, dtype=f32) / f32(DH0)
    freq = (f32(1.0 / (2.0 * math.pi)) * f32(500000.0) ** (-i)).astype(f32)
    factor, lo, hi, context = 32.0, 1.0, 4.0, 1024
    scaled = np.where(freq < f32(lo / context), freq / f32(factor), freq)
    smooth = np.clip((f32(context) * freq - f32(lo)) / f32(hi - lo), f32(0), f32(1))
    mixed = (f32(1) - smooth) * (freq / f32(factor)) + smooth * freq
    mid = (freq >= f32(lo / context)) & (freq <= f32(hi / context))
    freq = np.where(mid, mixed, scaled).astype(f32)
    phase = (f32(2.0 * math.pi) * np.arange(T).astype(f32)[:, None] * freq[None, :]).astype(f32)
    cos, sin = np.cos(phase).T, np.sin(phase).T
    return {
        "cos": np.ascontiguousarray(np.tile(np.concatenate([cos, cos]), (P // DH0, 1)), dtype=f32),
        "sin": np.ascontiguousarray(np.tile(np.concatenate([-sin, sin]), (P // DH0, 1)), dtype=f32),
        "ident": np.eye(P, dtype=f32),
        "mask": np.concatenate([np.zeros((P, T - P), f32), np.triu(np.full((P, P), MASKED, f32), 1)], axis=1),
        "shift": (4 * (np.arange(P) % NIBBLES)).astype(np.uint32)[:, None],
        "before": np.ascontiguousarray(np.broadcast_to(np.tril(np.ones((EXPERTS, EXPERTS), f32), -1), (P, EXPERTS, EXPERTS))),
    }


_INS = ["L0_attn_resid", "L0_attn_Wq", "L0_attn_Wk", "L0_attn_Wv", "L0_attn_Wo", "L0_ffn_qweight_gu",
        "L0_ffn_qzeros_gu", "L0_ffn_scales_gu", "L0_ffn_g_idx_gu", "L0_ffn_qweight_down", "L0_ffn_qzeros_down",
        "L0_ffn_scales_down", "L0_ffn_g_idx_down", "L1_attn_w_q", "L1_attn_w_k", "L1_attn_w_v", "L1_attn_w_o",
        "L1_ffn_W_base", "L1_ffn_b_base", "L1_ffn_W_router", "L1_ffn_lora_A", "L1_ffn_lora_B"]


def kernel(**inputs):
    import numpy as np

    import concourse.bacc as bacc
    from concourse.bass_utils import run_bass_kernel_spmd

    nc = bacc.Bacc("TRN2", target_bir_lowering=False, num_devices=1)
    arrays = {name: np.ascontiguousarray(inputs[name]) for name in _INS}
    arrays.update(shape_constants())
    fed = {f"in_{name}": a for name, a in arrays.items()}
    io = {name: nc.dram_tensor(f"in_{name}", a.shape, mybir.dt.from_np(a.dtype), kind="ExternalInput").ap()
          for name, a in arrays.items()}
    out = nc.dram_tensor("out_x", (1, T, D), F32, kind="ExternalOutput").ap()
    program(nc, io, out)
    got = run_bass_kernel_spmd(nc, [fed], core_ids=[0])
    return got.results[0]["out_x"]
```

```python
from contextlib import ExitStack, contextmanager

import concourse.bass as bass
import concourse.mybir as mybir

F32 = mybir.dt.float32
F32R = mybir.dt.float32r
I32 = mybir.dt.int32
U32 = mybir.dt.uint32
ALU = mybir.AluOpType
ACT = mybir.ActivationFunctionType
AX = mybir.AxisListType

P = 128
T = 1024
D = 512
KT = D // P
TB = T // P
HALF = 512
EPS = 1e-5
MASKED = 1e30

HEADS = 32
KV = 8
GH = HEADS // KV
DH0 = D // HEADS
DH1 = 128

INTER = 1376
NIBBLES = 8
GU_GROUPS = 4
DN_GROUPS = INTER // 128
FT = -(-INTER // P)
F_LAST = INTER - (FT - 1) * P

EXPERTS = 8
RANK = 16
LORA_SCALE = 2.0


class Core:

    def __init__(self, nc, ctx):
        self.nc, self.own = nc, []
        self.banks = [ctx.enter_context(nc.psum_tensor(f"bank{i}", [P, HALF], F32)) for i in range(4)]
        self.slots = [ctx.enter_context(nc.psum_tensor(f"slot{i}", [P, 2 * HALF], F32)) for i in range(2)]

    def sem(self, name):
        handle = self.nc.alloc_semaphore(name=name)
        self.own.append(handle)
        return handle

    @contextmanager
    def stage(self, name):
        before, self.own = self.own, []
        with ExitStack() as ctx:
            yield lambda n, shape, dt=F32: ctx.enter_context(self.nc.sbuf_tensor(f"{name}_{n}", shape, dt))
            self.nc.clear_and_free_semaphores(self.own)
            self.nc.all_engine_barrier()
        self.own = before


def constants(core, tensors, ident_d, mask_d):
    nc = core.nc
    ident, mask, eps, ones = tensors
    loaded = core.sem("const_loaded")
    set_ = core.sem("const_set")
    with nc.Block() as block:

        @block.sync
        def _(sp):
            sp.dma_start(ident[:, :], ident_d).then_inc(loaded, 16)
            sp.dma_start(mask[:, :], mask_d).then_inc(loaded, 16)
            sp.wait_ge(loaded, 32)

        @block.vector
        def _(dve):
            dve.memset(eps[:, :], EPS).then_inc(set_, 1)
            dve.memset(ones[:, :], 1.0).then_inc(set_, 1)
            dve.wait_ge(set_, 2)


def seam(core, name, consts, acc, xh, xl, x_src, x_dst, residual, last):
    nc = core.nc
    ident, mask, eps, ones = consts
    src = x_src.rearrange("(b p) d -> p b d", p=P)
    dst = x_dst.rearrange("(b p) d -> p b d", p=P) if x_dst is not None else None
    with core.stage(name) as sb:
        x_in = sb("x_in", [P, TB, D]) if residual else acc
        xn = sb("xn", [P, TB, D])
        stats = [sb(f"stats{i}", [P, TB, 6]) for i in range(2)]
        mv = [sb(f"mv{i}", [P, TB, 2]) for i in range(2)]
        std = [sb(f"std{i}", [P, TB]) for i in range(2)]
        rstd = [sb(f"rstd{i}", [P, TB]) for i in range(2)]
        x_loaded = [core.sem(f"{name}_x_loaded{h}") for h in range(2)]
        stored = core.sem(f"{name}_stored")
        stat = core.sem(f"{name}_stat")
        std_ready = core.sem(f"{name}_std_ready")
        scaled = core.sem(f"{name}_scaled")
        x_new = core.sem(f"{name}_x_new")
        xn_ready = core.sem(f"{name}_xn_ready")
        turned = core.sem(f"{name}_turned")
        hi_ready = core.sem(f"{name}_hi_ready")
        lo_ready = core.sem(f"{name}_lo_ready")
        hb = TB // 2
        with nc.Block() as block:

            @block.sync
            def _(sp):
                for h in range(2):
                    sp.dma_start(x_in[:, h * hb:(h + 1) * hb, :], src[:, h * hb:(h + 1) * hb, :]).then_inc(x_loaded[h], 16)
                if dst is not None:
                    for h in range(2):
                        sp.wait_ge(x_new, (h + 1) * hb)
                        sp.dma_start(dst[:, h * hb:(h + 1) * hb, :], acc[:, h * hb:(h + 1) * hb, :]).then_inc(stored, 16)
                    sp.wait_ge(stored, 32)

            @block.scalar
            def _(act):
                for n in range((2 if residual else 0) + (0 if last else 2)):
                    i, h = (n // 2 if residual else 1), n % 2
                    act.wait_ge(stat, n * (2 * hb + 1) + 2 * hb)
                    act.activation(std[i][:, h * hb:(h + 1) * hb], mv[i][:, h * hb:(h + 1) * hb, 1], ACT.Sqrt,
                                   bias=eps[:, 0:1]).then_inc(std_ready, 1)
                if not last:
                    for n in range(2 * KT):
                        act.wait_ge(turned, n + 1)
                        k, h = n % KT, n // KT
                        act.activation(xh[:, k, h * HALF:(h + 1) * HALF], core.banks[n % 4][:, :],
                                       ACT.Copy).then_inc(hi_ready, 1)

            @block.vector
            def _(dve):
                count = [0]

                def statistics(i, h, ready):
                    blocks = range(h * hb, (h + 1) * hb)
                    for b in blocks:
                        ready(b)
                        dve.bn_stats(stats[i][:, b, :], acc[:, b, :]).then_inc(stat, 1)
                    for n, b in enumerate(blocks):
                        dve.wait_ge(stat, count[0] + n + 1)
                        dve.bn_aggr(mv[i][:, b, :], stats[i][:, b, :]).then_inc(stat, 1)
                    count[0] += 2 * hb

                def root(i, h, n):
                    dve.wait_ge(std_ready, n)
                    dve.reciprocal(rstd[i][:, h * hb:(h + 1) * hb], std[i][:, h * hb:(h + 1) * hb]).then_inc(stat, 1)
                    count[0] += 1
                    dve.wait_ge(stat, count[0])

                done = 0
                if residual:
                    for h in range(2):
                        statistics(0, h, lambda b: None)
                        done += 1
                        root(0, h, done)
                        for b in range(h * hb, (h + 1) * hb):
                            dve.tensor_scalar(acc[:, b, :], acc[:, b, :], mv[0][:, b, 0:1], rstd[0][:, b:b + 1],
                                              ALU.subtract, ALU.mult).then_inc(scaled, 1)
                        dve.wait_ge(x_loaded[h], 16)
                        for b in range(h * hb, (h + 1) * hb):
                            dve.wait_ge(scaled, b + 1)
                            dve.tensor_tensor(acc[:, b, :], acc[:, b, :], x_in[:, b, :], ALU.add).then_inc(x_new, 1)
                else:
                    for h in range(2):
                        dve.wait_ge(x_loaded[h], 16)
                if last:
                    return
                for h in range(2):
                    statistics(1, h, (lambda b: dve.wait_ge(x_new, b + 1)) if residual else (lambda b: None))
                    done += 1
                    root(1, h, done)
                    for b in range(h * hb, (h + 1) * hb):
                        dve.tensor_scalar(xn[:, b, :], acc[:, b, :], mv[1][:, b, 0:1], rstd[1][:, b:b + 1],
                                          ALU.subtract, ALU.mult).then_inc(xn_ready, 1)
                for n in range(2 * KT):
                    dve.wait_ge(hi_ready, n + 1)
                    k, h = n % KT, n // KT
                    cols = slice(h * HALF, (h + 1) * HALF)
                    dve.tensor_tensor(xl[:, k, cols], core.banks[n % 4][:, :], xh[:, k, cols].bitcast(F32),
                                      ALU.subtract).then_inc(lo_ready, 1)

            @block.tensor
            def _(pe):
                if last:
                    return
                for n in range(2 * KT):
                    k, h = n % KT, n // KT
                    if n >= 4:
                        pe.wait_ge(lo_ready, n - 3)
                    for b in range(hb):
                        pe.wait_ge(xn_ready, h * hb + b + 1)
                        t = pe.transpose(core.banks[n % 4][:, b * P:(b + 1) * P], xn[:, h * hb + b, k * P:(k + 1) * P],
                                         ident[:, :])
                    t.then_inc(turned, 1)


def products(pe, out, pairs, start=True, stop=True):
    for n, (w, m) in enumerate(pairs):
        mm = pe.matmul(out, w, m, start=start and n == 0, stop=stop and n == len(pairs) - 1)
    return mm


def three(wh, wl, mh, ml):
    return [(wh, mh), (wh, ml), (wl, mh)]


def project_layer0(core, consts, xh, xl, wq_d, wk_d, wv_d, cos_d, sin_d, q_scr, k_scr, v0, v0l):
    nc = core.nc
    NW = 2 * D + 3 * P
    SW = D + 2 * P
    QK = D // P + 1
    with core.stage("p0") as sb:
        raw = sb("raw", [P, KT, SW])
        wh = sb("wh", [P, KT, NW], F32R)
        wl = sb("wl", [P, KT, NW], F32R)
        cos, sin = sb("cos", [P, T]), sb("sin", [P, T])
        direct = sb("direct", [P, 2, HALF])
        swapped = sb("swapped", [P, 2, HALF])
        rot = sb("rot", [P, 2, HALF])
        rh = sb("rh", [P, 2, HALF], F32R)
        rl = sb("rl", [P, 2, HALF], F32R)
        w_loaded, tables = core.sem("p0_w_loaded"), core.sem("p0_tables")
        w_split = core.sem("p0_w_split")
        w_hi = core.sem("p0_w_hi")
        w_swap = core.sem("p0_w_swap")
        proj = core.sem("p0_proj")
        prod = core.sem("p0_prod")
        rotated = core.sem("p0_rotated")
        rh_ready, rl_ready = core.sem("p0_rh_ready"), core.sem("p0_rl_ready")
        sent = [core.sem(f"p0_sent{i}") for i in range(2)]
        v_proj, v_hi, v_lo = core.sem("p0_v_proj"), core.sem("p0_v_hi"), core.sem("p0_v_lo")
        CH = 2 * QK

        def swap_view(t, a, b):
            return t[:, :, a:b].rearrange("p k (h s i) -> p k h s i", s=2, i=DH0 // 2)

        with nc.Block() as block:

            @block.sync
            def _(sp):
                for w, a, b in ((wq_d, 0, D), (wk_d, D, D + P), (wv_d, D + P, SW)):
                    sp.dma_start(raw[:, :, a:b], w.rearrange("(k p) n -> p k n", p=P)).then_inc(w_loaded, 16)
                sp.dma_start(cos[:, :], cos_d).then_inc(tables, 16)
                sp.dma_start(sin[:, :], sin_d).then_inc(tables, 16)
                for n in range(CH):
                    m, h = n // 2, n % 2
                    sp.wait_ge(rl_ready, n + 1)
                    for part, r in ((0, rh), (1, rl)):
                        out = (q_scr[part, m * P:(m + 1) * P, h * HALF:(h + 1) * HALF] if m < QK - 1
                               else k_scr[part, :, h * HALF:(h + 1) * HALF])
                        sp.dma_start(out, r[:, n % 2, :].bitcast(F32)).then_inc(sent[n % 2], 16)
                for i in range(2):
                    sp.wait_ge(sent[i], 32 * (CH // 2))

            @block.scalar
            def _(act):
                act.wait_ge(w_loaded, 48)
                act.activation(wh[:, :, 0:SW], raw[:, :, :], ACT.Copy).then_inc(w_hi, 1)
                for n in range(CH):
                    act.wait_ge(rotated, n + 1)
                    if n >= 2:
                        act.wait_ge(sent[n % 2], 32 * (n // 2))
                    act.activation(rh[:, n % 2, :], rot[:, n % 2, :], ACT.Copy,
                                   scale=(-DH0 ** -0.5 if n // 2 < QK - 1 else 1.0)).then_inc(rh_ready, 1)
                act.wait_ge(v_proj, 1)
                for b in range(2):
                    act.activation(v0[:, 4 * b:4 * b + 4, :], core.banks[b][:, :].rearrange("p (b n) -> p b n", n=P),
                                   ACT.Copy).then_inc(v_hi, 1)

            @block.gpsimd
            def _(pool):
                pool.wait_ge(w_split, 1)
                for t in (wh, wl):
                    for a, b, o in ((0, D, SW), (D, D + P, SW + D)):
                        for s in range(2):
                            pool.tensor_copy(swap_view(t, o, o + b - a)[:, :, :, s, :],
                                             swap_view(t, a, b)[:, :, :, 1 - s, :]).then_inc(w_swap, 1)

            @block.vector
            def _(dve):
                dve.wait_ge(w_hi, 1)
                dve.tensor_tensor(wl[:, :, 0:SW], raw[:, :, :], wh[:, :, 0:SW].bitcast(F32),
                                  ALU.subtract).then_inc(w_split, 1)
                dve.wait_ge(tables, 32)
                for n in range(CH):
                    m, h = n // 2, n % 2
                    cols = slice(h * HALF, (h + 1) * HALF)
                    scale = -DH0 ** -0.5 if m < QK - 1 else 1.0
                    dve.wait_ge(proj, n + 1)
                    dve.tensor_tensor(direct[:, n % 2, :], core.slots[n % 2][:, 0:HALF], cos[:, cols],
                                      ALU.mult).then_inc(prod, 1)
                    dve.tensor_tensor(swapped[:, n % 2, :], core.slots[n % 2][:, HALF:2 * HALF], sin[:, cols],
                                      ALU.mult).then_inc(prod, 1)
                    dve.wait_ge(prod, 2 * n + 2)
                    dve.tensor_tensor(rot[:, n % 2, :], direct[:, n % 2, :], swapped[:, n % 2, :],
                                      ALU.add).then_inc(rotated, 1)
                    dve.wait_ge(rh_ready, n + 1)
                    dve.scalar_tensor_tensor(rl[:, n % 2, :], rot[:, n % 2, :], scale, rh[:, n % 2, :].bitcast(F32),
                                             ALU.mult, ALU.subtract).then_inc(rl_ready, 1)
                for b in range(2):
                    dve.wait_ge(v_hi, b + 1)
                    dve.tensor_tensor(v0l[:, 4 * b:4 * b + 4, :], core.banks[b][:, :].rearrange("p (b n) -> p b n", n=P),
                                      v0[:, 4 * b:4 * b + 4, :].bitcast(F32), ALU.subtract).then_inc(v_lo, 1)

            @block.tensor
            def _(pe):
                pe.wait_ge(w_split, 1)
                for b in range(TB):
                    toks = slice(b * P, (b + 1) * P)
                    vc = slice(D + P, SW)
                    pairs = [pr for k in range(KT)
                             for pr in three(xh[:, k, toks], xl[:, k, toks], wh[:, k, vc], wl[:, k, vc])]
                    mm = products(pe, core.banks[b // 4][:, (b % 4) * P:(b % 4 + 1) * P], pairs)
                mm.then_inc(v_proj, 1)
                pe.wait_ge(w_swap, 8)
                for n in range(CH):
                    m, h = n // 2, n % 2
                    cols = slice(h * HALF, (h + 1) * HALF)
                    if n >= 2:
                        pe.wait_ge(prod, 2 * (n - 1))
                    for s, base in ((0, 0), (1, SW)):
                        wc = slice(base + m * P, base + (m + 1) * P)
                        pairs = [pr for k in range(KT)
                                 for pr in three(wh[:, k, wc], wl[:, k, wc], xh[:, k, cols], xl[:, k, cols])]
                        mm = products(pe, core.slots[n % 2][:, s * HALF:(s + 1) * HALF], pairs)
                    mm.then_inc(proj, 1)


def attention(core, name, layer, consts, acc, xh, xl, io):
    nc = core.nc
    ident, mask, eps, ones = consts
    one = layer == 1
    UNITS = 2 * GH
    AHEAD = 2
    NB = 2 * AHEAD
    BLOCKS = ((0, 1, 6, 7), (2, 3, 4, 5))
    KBS = (8, 6)
    TURN = GH * sum(KBS)
    LAG = 2
    first_tile = [sum(KBS[v % 2] for v in range(u)) for u in range(UNITS + 1)]
    S_AT = ((1, 3, 5, 6), (0, 1, 3, 4)) if one else ((0, 2, 4, 6), (0, 1, 3, 4))
    NORM_AT = (3, 2) if one else (8, 6)
    NORM_AHEAD = 1 if one else AHEAD

    def steps(u, has_next):
        v = u + AHEAD
        out = [[] for _ in range(KBS[u % 2])]
        if v < UNITS or has_next:
            for b, t in zip((3, 2, 1, 0), S_AT[u % 2]):
                out[t].append(("S", v, b))
        j = (u + 3) // 2
        if one and u % 2 and (j < GH or has_next):
            out[2].append(("Q", j))
        if one and u == UNITS - 3 and has_next:
            out[5].append(("K", GH))
        if one and u == UNITS // 2:
            for c, t in enumerate((2, 4, 5, 7)):
                out[t].append(("W", c))
        return out

    def tail(has_next):
        if one and has_next:
            return [("VT", 0), ("VT", 1), ("W", 4), ("V", GH), ("W", 5), ("W", 6), ("W", 7)]
        return [("W", 4 + c) for c in range(4)]

    def schedule(has_next):
        return [it for u in range(UNITS) for tile in steps(u, has_next) for it in tile] + tail(has_next)

    start = [("K", 0), ("VT", 0), ("VT", 1), ("Q", 0), ("V", GH), ("Q", 1)] if one else []
    start += [("S", u, b) for u in range(AHEAD) for b in (3, 2, 1, 0)]
    N0, N = len(start), len(schedule(True))
    assert N % 2 == 0
    place_start = {it: n - N0 for n, it in enumerate(start)}
    place_turn = {it: n for n, it in enumerate(schedule(True))}
    place_last = {it: n for n, it in enumerate(schedule(False))}
    HI0 = sum(it[0] in ("K", "Q", "V") for it in start)

    with core.stage(name) as sb:
        probs = [sb(f"probs{i}", [P, 18 * P]) for i in range(NB)]
        pt_h = sb("pt_h", [P, 4, HALF], F32R)
        pt_l = sb("pt_l", [P, 4, HALF], F32R)
        low = sb("low", [P, NB, 4])
        sums = sb("sums", [P, NB, 4])
        rinv = sb("rinv", [P, NB, 4])
        AJ = 2 if one else 1
        at_h = sb("at_h", [P, AJ, T], F32R)
        at_l = sb("at_l", [P, AJ, T], F32R)
        wo_h = sb("wo_h", [P, AJ, D], F32R)
        wo_l = sb("wo_l", [P, AJ, D], F32R)
        wo_raw = sb("wo_raw", [P, 2, D])
        if one:
            qh, ql = sb("qh", [P, 2, T], F32R), sb("ql", [P, 2, T], F32R)
            kh, kl = sb("kh", [P, T], F32R), sb("kl", [P, T], F32R)
            vh, vl = sb("vh", [P, TB, P], F32R), sb("vl", [P, TB, P], F32R)
            wq_raw, wkv_raw = sb("wq_raw", [P, 2, KT, P]), sb("wkv_raw", [P, KT, 2 * P])
            wqh, wql = sb("wqh", [P, 2, KT, P], F32R), sb("wql", [P, 2, KT, P], F32R)
            vt = sb("vt", [P, T])
            wkvh, wkvl = sb("wkvh", [P, KT, 2 * P], F32R), sb("wkvl", [P, KT, 2 * P], F32R)
        else:
            DQ = 4 * DH0
            q_stack = sb("q_stack", [DQ, GH, T], F32R)
            k_stack = sb("k_stack", [DQ, KV, T], F32R)
            v_pad = sb("v_pad", [P, TB, GH, P], F32R)
        tbank, obank = core.banks[0:2], core.banks[2:4]

        kv_loaded = core.sem(f"{name}_kv_loaded")
        q_loaded = [core.sem(f"{name}_q_loaded{i}") for i in range(2 if one else GH)]
        wo_loaded = [core.sem(f"{name}_wo_loaded{i}") for i in range(2)]
        kv_split = core.sem(f"{name}_kv_split")
        q_split = core.sem(f"{name}_q_split")
        wo_split = core.sem(f"{name}_wo_split")
        w_hi = core.sem(f"{name}_w_hi")
        slot_full = core.sem(f"{name}_slot_full")
        hi_done = core.sem(f"{name}_hi_done")
        slot_free = core.sem(f"{name}_slot_free")
        exp_done = core.sem(f"{name}_exp_done")
        inv_done = core.sem(f"{name}_inv_done")
        norm_done = core.sem(f"{name}_norm_done")
        turned = core.sem(f"{name}_turned")
        pt_hi = core.sem(f"{name}_pt_hi")
        pt_lo = core.sem(f"{name}_pt_lo")
        pv_done = core.sem(f"{name}_pv_done")
        out_hi = core.sem(f"{name}_out_hi")
        out_lo = core.sem(f"{name}_out_lo")
        acc_zero = core.sem(f"{name}_acc_zero")
        own_pe, own_dve, own_pool = (core.sem(f"{name}_own_{e}") for e in ("pe", "dve", "pool"))
        pad_zero = core.sem(f"{name}_pad_zero")
        OUTS = UNITS if one else 2
        HIS = 2 + GH
        W_FIRST = [("kv", 0), ("q", 0), ("q", 1)]
        W_TURN = [("q", 2), ("wo", 0), ("q", 3), ("wo", 1), ("kv", 1), ("q", GH), ("q", GH + 1), ("wo", 2), ("wo", 3)]
        W_LAST = [w for w in W_TURN if w[0] == "wo" or w[0] == "q" and w[1] < GH]
        NW = len(W_TURN)

        full = lambda g, n: (g + 1) * N + (N0 + n + 1)
        read = lambda g, n: g * N + (N0 + n + 1 + 2)
        vacant = lambda g, n: g * N + (N0 + n + 1)
        slot_of = lambda n: core.slots[(N0 + n) % 2]
        full_before = lambda g, it, first: g * N + max(N0 + place_turn[it] + 1, N + N0 + place_start[first] + 1)
        read_before = lambda g, it, first: g * N + max(N0 + place_turn[it] + 3 - N, N0 + place_start[first] + 3)

        def out_index(u):
            return u if one else ({UNITS - 2: 0, UNITS - 1: 1}.get(u))

        width = lambda u, b: (BLOCKS[u % 2][b] + 1) * P
        offset = lambda u, b: sum(width(u, a) for a in range(b))
        block_of = lambda u, b: probs[u % NB][:, offset(u, b):offset(u, b) + width(u, b)]
        tile_col = lambda u, kb: sum(q < kb for q in BLOCKS[u % 2]) * P

        def out_view(t, j, u):
            if u % 2:
                return t[:, j, 2 * P:6 * P]
            return t[:, j, :].rearrange("p (a c) -> p a c", a=4)[:, 0:4:3, :]

        def bank_out(u):
            return obank[u % 2][:, :] if u % 2 else obank[u % 2][:, :].rearrange("p (a c) -> p a c", a=2)

        def turns(eng, turn):
            with eng.Fori(0, KV - 1) as g:
                turn(g, place_turn, True)
            turn(KV - 1, place_last, False)

        with nc.Block() as block:

            @block.sync
            def _(sp):
                def load_q(g, j):
                    for rows in range(4):
                        sp.dma_start(q_stack[rows * DH0:(rows + 1) * DH0, j, :].bitcast(F32),
                                     io["q"][rows % 2][bass.ds(g * (GH * DH0) + j * DH0, DH0), :]).then_inc(q_loaded[j], 16)

                def load(g, what, j):
                    if what == "kv":
                        sp.wait_ge(kv_split, g + (j + 1))
                        for s, w in enumerate((io["wk"], io["wv"])):
                            sp.dma_start(wkv_raw[:, :, s * P:(s + 1) * P],
                                         w.rearrange("(k p) n -> p k n", p=P)[:, :, bass.ds(g * P + j * P, P)]).then_inc(kv_loaded, 16)
                    elif what == "q":
                        sp.wait_ge(q_split, g * GH + (j + 1))
                        sp.dma_start(wq_raw[:, j % 2, :, :], io["wq"].rearrange("(k p) n -> p k n", p=P)
                                     [:, :, bass.ds(g * (GH * P) + j * P, P)]).then_inc(q_loaded[j % 2], 16)
                    else:
                        sp.wait_ge(wo_split, g * GH + (j + 1))
                        sp.dma_start(wo_raw[:, j % 2, :],
                                     io["wo"][bass.ds(g * (GH * P) + j * P, P), :]).then_inc(wo_loaded[j % 2], 16)

                def turn(g, place, has_next):
                    if one:
                        for what, j in W_TURN if has_next else W_LAST:
                            load(g, what, j)
                        return
                    sp.wait_ge(wo_split, g + 1)
                    for s in range(2):
                        sp.dma_start(wo_raw[s * 64:(s + 1) * 64, 0, :], io["wo"][bass.ds(g * 64, 64), :]).then_inc(wo_loaded[0], 16)
                    for j in range(GH) if has_next else ():
                        sp.wait_ge(slot_full, full(g, place[("S", 2 * j + 1, 0)] if j else -1))
                        load_q(g + 1, j)

                if one:
                    for what, j in W_FIRST:
                        load(0, what, j)
                else:
                    load_q(0, 0)
                    for part, rows in ((0, 0), (0, 1), (1, 2), (1, 3)):
                        sp.dma_start(k_stack[rows * DH0:(rows + 1) * DH0, :, :].bitcast(F32),
                                     io["k"][part].rearrange("(g i) t -> i g t", i=DH0)).then_inc(kv_loaded, 16)
                    for j in range(1, GH):
                        load_q(0, j)
                turns(sp, turn)

            @block.gpsimd
            def _(pool):
                pool.sem_inc(kv_split, 1)
                pool.sem_inc(q_split, 2)
                pool.sem_inc(wo_split, 2 if one else 1)

                def split(raw, hi, lo, count, done):
                    pool.sem_inc(own_pool, 1)
                    pool.tensor_copy(hi, raw).then_inc(w_hi, 1)
                    pool.wait_ge(w_hi, count)
                    pool.tensor_tensor(lo, raw, hi.bitcast(F32), ALU.subtract).then_inc(done, 1)

                def prepare(g, what, j, count):
                    if what == "kv":
                        pool.wait_ge(kv_loaded, g * 32 + (32 * j + 32))
                        if j:
                            pool.wait_ge(slot_full, full_before(g, ("VT", 1), ("VT", 1)))
                        split(wkv_raw[:, :, :], wkvh[:, :, :], wkvl[:, :, :], count, kv_split)
                    elif what == "q":
                        pool.wait_ge(q_loaded[j % 2], g * 32 + (j // 2) * 16 + 16)
                        if j >= GH:
                            pool.wait_ge(slot_full, full(g, place_turn[("Q", j - 2)]))
                        elif j >= 2:
                            pool.wait_ge(slot_full, full_before(g, ("Q", j + 2), ("Q", j - 2)))
                        split(wq_raw[:, j % 2, :, :], wqh[:, j % 2, :, :], wql[:, j % 2, :, :], count, q_split)
                    else:
                        pool.wait_ge(wo_loaded[j % 2], g * 32 + (j // 2) * 16 + 16)
                        pool.wait_ge(slot_full, full(g, place_turn[("W", 3)]) if j >= 2 else g * N + (N + N0))
                        split(wo_raw[:, j % 2, :], wo_h[:, j % 2, :], wo_l[:, j % 2, :], count, wo_split)

                def place_v(g, j):
                    pool.sem_inc(own_pool, 1)
                    for part, t in ((0, io["v0"]), (1, io["v0l"])):
                        c = part * 64 + j * DH0
                        pool.tensor_copy(v_pad[:, :, j, c:c + DH0], t[:, :, bass.ds(g * DH0, DH0)]).then_inc(kv_split, 1)

                def normalise(g, u):
                    pool.wait_ge(inv_done, g * UNITS + (u + 1))
                    for b in (3, 2, 1, 0):
                        pool.tensor_tensor(block_of(u, b), block_of(u, b),
                                           rinv[:, u % NB, b:b + 1].to_broadcast([P, width(u, b)]), ALU.mult).then_inc(norm_done, 1)

                def turn(g, place, has_next):
                    if one:
                        for n, (what, j) in enumerate(W_TURN if has_next else W_LAST):
                            prepare(g, what, j, g * NW + (n + 1 + len(W_FIRST)))
                        return
                    for u in range(UNITS):
                        if u + AHEAD < UNITS or has_next:
                            normalise(g, u + AHEAD)
                        if u == 1:
                            pool.wait_ge(wo_loaded[0], g * 32 + 32)
                            pool.wait_ge(slot_full, g * N + (N + N0))
                            split(wo_raw[:, 0, :], wo_h[:, 0, :], wo_l[:, 0, :], g + 1, wo_split)
                        if has_next and u % 2 == 0 and u:
                            pool.wait_ge(pv_done, g * TURN + (first_tile[u] + 4))
                            place_v(g + 1, u // 2 - 1)
                    if has_next:
                        pool.wait_ge(pv_done, g * TURN + (TURN + 4))
                        place_v(g + 1, GH - 1)

                if one:
                    for n, (what, j) in enumerate(W_FIRST):
                        prepare(0, what, j, n + 1)
                else:
                    pool.memset(v_pad[:, :, :, :].bitcast(F32), 0.0).then_inc(pad_zero, 1)
                    pool.wait_ge(pad_zero, 1)
                    for j in range(GH):
                        place_v(0, j)
                    for u in range(AHEAD):
                        normalise(0, u)
                turns(pool, turn)

            @block.scalar
            def _(act):
                def high(g, n, count, dst, scale):
                    act.wait_ge(slot_full, full(g, n))
                    act.activation(dst, slot_of(n)[:, :], ACT.Copy, scale=scale).then_inc(hi_done, 1)

                def exp(g, n, u, b):
                    i = u % NB
                    act.wait_ge(slot_free, read(g, n))
                    act.activation(block_of(u, b), block_of(u, b), ACT.Exp, bias=low[:, i, b:b + 1],
                                   scale=-1.0, accum_out=sums[:, i, b:b + 1]).then_inc(exp_done, 1)

                def item(g, place, it):
                    n = place[it]
                    if it[0] == "S":
                        exp(g, n, it[1], it[2])
                    elif it[0] == "K":
                        high(g, n, 0, kh[:, :], 1.0)
                    elif it[0] == "V":
                        high(g, n, 1, vh[:, :, :].rearrange("p b n -> p (b n)"), 1.0)
                    elif it[0] == "Q":
                        high(g, n, 2, qh[:, it[1] % 2, :], -DH1 ** -0.5)

                def turn(g, place, has_next):
                    for u in range(UNITS):
                        late = []
                        for kb, its in enumerate(steps(u, has_next)):
                            n, c = first_tile[u] + kb, tile_col(u, kb)
                            act.wait_ge(turned, g * TURN + (n + 1))
                            act.wait_ge(pv_done, g * TURN + (n + 1))
                            act.activation(pt_h[:, n % 4, c:HALF], tbank[n % 2][:, c:HALF], ACT.Copy).then_inc(pt_hi, 1)
                            for it in late:
                                item(g, place, it)
                            late = its
                        for it in late:
                            item(g, place, it)
                        if out_index(u) is not None:
                            act.wait_ge(pv_done, g * TURN + (first_tile[u + 1] + 4))
                            if one:
                                act.wait_ge(slot_full, full(g, place[("W", 3)]) if u >= 4 else g * N + (N + N0))
                            act.activation(out_view(at_h, u // 2 % AJ, u), bank_out(u), ACT.Copy).then_inc(out_hi, 1)
                    if one and has_next:
                        item(g, place, ("V", GH))

                for it in start:
                    item(0, place_start, it)
                turns(act, turn)

            @block.vector
            def _(dve):
                dve.sem_inc(slot_free, 2)
                dve.sem_inc(pt_lo, 2)
                dve.sem_inc(out_lo, 2)
                dve.memset(acc[:, :, :], 0.0).then_inc(acc_zero, 1)
                dve.wait_ge(acc_zero, 1)

                def low_part(g, n, count, hi, lo, scale):
                    dve.wait_ge(hi_done, count)
                    dve.scalar_tensor_tensor(lo, slot_of(n)[:, :], scale, hi.bitcast(F32), ALU.mult,
                                             ALU.subtract).then_inc(slot_free, 1)

                def minimum(g, n, u, b):
                    i, w = u % NB, width(u, b)
                    dve.wait_ge(slot_full, full(g, n))
                    dve.sem_inc(own_dve, 1)
                    dve.tensor_tensor_reduce(block_of(u, b), slot_of(n)[:, 0:w], mask[:, T - w:T], 1.0, 3e38,
                                             ALU.add, ALU.min, low[:, i, b:b + 1]).then_inc(slot_free, 1)

                def item(g, place, it, his):
                    n = place[it]
                    if it[0] == "S":
                        minimum(g, n, it[1], it[2])
                    elif it[0] == "K":
                        low_part(g, n, his + 1, kh[:, :], kl[:, :], 1.0)
                    elif it[0] == "VT":
                        dve.wait_ge(slot_full, full(g, n))
                        dve.tensor_copy(vt[:, it[1] * HALF:(it[1] + 1) * HALF], slot_of(n)[:, 0:HALF]).then_inc(slot_free, 1)
                    elif it[0] == "V":
                        low_part(g, n, his + 1, vh[:, :, :].rearrange("p b n -> p (b n)"),
                                 vl[:, :, :].rearrange("p b n -> p (b n)"), 1.0)
                    elif it[0] == "Q":
                        low_part(g, n, his + 1, qh[:, it[1] % 2, :], ql[:, it[1] % 2, :], -DH1 ** -0.5)
                    else:
                        dve.wait_ge(slot_full, full(g, n))
                        c = it[1] % 4
                        part = acc[:, 2 * c:2 * c + 2, :].rearrange("p b n -> p (b n)")
                        dve.tensor_tensor(part, part, slot_of(n)[:, :], ALU.add).then_inc(slot_free, 1)

                def invert(g, u):
                    i = u % NB
                    dve.wait_ge(exp_done, g * (4 * UNITS) + 4 * (u + 1))
                    dve.reciprocal(rinv[:, i, :], sums[:, i, :]).then_inc(inv_done, 1)
                    if one:
                        dve.wait_ge(inv_done, g * UNITS + (u + 1))
                        for b in range(4):
                            dve.tensor_scalar(block_of(u, b), block_of(u, b), rinv[:, i, b:b + 1], None,
                                              ALU.mult).then_inc(norm_done, 1)

                def turn(g, place, has_next):
                    his = 0
                    for u in range(UNITS):
                        for kb, its in enumerate(steps(u, has_next)):
                            if kb == NORM_AT[u % 2] and (u + NORM_AHEAD < UNITS or has_next):
                                invert(g, u + NORM_AHEAD)
                            for it in its:
                                item(g, place, it, g * HIS + (HI0 + his))
                                his += it[0] in ("K", "Q", "V")
                            n, c = first_tile[u] + kb, tile_col(u, kb)
                            dve.wait_ge(pt_hi, g * TURN + (n + 1))
                            dve.tensor_tensor(pt_l[:, n % 4, c:HALF], tbank[n % 2][:, c:HALF],
                                              pt_h[:, n % 4, c:HALF].bitcast(F32), ALU.subtract).then_inc(pt_lo, 1)
                        if NORM_AT[u % 2] == KBS[u % 2] and (u + NORM_AHEAD < UNITS or has_next):
                            invert(g, u + NORM_AHEAD)
                        e = out_index(u)
                        if e is not None:
                            dve.wait_ge(out_hi, g * OUTS + (e + 1))
                            j = u // 2 % AJ
                            dve.tensor_tensor(out_view(at_l, j, u), bank_out(u), out_view(at_h, j, u).bitcast(F32),
                                              ALU.subtract).then_inc(out_lo, 1)
                    for it in tail(has_next):
                        item(g, place, it, g * HIS + (HI0 + his))

                his = 0
                for it in start:
                    item(0, place_start, it, his)
                    his += it[0] in ("K", "Q", "V")
                for u in range(NORM_AHEAD):
                    invert(0, u)
                turns(dve, turn)

            @block.tensor
            def _(pe):
                pe.sem_inc(pv_done, 4)
                pe.sem_inc(slot_full, N)

                def project(out, hi, lo):
                    for h in range(2):
                        cols = slice(h * HALF, (h + 1) * HALF)
                        pairs = [pr for k in range(KT) for pr in three(hi(k), lo(k), xh[:, k, cols], xl[:, k, cols])]
                        mm = products(pe, out[:, cols], pairs)
                    return mm

                def item(g, place, it):
                    n = place[it]
                    out = slot_of(n)
                    pe.wait_ge(slot_free, vacant(g, n))
                    if it[0] == "K":
                        pe.wait_ge(kv_split, g + (2 + (it[1] > 0)))
                        mm = project(out, lambda k: wkvh[:, k, 0:P], lambda k: wkvl[:, k, 0:P])
                    elif it[0] == "VT":
                        cols = slice(it[1] * HALF, (it[1] + 1) * HALF)
                        mm = products(pe, out[:, 0:HALF], [pr for k in range(KT) for pr in three(
                            wkvh[:, k, P:2 * P], wkvl[:, k, P:2 * P], xh[:, k, cols], xl[:, k, cols])])
                    elif it[0] == "V":
                        pe.wait_ge(slot_free, read(g, place[("VT", 1)]))
                        for b in range(TB):
                            mm = pe.transpose(out[:, b * P:(b + 1) * P], vt[:, b * P:(b + 1) * P], ident[:, :])
                    elif it[0] == "Q":
                        j = it[1]
                        pe.wait_ge(q_split, g * GH + (j + 1 + 2))
                        mm = project(out, lambda k: wqh[:, j % 2, k, :], lambda k: wql[:, j % 2, k, :])
                    elif it[0] == "S":
                        u, b = it[1], it[2]
                        j, w = u // 2, width(u, b)
                        gs = g + (1 if u >= UNITS else 0)
                        if one and u % 2 == 0 and b == 3:
                            if ("Q", j) in place:
                                pe.wait_ge(slot_free, read(g, max(place[("Q", j)], place.get(("K", j), -N0))))
                            else:
                                pe.wait_ge(slot_free, read_before(g, ("Q", j + GH), ("Q", j)))
                        if not one and u % 2 == 0 and b == 3:
                            pe.wait_ge(q_loaded[j % GH], g * 64 + (64 if j < GH else 128))
                        if not one:
                            pe.sem_inc(own_pe, 1)
                        qc = slice(w - P, w)
                        for c0 in range(0, w, HALF):
                            c1 = min(c0 + HALF, w)
                            if one:
                                pairs = three(qh[:, j % 2, qc], ql[:, j % 2, qc], kh[:, c0:c1], kl[:, c0:c1])
                            else:
                                pairs = [(q_stack[:, j % GH, qc], k_stack[:, bass.ds(gs, 1), c0:c1]
                                          .rearrange("p g t -> p (g t)"))]
                            mm = products(pe, out[:, c0:c1], pairs)
                    else:
                        half, c = it[1] // 4, it[1] % 4
                        if c == 0 and one:
                            pe.wait_ge(wo_split, g * GH + (2 * half + 2 + 2))
                            pe.wait_ge(out_lo, g * OUTS + (4 * half + 4 + 2))
                        elif c == 0:
                            pe.wait_ge(wo_split, g + 2)
                            pe.wait_ge(out_lo, g * OUTS + (OUTS + 2))
                        for b in (2 * c, 2 * c + 1):
                            toks = slice(b * P, (b + 1) * P)
                            pairs = [pr for j in range(AJ) for pr in three(at_h[:, j, toks], at_l[:, j, toks],
                                                                           wo_h[:, j, :], wo_l[:, j, :])]
                            mm = products(pe, out[:, (b % 2) * HALF:(b % 2 + 1) * HALF], pairs)
                    mm.then_inc(slot_full, 1)

                def times_v(g, u, kb):
                    n, j, s, c = first_tile[u] + kb, u // 2, u % 2, tile_col(u, kb)
                    pe.wait_ge(pt_lo, g * TURN + (n + 1 + 2))
                    if kb == 0 and one:
                        pe.wait_ge(out_lo, g * OUTS + (u + 1))
                    if kb == 0 and not one:
                        pe.wait_ge(kv_split, g * 8 + (2 * (j + 1) + 1))
                        if j == 0:
                            pe.wait_ge(out_lo, g * OUTS + (s + 1))
                    ph, pl = pt_h[:, n % 4, c:HALF], pt_l[:, n % 4, c:HALF]
                    if one:
                        pairs = three(vh[:, kb, :], vl[:, kb, :], ph, pl)
                    else:
                        pairs = [(v_pad[:, kb, j, :], ph), (v_pad[:, kb, j, :], pl)]
                    first = kb == 0 and (one or j == 0)
                    final = kb == KBS[s] - 1 and (one or j == GH - 1)
                    products(pe, obank[s][:, c:HALF], pairs, first, final).then_inc(pv_done, 1)

                def turn(g, place, has_next):
                    for u in range(UNITS):
                        kbs = KBS[u % 2]
                        its = steps(u, has_next)
                        for kb in range(kbs + LAG):
                            if kb < kbs:
                                for it in its[kb]:
                                    item(g, place, it)
                                n, c = first_tile[u] + kb, tile_col(u, kb)
                                if kb == 0:
                                    pe.wait_ge(norm_done, g * (4 * UNITS) + 4 * (u + 1))
                                pe.wait_ge(pt_lo, g * TURN + (n + 1))
                                for b in range(c // P, 4):
                                    t = pe.transpose(tbank[n % 2][:, b * P:(b + 1) * P],
                                                     block_of(u, b)[:, kb * P:(kb + 1) * P], ident[:, :])
                                t.then_inc(turned, 1)
                            if kb >= LAG:
                                times_v(g, u, kb - LAG)
                    for it in tail(has_next):
                        item(g, place, it)

                if not one:
                    pe.wait_ge(kv_loaded, 64)
                else:
                    pe.wait_ge(kv_split, 2)
                for it in start:
                    item(0, place_start, it)
                turns(pe, turn)


def swiglu(core, consts, acc, xh, xl, io):
    nc = core.nc
    with core.stage("f0") as sb:
        w_gu = sb("w_gu", [P, KT, 2 * INTER])
        w_dn = sb("w_dn", [P, FT, D])
        shift = sb("shift", [P, 1], U32)
        loads = core.sem("f0_loads")
        idx_done = core.sem("f0_idx")
        gathered = core.sem("f0_gathered")
        raw_loaded = [core.sem(f"f0_raw{i}") for i in range(2)]
        raw_free = core.sem("f0_raw_free")
        nib, zeros_ready, diff, ready = (core.sem(f"f0_{n}") for n in ("nib", "zeros", "diff", "ready"))

        with ExitStack() as ctx2:
            sb2 = lambda n, shape, dt=F32: ctx2.enter_context(nc.sbuf_tensor(f"f0_{n}", shape, dt))
            idx = sb2("idx", [P, KT + FT], I32)
            wrap = sb2("wrap", [P, KT + FT], I32)
            z_gu = sb2("z_gu", [P, KT, 2 * INTER // NIBBLES], U32)
            z_dn = sb2("z_dn", [P, FT, D // NIBBLES], U32)
            WIDE = 2 * INTER
            raw = sb2("raw", [P, 2, WIDE], U32)
            wi = sb2("wi", [P, WIDE], U32)
            zi = sb2("zi", [P, WIDE], U32)
            parts = [(P, io["qgu"], 16 * k, WIDE, k, z_gu[:, k, :], w_gu[:, k, :], 1) for k in range(KT)]
            parts += [(P, io["qdn"], 16 * k, D * 5, KT + k, z_dn[:, k:k + 5, :], w_dn[:, k:k + 5, :], 5) for k in (0, 5)]
            parts += [(F_LAST, io["qdn"], 160, D, KT + 10, z_dn[:, 10, :], w_dn[:, 10, :], 1)]
            with nc.Block() as block:

                @block.sync
                def _(sp):
                    sp.dma_start(idx[:, 0:KT], io["ggu"].rearrange("(k p) -> p k", p=P), allow_slow_non_contiguous=True).then_inc(loads, 16)
                    sp.dma_start(idx[:, KT:KT + FT - 1], io["gdn"][0:(FT - 1) * P].rearrange("(k p) -> p k", p=P), allow_slow_non_contiguous=True).then_inc(loads, 16)
                    sp.dma_start(idx[0:F_LAST, KT + FT - 1:KT + FT], io["gdn"][(FT - 1) * P:INTER].rearrange("(p a) -> p a", a=1), allow_slow_non_contiguous=True).then_inc(loads, 16)
                    sp.dma_start(shift[:, :], io["shift"]).then_inc(loads, 16)
                    for n, (rows, src, r0, width, _, _, _, tiles) in enumerate(parts):
                        if n >= 2:
                            sp.wait_ge(raw_free, n - 1)
                        for s in range(NIBBLES):
                            if tiles == 1:
                                out = raw[s:rows:NIBBLES, n % 2, 0:width]
                                sp.dma_start(out, src[r0:r0 + rows // NIBBLES, :]).then_inc(raw_loaded[n % 2], 16)
                            else:
                                out = raw[s:rows:NIBBLES, n % 2, 0:width].rearrange("r (k n) -> r k n", n=D)
                                sp.dma_start(out, src[r0:r0 + tiles * 16, :].rearrange("(k r) n -> r k n", r=16)).then_inc(raw_loaded[n % 2], 16)

                @block.gpsimd
                def _(pool):
                    pool.wait_ge(idx_done, 7)
                    for k in range(KT + FT):
                        rows = F_LAST if k == KT + FT - 1 else P
                        at = bass.IndirectOffsetOnAxis(ap=idx[0:rows, k:k + 1].bitcast(U32), axis=0)
                        if k < KT:
                            pairs = ((z_gu[:, k, :], io["zgu"]), (w_gu[:, k, :], io["sgu"]))
                        else:
                            pairs = ((z_dn[0:rows, k - KT, :], io["zdn"]), (w_dn[0:rows, k - KT, :], io["sdn"]))
                        for out, src in pairs:
                            pool.indirect_dma_start(out=out, out_offset=None, in_=src[:, :], in_offset=at).then_inc(gathered, 16)
                    pool.wait_ge(gathered, 32 * (KT + FT))

                @block.vector
                def _(dve):
                    dve.wait_ge(loads, 64)
                    dve.memset(wrap[:, :], 0.0).then_inc(idx_done, 1)
                    dve.wait_ge(idx_done, 1)
                    views = ((slice(0, KT), P, GU_GROUPS), (slice(KT, KT + FT - 1), P, DN_GROUPS),
                             (slice(KT + FT - 1, KT + FT), F_LAST, DN_GROUPS))
                    for c, rows, groups in views:
                        dve.tensor_scalar(wrap[0:rows, c], idx[0:rows, c], 0, groups, ALU.is_lt, ALU.mult).then_inc(idx_done, 1)
                    dve.wait_ge(idx_done, 4)
                    for c, rows, groups in views:
                        dve.tensor_tensor(wrap[0:rows, c], idx[0:rows, c], wrap[0:rows, c], ALU.add).then_inc(nib, 1)
                    dve.wait_ge(nib, 3)
                    for c, rows, groups in views:
                        dve.tensor_scalar(idx[0:rows, c], wrap[0:rows, c], 0, groups - 1, ALU.max, ALU.min).then_inc(idx_done, 1)
                    dve.wait_ge(gathered, 32 * (KT + FT))
                    for n, (rows, _, _, width, _, z, w, tiles) in enumerate(parts):
                        z, w = z[0:rows], w[0:rows]
                        if n:
                            dve.wait_ge(ready, n)
                        zo = zi[0:rows, 0:width]
                        if tiles > 1:
                            zo = zo.rearrange("p (k c s) -> p k c s", k=tiles, s=NIBBLES)
                            w = w.rearrange("p k n -> p (k n)")
                        else:
                            zo = zo.rearrange("p (c s) -> p c s", s=NIBBLES)
                        for s in range(NIBBLES):
                            o = zo[:, :, :, s] if tiles > 1 else zo[:, :, s]
                            dve.tensor_scalar(o, z, 4 * s, 15, ALU.logical_shift_right, ALU.bitwise_and).then_inc(zeros_ready, 1)
                        dve.wait_ge(raw_loaded[n % 2], 16 * NIBBLES * (n // 2 + 1))
                        dve.tensor_scalar(wi[0:rows, 0:width], raw[0:rows, n % 2, 0:width], shift[0:rows, 0:1], 15,
                                          ALU.logical_shift_right, ALU.bitwise_and).then_inc(raw_free, 1)
                        dve.wait_ge(raw_free, n + 1)
                        dve.wait_ge(zeros_ready, NIBBLES * (n + 1))
                        d = raw[0:rows, n % 2, 0:width].bitcast(F32) if False else wf_view(zi, rows, width)
                        dve.scalar_tensor_tensor(d, wi[0:rows, 0:width], -1.0, zi[0:rows, 0:width], ALU.add,
                                                 ALU.subtract).then_inc(diff, 1)
                        dve.wait_ge(diff, n + 1)
                        dve.tensor_tensor(w, w, d, ALU.mult).then_inc(ready, 1)
                    dve.wait_ge(ready, len(parts))

        silu_sets(core, acc, xh, xl, w_gu, w_dn)


def wf_view(zi, rows, width):
    return zi[0:rows, 0:width].bitcast(F32)


def silu_sets(core, acc, xh, xl, w_gu, w_dn):
    nc = core.nc
    with core.stage("f1") as sb:
        wh, wl = sb("wh", [P, KT, 2, P], F32R), sb("wl", [P, KT, 2, P], F32R)
        dh, dl = sb("dh", [P, D], F32R), sb("dl", [P, D], F32R)
        gate = sb("gate", [P, 2, HALF])
        hid = sb("hid", [P, 2, HALF])
        hh, hl = sb("hh", [P, T], F32R), sb("hl", [P, T], F32R)
        S = {n: core.sem(f"f1_{n}") for n in
             ("acc_zero", "wh", "wl", "dh", "dl", "gu", "gate", "hid", "hh", "hl", "dn", "added", "own_pool")}
        gu_bank = [core.slots[0], core.slots[1]]

        def turns(eng, body, lag_last=None):
            with eng.Fori(0, FT - 1) as f:
                body(f, f * P, P)
            body(FT - 1, (FT - 1) * P, F_LAST)

        with nc.Block() as block:

            @block.gpsimd
            def _(pool):
                pool.memset(acc[:, :, :], 0.0).then_inc(S["acc_zero"], 1)

                def body(f, c0, F):
                    pool.wait_ge(S["gu"], f * 2 + 2)
                    pool.sem_inc(S["own_pool"], 1)
                    for s in range(2):
                        cols = bass.ds(c0 + s * INTER, F)
                        pool.tensor_copy(wh[:, :, s, 0:F], w_gu[:, :, cols]).then_inc(S["wh"], 1)
                    for s in range(2):
                        cols = bass.ds(c0 + s * INTER, F)
                        pool.wait_ge(S["wh"], f * 2 + s + 1)
                        pool.sem_inc(S["own_pool"], 1)
                        pool.tensor_tensor(wl[:, :, s, 0:F], w_gu[:, :, cols], wh[:, :, s, 0:F].bitcast(F32),
                                           ALU.subtract).then_inc(S["wl"], 1)
                    row = (w_dn[0:F, bass.ds(f, 1), :]).rearrange("p a n -> p (a n)")
                    pool.wait_ge(S["dn"], f * 8 + 8)
                    pool.sem_inc(S["own_pool"], 1)
                    pool.tensor_copy(dh[0:F, :], row).then_inc(S["dh"], 1)
                    pool.wait_ge(S["dh"], f + 1)
                    pool.sem_inc(S["own_pool"], 1)
                    pool.tensor_tensor(dl[0:F, :], row, dh[0:F, :].bitcast(F32), ALU.subtract).then_inc(S["dl"], 1)

                turns(pool, body)

            @block.scalar
            def _(act):
                def body(f, c0, F):
                    for h in range(2):
                        act.wait_ge(S["gu"], f * 2 + h + 1 + 2)
                        act.activation(gate[0:F, h, :], gu_bank[h][0:F, 0:HALF], ACT.Silu).then_inc(S["gate"], 1)
                        act.wait_ge(S["hid"], f * 2 + h + 1)
                        act.wait_ge(S["dn"], f * 8 + 4 * h + 4)
                        act.activation(hh[0:F, h * HALF:(h + 1) * HALF], hid[0:F, h, :], ACT.Copy).then_inc(S["hh"], 1)

                turns(act, body)

            @block.vector
            def _(dve):
                dve.wait_ge(S["acc_zero"], 1)

                def add(f, half):
                    for b in range(4 * half, 4 * half + 4):
                        dve.wait_ge(S["dn"], f * 8 + b + 1 + 8)
                        dve.wait_ge(S["hl"], f * 2 + half + 1)
                        dve.tensor_tensor(acc[:, b, :], acc[:, b, :], core.banks[b % 4][:, :], ALU.add).then_inc(S["added"], 1)

                def hidden(f, h, F):
                    cols = slice(h * HALF, (h + 1) * HALF)
                    dve.wait_ge(S["gate"], f * 2 + h + 1)
                    dve.tensor_tensor(hid[0:F, h, :], gate[0:F, h, :], gu_bank[h][0:F, HALF:2 * HALF],
                                      ALU.mult).then_inc(S["hid"], 1)
                    dve.wait_ge(S["hh"], f * 2 + h + 1)
                    dve.tensor_tensor(hl[0:F, cols], hid[0:F, h, :], hh[0:F, cols].bitcast(F32),
                                      ALU.subtract).then_inc(S["hl"], 1)

                def body(f, c0, F):
                    hidden(f, 0, F)
                    hidden(f, 1, F)
                    add(f, 0)
                    add(f, 1)

                turns(dve, body)

            @block.tensor
            def _(pe):
                pe.sem_inc(S["gu"], 2)
                pe.sem_inc(S["dn"], 8)

                def body(f, c0, F):
                    for h in range(2):
                        if h == 0:
                            pe.wait_ge(S["wl"], f * 2 + 2)
                        cols = slice(h * HALF, (h + 1) * HALF)
                        for s in range(2):
                            pairs = [pr for k in range(KT) for pr in three(wh[:, k, s, 0:F], wl[:, k, s, 0:F],
                                                                           xh[:, k, cols], xl[:, k, cols])]
                            mm = products(pe, gu_bank[h][0:F, s * HALF:(s + 1) * HALF], pairs)
                        mm.then_inc(S["gu"], 1)
                    pe.wait_ge(S["dl"], f + 1)
                    for b in range(TB):
                        if b % 4 == 0:
                            pe.wait_ge(S["hl"], f * 2 + b // 4 + 1)
                        toks = slice(b * P, (b + 1) * P)
                        if b >= 4:
                            pe.wait_ge(S["added"], f * 8 + b - 3)
                        mm = products(pe, core.banks[b % 4][:, :], three(hh[0:F, toks], hl[0:F, toks], dh[0:F, :], dl[0:F, :]))
                        mm.then_inc(S["dn"], 1)

                turns(pe, body)


def lora_mixture(core, consts, acc, xh, xl, io):
    nc = core.nc
    ident, mask, eps, ones = consts
    ER = EXPERTS * RANK
    with core.stage("m") as sb:
        wb = sb("wb", [P, KT, D])
        la = sb("la", [ER, D])
        wr = sb("wr", [EXPERTS, D])
        lb = sb("lb", [P, KT, EXPERTS, RANK])
        bias = sb("bias", [1, D])
        NW = D + ER + EXPERTS
        wth, wtl = sb("wth", [P, KT, NW], F32R), sb("wtl", [P, KT, NW], F32R)
        bth, btl = sb("bth", [ER, D], F32R), sb("btl", [ER, D], F32R)
        prob = sb("prob", [P, TB, EXPERTS])
        top = sb("top", [P, TB])
        tot = sb("tot", [P, TB])
        gt = sb("gt", [P, TB, EXPERTS, EXPERTS])
        eq = sb("eq", [P, TB, EXPERTS, EXPERTS])
        before = sb("before", [P, EXPERTS, EXPERTS])
        rank_of = sb("rank_of", [P, TB, EXPERTS])
        gated = sb("gated", [P, TB, EXPERTS])
        h = sb("h", [P, TB, EXPERTS, RANK])
        hth, htl = sb("hth", [ER, T], F32R), sb("htl", [ER, T], F32R)
        loaded = core.sem("m_loaded")
        turned, hi, lo = core.sem("m_turned"), core.sem("m_hi"), core.sem("m_lo")
        route, r = core.sem("m_route"), core.sem("m_r")
        expd, weighted = core.sem("m_expd"), core.sem("m_weighted")
        ht, hth_ready, htl_ready = core.sem("m_ht"), core.sem("m_hth"), core.sem("m_htl")
        outs, copied = core.sem("m_outs"), core.sem("m_copied")
        with nc.Block() as block:

            @block.sync
            def _(sp):
                sp.dma_start(wb[:, :, :], io["wb"].rearrange("(k p) d -> p k d", p=P)).then_inc(loaded, 16)
                sp.dma_start(la[:, :], io["la"].rearrange("e r d -> (e r) d")).then_inc(loaded, 16)
                sp.dma_start(wr[:, :], io["wr"]).then_inc(loaded, 16)
                sp.dma_start(bias[:, :], io["bb"].rearrange("(a n) -> a n", a=1)).then_inc(loaded, 16)
                for k in range(KT):
                    sp.dma_start(lb[:, k, :, :], io["lb"][:, k * P:(k + 1) * P, :].rearrange("e p r -> p e r")).then_inc(loaded, 16)
                sp.dma_start(before[:, :, :], io["before"]).then_inc(loaded, 16)

            pieces = [(k, slice(0, D), wth[:, k, 0:D], wtl[:, k, 0:D]) for k in range(KT)]
            pieces += [(KT, slice(0, HALF), wth[:, :, D:D + ER], wtl[:, :, D:D + ER])]
            pieces += [(KT + 1, slice(0, KT * EXPERTS), wth[:, :, D + ER:NW], wtl[:, :, D + ER:NW])]
            pieces += [(KT + 2, slice(0, D), bth[:, :], btl[:, :])]

            def bank_view(n, cols):
                v = core.banks[n % 4][:, cols]
                if n == KT:
                    return v.rearrange("p (k c) -> p k c", k=KT)
                if n == KT + 1:
                    return v.rearrange("p (k c) -> p k c", k=KT)
                return v

            @block.scalar
            def _(act):
                for n, cols, h_, l_ in pieces:
                    act.wait_ge(turned, n + 1)
                    act.activation(h_, bank_view(n, cols), ACT.Copy).then_inc(hi, 1)
                act.wait_ge(r, 2)
                act.activation(prob[:, :, :], prob[:, :, :], ACT.Exp).then_inc(expd, 1)
                for n in range(2):
                    act.wait_ge(ht, n + 1)
                    act.activation(hth[:, n * HALF:(n + 1) * HALF], core.banks[n][:, :], ACT.Copy).then_inc(hth_ready, 1)
                for b in range(TB):
                    act.wait_ge(outs, b + 1)
                    if b % 2:
                        act.activation(acc[:, b, :], core.banks[b % 4][:, :], ACT.Copy).then_inc(copied, 1)
                    else:
                        act.activation(acc[:, b, :], core.banks[b % 4][:, :], ACT.Copy).then_inc(copied, 1)

            @block.vector
            def _(dve):
                for n, cols, h_, l_ in pieces:
                    dve.wait_ge(hi, n + 1)
                    dve.tensor_tensor(l_, bank_view(n, cols), h_.bitcast(F32), ALU.subtract).then_inc(lo, 1)
                steps = [0]

                def step(ins):
                    steps[0] += 1
                    ins.then_inc(r, 1)
                    dve.wait_ge(r, steps[0])

                wide = lambda t: t[:, :, :].unsqueeze(3).to_broadcast([P, TB, EXPERTS, EXPERTS])
                across = lambda t: t[:, :, :].unsqueeze(2).to_broadcast([P, TB, EXPERTS, EXPERTS])
                dve.wait_ge(route, 1)
                step(dve.tensor_reduce(top[:, :], core.slots[1][:, 0:TB * EXPERTS].rearrange("p (b e) -> p b e", b=TB), AX.X, ALU.max))
                step(dve.tensor_tensor(prob[:, :, :], core.slots[1][:, 0:TB * EXPERTS].rearrange("p (b e) -> p b e", b=TB),
                                       top[:, :].unsqueeze(2).to_broadcast([P, TB, EXPERTS]), ALU.subtract))
                dve.wait_ge(expd, 1)
                step(dve.tensor_reduce(tot[:, :], prob[:, :, :], AX.X, ALU.add))
                step(dve.reciprocal(tot[:, :], tot[:, :]))
                step(dve.tensor_tensor(prob[:, :, :], prob[:, :, :], tot[:, :].unsqueeze(2).to_broadcast([P, TB, EXPERTS]), ALU.mult))
                step(dve.tensor_tensor(gt[:, :, :, :], across(prob), wide(prob), ALU.is_gt))
                step(dve.tensor_tensor(eq[:, :, :, :], across(prob), wide(prob), ALU.is_equal))
                step(dve.tensor_tensor(eq[:, :, :, :], eq[:, :, :, :],
                                       before[:, :, :].unsqueeze(1).to_broadcast([P, TB, EXPERTS, EXPERTS]), ALU.mult))
                step(dve.tensor_tensor(gt[:, :, :, :], gt[:, :, :, :], eq[:, :, :, :], ALU.add))
                step(dve.tensor_reduce(rank_of[:, :, :], gt[:, :, :, :], AX.X, ALU.add))
                step(dve.scalar_tensor_tensor(gated[:, :, :], rank_of[:, :, :], 2.0, prob[:, :, :], ALU.is_lt, ALU.mult))
                step(dve.tensor_reduce(tot[:, :], gated[:, :, :], AX.X, ALU.add))
                step(dve.reciprocal(tot[:, :], tot[:, :]))
                step(dve.scalar_tensor_tensor(gated[:, :, :], gated[:, :, :], LORA_SCALE,
                                              tot[:, :].unsqueeze(2).to_broadcast([P, TB, EXPERTS]), ALU.mult, ALU.mult))
                dve.tensor_tensor(h[:, :, :, :], core.slots[0][:, :].rearrange("p (b e r) -> p b e r", b=TB, r=RANK),
                                  gated[:, :, :].unsqueeze(3).to_broadcast([P, TB, EXPERTS, RANK]), ALU.mult).then_inc(weighted, 1)
                for n in range(2):
                    dve.wait_ge(hth_ready, n + 1)
                    cols = slice(n * HALF, (n + 1) * HALF)
                    dve.tensor_tensor(htl[:, cols], core.banks[n][:, :], hth[:, cols].bitcast(F32), ALU.subtract).then_inc(htl_ready, 1)

            @block.tensor
            def _(pe):
                pe.wait_ge(loaded, 16 * (5 + KT))
                for n in range(KT + 3):
                    if n >= 4:
                        pe.wait_ge(lo, n - 3)
                    bank = core.banks[n % 4]
                    for k in range(KT):
                        if n < KT:
                            t = pe.transpose(bank[:, k * P:(k + 1) * P], wb[:, k, n * P:(n + 1) * P], ident[:, :])
                        elif n == KT:
                            t = pe.transpose(bank[:, k * P:(k + 1) * P], la[:, k * P:(k + 1) * P], ident[:, :])
                        elif n == KT + 1:
                            t = pe.transpose(bank[:, k * EXPERTS:(k + 1) * EXPERTS], wr[:, k * P:(k + 1) * P],
                                             ident[0:EXPERTS, 0:EXPERTS])
                        else:
                            t = pe.transpose(bank[:, k * P:(k + 1) * P],
                                             lb[:, k, :, :].rearrange("p e r -> p (e r)"), ident[:, :])
                    t.then_inc(turned, 1)
                pe.wait_ge(lo, KT + 3)
                for b in range(TB):
                    toks = slice(b * P, (b + 1) * P)
                    for out, c0, c1 in ((core.slots[1][:, b * EXPERTS:(b + 1) * EXPERTS], D + ER, NW),
                                        (core.slots[0][:, b * ER:(b + 1) * ER], D, D + ER)):
                        pairs = [pr for k in range(KT) for pr in three(xh[:, k, toks], xl[:, k, toks],
                                                                       wth[:, k, c0:c1], wtl[:, k, c0:c1])]
                        mm = products(pe, out, pairs)
                mm.then_inc(route, 1)
                pe.wait_ge(weighted, 1)
                for n in range(2):
                    for b in range(4):
                        t = pe.transpose(core.banks[n][:, b * P:(b + 1) * P],
                                         h[:, 4 * n + b, :, :].rearrange("p e r -> p (e r)"), ident[:, :])
                    t.then_inc(ht, 1)
                for b in range(TB):
                    toks = slice(b * P, (b + 1) * P)
                    pe.wait_ge(htl_ready, 2)
                    if b >= 4:
                        pe.wait_ge(copied, b - 3)
                    pairs = [pr for k in range(KT) for pr in three(xh[:, k, toks], xl[:, k, toks],
                                                                   wth[:, k, 0:D], wtl[:, k, 0:D])]
                    pairs += three(hth[:, toks], htl[:, toks], bth[:, :], btl[:, :])
                    products(pe, core.banks[b % 4][:, :], pairs, True, False)
                    mm = pe.matmul(core.banks[b % 4][:, :], ones[0:1, :], bias[0:1, :], start=False, stop=True)
                    mm.then_inc(outs, 1)


def program(nc, io, out):
    with ExitStack() as ctx:
        core = Core(nc, ctx)
        sb = lambda n, shape, dt=F32: ctx.enter_context(nc.sbuf_tensor(n, shape, dt))
        ident, mask, eps, ones = sb("ident", [P, P]), sb("mask", [P, T]), sb("eps", [P, 1]), sb("ones", [P, P])
        consts = (ident, mask, eps, ones)
        acc = sb("acc", [P, TB, D])
        x_scr = [nc.dram_tensor(f"x_after_{i}", (T, D), F32).ap() for i in range(3)]
        q_scr = nc.dram_tensor("q_parts", (2, D, T), F32).ap()
        k_scr = nc.dram_tensor("k_parts", (2, P, T), F32).ap()
        constants(core, consts, io["ident"], io["mask"])
        resid = io["L0_attn_resid"].rearrange("b t d -> (b t) d")
        with nc.sbuf_tensor("v0", [P, TB, P], F32R) as v0, nc.sbuf_tensor("v0l", [P, TB, P], F32R) as v0l:
            with nc.sbuf_tensor("xh0", [P, KT, T], F32R) as xh, nc.sbuf_tensor("xl0", [P, KT, T], F32R) as xl:
                seam(core, "s0", consts, acc, xh, xl, resid, None, False, False)
                project_layer0(core, consts, xh, xl, io["L0_attn_Wq"], io["L0_attn_Wk"], io["L0_attn_Wv"],
                               io["cos"], io["sin"], q_scr, k_scr, v0, v0l)
            attention(core, "a0", 0, consts, acc, None, None,
                      {"q": q_scr, "k": k_scr, "v0": v0, "v0l": v0l, "wo": io["L0_attn_Wo"]})
        xh, xl = sb("xh", [P, KT, T], F32R), sb("xl", [P, KT, T], F32R)
        seam(core, "s1", consts, acc, xh, xl, resid, x_scr[0], True, False)
        swiglu(core, consts, acc, xh, xl,
               {"qgu": io["L0_ffn_qweight_gu"], "zgu": io["L0_ffn_qzeros_gu"], "sgu": io["L0_ffn_scales_gu"],
                "ggu": io["L0_ffn_g_idx_gu"], "qdn": io["L0_ffn_qweight_down"], "zdn": io["L0_ffn_qzeros_down"],
                "sdn": io["L0_ffn_scales_down"], "gdn": io["L0_ffn_g_idx_down"], "shift": io["shift"]})
        seam(core, "s2", consts, acc, xh, xl, x_scr[0], x_scr[1], True, False)
        attention(core, "a1", 1, consts, acc, xh, xl,
                  {"wq": io["L1_attn_w_q"], "wk": io["L1_attn_w_k"], "wv": io["L1_attn_w_v"], "wo": io["L1_attn_w_o"]})
        seam(core, "s3", consts, acc, xh, xl, x_scr[1], x_scr[2], True, False)
        lora_mixture(core, consts, acc, xh, xl,
                     {"wb": io["L1_ffn_W_base"], "bb": io["L1_ffn_b_base"], "wr": io["L1_ffn_W_router"],
                      "la": io["L1_ffn_lora_A"], "lb": io["L1_ffn_lora_B"], "before": io["before"]})
        seam(core, "s4", consts, acc, xh, xl, x_scr[2], out.rearrange("b t d -> (b t) d"), True, True)


def shape_constants():
    import math

    import numpy as np

    f32 = np.float32
    i = np.arange(0, DH0, 2, dtype=f32) / f32(DH0)
    freq = (f32(1.0 / (2.0 * math.pi)) * f32(500000.0) ** (-i)).astype(f32)
    factor, lo, hi, context = 32.0, 1.0, 4.0, 1024
    scaled = np.where(freq < f32(lo / context), freq / f32(factor), freq)
    smooth = np.clip((f32(context) * freq - f32(lo)) / f32(hi - lo), f32(0), f32(1))
    mixed = (f32(1) - smooth) * (freq / f32(factor)) + smooth * freq
    mid = (freq >= f32(lo / context)) & (freq <= f32(hi / context))
    freq = np.where(mid, mixed, scaled).astype(f32)
    phase = (f32(2.0 * math.pi) * np.arange(T).astype(f32)[:, None] * freq[None, :]).astype(f32)
    cos, sin = np.cos(phase).T, np.sin(phase).T
    return {
        "cos": np.ascontiguousarray(np.tile(np.concatenate([cos, cos]), (P // DH0, 1)), dtype=f32),
        "sin": np.ascontiguousarray(np.tile(np.concatenate([-sin, sin]), (P // DH0, 1)), dtype=f32),
        "ident": np.eye(P, dtype=f32),
        "mask": np.concatenate([np.zeros((P, T - P), f32), np.triu(np.full((P, P), MASKED, f32), 1)], axis=1),
        "shift": (4 * (np.arange(P) % NIBBLES)).astype(np.uint32)[:, None],
        "before": np.ascontiguousarray(np.broadcast_to(np.tril(np.ones((EXPERTS, EXPERTS), f32), -1), (P, EXPERTS, EXPERTS))),
    }


_INS = ["L0_attn_resid", "L0_attn_Wq", "L0_attn_Wk", "L0_attn_Wv", "L0_attn_Wo", "L0_ffn_qweight_gu",
        "L0_ffn_qzeros_gu", "L0_ffn_scales_gu", "L0_ffn_g_idx_gu", "L0_ffn_qweight_down", "L0_ffn_qzeros_down",
        "L0_ffn_scales_down", "L0_ffn_g_idx_down", "L1_attn_w_q", "L1_attn_w_k", "L1_attn_w_v", "L1_attn_w_o",
        "L1_ffn_W_base", "L1_ffn_b_base", "L1_ffn_W_router", "L1_ffn_lora_A", "L1_ffn_lora_B"]


def kernel(**inputs):
    import numpy as np

    import concourse.bacc as bacc
    from concourse.bass_utils import run_bass_kernel_spmd

    nc = bacc.Bacc("TRN2", target_bir_lowering=False, num_devices=1)
    arrays = {name: np.ascontiguousarray(inputs[name]) for name in _INS}
    arrays.update(shape_constants())
    fed = {f"in_{name}": a for name, a in arrays.items()}
    io = {name: nc.dram_tensor(f"in_{name}", a.shape, mybir.dt.from_np(a.dtype), kind="ExternalInput").ap()
          for name, a in arrays.items()}
    out = nc.dram_tensor("out_x", (1, T, D), F32, kind="ExternalOutput").ap()
    program(nc, io, out)
    got = run_bass_kernel_spmd(nc, [fed], core_ids=[0])
    return got.results[0]["out_x"]
```

```python
from contextlib import ExitStack, contextmanager

import concourse.bass as bass
import concourse.mybir as mybir

F32 = mybir.dt.float32
F32R = mybir.dt.float32r
I32 = mybir.dt.int32
U32 = mybir.dt.uint32
ALU = mybir.AluOpType
ACT = mybir.ActivationFunctionType
AX = mybir.AxisListType

P = 128
T = 1024
D = 512
KT = D // P
TB = T // P
HALF = 512
EPS = 1e-5
MASKED = 1e30

HEADS = 32
KV = 8
GH = HEADS // KV
DH0 = D // HEADS
DH1 = 128

INTER = 1376
NIBBLES = 8
GU_GROUPS = 4
DN_GROUPS = INTER // 128
FT = -(-INTER // P)
F_LAST = INTER - (FT - 1) * P

EXPERTS = 8
RANK = 16
LORA_SCALE = 2.0


class Core:

    def __init__(self, nc, ctx):
        self.nc, self.own = nc, []
        self.banks = [ctx.enter_context(nc.psum_tensor(f"bank{i}", [P, HALF], F32)) for i in range(4)]
        self.slots = [ctx.enter_context(nc.psum_tensor(f"slot{i}", [P, 2 * HALF], F32)) for i in range(2)]

    def sem(self, name):
        handle = self.nc.alloc_semaphore(name=name)
        self.own.append(handle)
        return handle

    @contextmanager
    def stage(self, name):
        before, self.own = self.own, []
        with ExitStack() as ctx:
            yield lambda n, shape, dt=F32: ctx.enter_context(self.nc.sbuf_tensor(f"{name}_{n}", shape, dt))
            self.nc.clear_and_free_semaphores(self.own)
            self.nc.all_engine_barrier()
        self.own = before


def constants(core, tensors, ident_d, mask_d):
    nc = core.nc
    ident, mask, eps, ones = tensors
    loaded = core.sem("const_loaded")
    set_ = core.sem("const_set")
    with nc.Block() as block:

        @block.sync
        def _(sp):
            sp.dma_start(ident[:, :], ident_d).then_inc(loaded, 16)
            sp.dma_start(mask[:, :], mask_d).then_inc(loaded, 16)
            sp.wait_ge(loaded, 32)

        @block.vector
        def _(dve):
            dve.memset(eps[:, :], EPS).then_inc(set_, 1)
            dve.memset(ones[:, :], 1.0).then_inc(set_, 1)
            dve.wait_ge(set_, 2)


def seam(core, name, consts, acc, xh, xl, x_src, x_dst, residual, last, ahead=(), on_pool=None):
    nc = core.nc
    ident, mask, eps, ones = consts
    src = x_src.rearrange("(b p) d -> p b d", p=P)
    dst = x_dst.rearrange("(b p) d -> p b d", p=P) if x_dst is not None else None
    with core.stage(name) as sb:
        x_in = sb("x_in", [P, TB, D]) if residual else acc
        xn = sb("xn", [P, TB, D])
        stats = [sb(f"stats{i}", [P, TB, 6]) for i in range(2)]
        mv = [sb(f"mv{i}", [P, TB, 2]) for i in range(2)]
        std = [sb(f"std{i}", [P, TB]) for i in range(2)]
        rstd = [sb(f"rstd{i}", [P, TB]) for i in range(2)]
        shift = sb("shift", [P, TB])
        x_loaded = [core.sem(f"{name}_x_loaded{h}") for h in range(2)]
        stored = core.sem(f"{name}_stored")
        ahead_loaded = core.sem(f"{name}_ahead_loaded")
        stat = core.sem(f"{name}_stat")
        std_ready = core.sem(f"{name}_std_ready")
        scaled = core.sem(f"{name}_scaled")
        x_new = core.sem(f"{name}_x_new")
        x_new_dve = core.sem(f"{name}_x_new_dve")
        shifted = core.sem(f"{name}_shifted")
        xn_ready = core.sem(f"{name}_xn_ready")
        pool_step = core.sem(f"{name}_pool_step")
        turned = core.sem(f"{name}_turned")
        hi_ready = core.sem(f"{name}_hi_ready")
        lo_ready = core.sem(f"{name}_lo_ready")
        hb = TB // 2
        with nc.Block() as block:

            @block.sync
            def _(sp):
                for h in range(2):
                    sp.dma_start(x_in[:, h * hb:(h + 1) * hb, :], src[:, h * hb:(h + 1) * hb, :]).then_inc(x_loaded[h], 16)
                for to, src_ in ahead:
                    sp.dma_start(to, src_).then_inc(ahead_loaded, 16)
                if dst is not None:
                    for h in range(2):
                        if last and h:
                            sp.wait_ge(x_new_dve, hb)
                        else:
                            sp.wait_ge(x_new, (h + 1) * hb)
                        sp.dma_start(dst[:, h * hb:(h + 1) * hb, :], acc[:, h * hb:(h + 1) * hb, :]).then_inc(stored, 16)
                    sp.wait_ge(stored, 32)
                if ahead:
                    sp.wait_ge(ahead_loaded, 16 * len(ahead))

            @block.gpsimd
            def _(pool):
                for b in range(hb if last else TB) if residual else ():
                    pool.wait_ge(x_loaded[b // hb], 16)
                    pool.wait_ge(scaled, b + 1)
                    pool.tensor_tensor(acc[:, b, :], acc[:, b, :], x_in[:, b, :], ALU.add).then_inc(x_new, 1)
                if on_pool is not None:
                    on_pool(pool, ahead_loaded, pool_step)

            @block.scalar
            def _(act):
                for n in range((2 if residual else 0) + (0 if last else 2)):
                    i, h = (n // 2 if residual else 1), n % 2
                    act.wait_ge(stat, n * (2 * hb + 1) + 2 * hb)
                    act.activation(std[i][:, h * hb:(h + 1) * hb], mv[i][:, h * hb:(h + 1) * hb, 1], ACT.Sqrt,
                                   bias=eps[:, 0:1]).then_inc(std_ready, 1)
                    if i:
                        act.wait_ge(shifted, h + 1)
                        for b in range(h * hb, (h + 1) * hb):
                            act.activation(xn[:, b, :], acc[:, b, :], ACT.Identity, scale=rstd[1][:, b:b + 1],
                                           bias=shift[:, b:b + 1]).then_inc(xn_ready, 1)
                if not last:
                    for n in range(2 * KT):
                        act.wait_ge(turned, n + 1)
                        k, h = n % KT, n // KT
                        act.activation(xh[:, k, h * HALF:(h + 1) * HALF], core.banks[n % 4][:, :],
                                       ACT.Copy).then_inc(hi_ready, 1)

            @block.vector
            def _(dve):
                count = [0]

                def statistics(i, h, ready):
                    blocks = range(h * hb, (h + 1) * hb)
                    for b in blocks:
                        ready(b)
                        dve.bn_stats(stats[i][:, b, :], acc[:, b, :]).then_inc(stat, 1)
                    for n, b in enumerate(blocks):
                        dve.wait_ge(stat, count[0] + n + 1)
                        dve.bn_aggr(mv[i][:, b, :], stats[i][:, b, :]).then_inc(stat, 1)
                    count[0] += 2 * hb

                def root(i, h, n):
                    dve.wait_ge(std_ready, n)
                    dve.reciprocal(rstd[i][:, h * hb:(h + 1) * hb], std[i][:, h * hb:(h + 1) * hb]).then_inc(stat, 1)
                    count[0] += 1
                    dve.wait_ge(stat, count[0])

                done = 0
                if residual:
                    for h in range(2):
                        statistics(0, h, lambda b: None)
                        done += 1
                        root(0, h, done)
                        for b in range(h * hb, (h + 1) * hb):
                            dve.tensor_scalar(acc[:, b, :], acc[:, b, :], mv[0][:, b, 0:1], rstd[0][:, b:b + 1],
                                              ALU.subtract, ALU.mult).then_inc(scaled, 1)
                else:
                    for h in range(2):
                        dve.wait_ge(x_loaded[h], 16)
                if last:
                    dve.wait_ge(x_loaded[1], 16)
                    for b in range(hb, TB):
                        dve.wait_ge(scaled, b + 1)
                        dve.tensor_tensor(acc[:, b, :], acc[:, b, :], x_in[:, b, :], ALU.add).then_inc(x_new_dve, 1)
                    return
                for h in range(2):
                    statistics(1, h, (lambda b: dve.wait_ge(x_new, b + 1)) if residual else (lambda b: None))
                    done += 1
                    root(1, h, done)
                    half = slice(h * hb, (h + 1) * hb)
                    dve.scalar_tensor_tensor(shift[:, half], mv[1][:, half, 0], -1.0, rstd[1][:, half],
                                             ALU.mult, ALU.mult).then_inc(shifted, 1)
                for n in range(2 * KT):
                    dve.wait_ge(hi_ready, n + 1)
                    k, h = n % KT, n // KT
                    cols = slice(h * HALF, (h + 1) * HALF)
                    dve.tensor_tensor(xl[:, k, cols], core.banks[n % 4][:, :], xh[:, k, cols].bitcast(F32),
                                      ALU.subtract).then_inc(lo_ready, 1)

            @block.tensor
            def _(pe):
                if last:
                    return
                for n in range(2 * KT):
                    k, h = n % KT, n // KT
                    if n >= 4:
                        pe.wait_ge(lo_ready, n - 3)
                    for b in range(hb):
                        pe.wait_ge(xn_ready, h * hb + b + 1)
                        t = pe.transpose(core.banks[n % 4][:, b * P:(b + 1) * P], xn[:, h * hb + b, k * P:(k + 1) * P],
                                         ident[:, :])
                    t.then_inc(turned, 1)


def products(pe, out, pairs, start=True, stop=True):
    for n, (w, m) in enumerate(pairs):
        mm = pe.matmul(out, w, m, start=start and n == 0, stop=stop and n == len(pairs) - 1)
    return mm


def three(wh, wl, mh, ml):
    return [(wh, mh), (wh, ml), (wl, mh)]


class Layer0Weights:

    NW = 2 * D + 3 * P
    SW = D + 2 * P

    def __init__(self, raw, cos, sin, io):
        self.raw, self.cos, self.sin = raw, cos, sin
        cols = (("Wq", 0, D), ("Wk", D, D + P), ("Wv", D + P, self.SW))
        self.loads = [(raw[:, :, a:b], io[f"L0_attn_{w}"].rearrange("(k p) n -> p k n", p=P)) for w, a, b in cols]
        self.loads += [(cos[:, :], io["cos"]), (sin[:, :], io["sin"])]

    def swap(self, pool, loaded, step):
        view = lambda a, b: self.raw[:, :, a:b].rearrange("p k (h s i) -> p k h s i", s=2, i=DH0 // 2)
        pool.wait_ge(loaded, 16 * len(self.loads))
        for a, b, o in ((0, D, self.SW), (D, D + P, self.SW + D)):
            for s in range(2):
                pool.tensor_copy(view(o, o + b - a)[:, :, :, s, :], view(a, b)[:, :, :, 1 - s, :]).then_inc(step, 1)
        pool.wait_ge(step, 4)


def project_layer0(core, consts, xh, xl, weights, q_scr, k_scr, v0, v0l):
    nc = core.nc
    ident, mask, eps, ones = consts
    raw, cos, sin, NW, SW = weights.raw, weights.cos, weights.sin, weights.NW, weights.SW
    QK = D // P + 1
    with core.stage("p0") as sb:
        vt = sb("vt", [P, T])
        wh = sb("wh", [P, KT, NW], F32R)
        wl = sb("wl", [P, KT, NW], F32R)
        direct = sb("direct", [P, 2, HALF])
        swapped = sb("swapped", [P, 2, HALF])
        rot = sb("rot", [P, 2, HALF])
        rh = sb("rh", [P, 2, HALF], F32R)
        rl = sb("rl", [P, 2, HALF], F32R)
        w_hi = core.sem("p0_w_hi")
        w_split = core.sem("p0_w_split")
        vt_done, vt_copied = core.sem("p0_vt_done"), core.sem("p0_vt_copied")
        proj = core.sem("p0_proj")
        prod = core.sem("p0_prod")
        rotated = core.sem("p0_rotated")
        rh_ready, rl_ready = core.sem("p0_rh_ready"), core.sem("p0_rl_ready")
        sent = [core.sem(f"p0_sent{i}") for i in range(2)]
        v_proj, v_hi, v_lo = core.sem("p0_v_proj"), core.sem("p0_v_hi"), core.sem("p0_v_lo")
        CH = 2 * QK

        W_PIECES = ((D + P, SW), (0, D + P), (SW, NW))

        with nc.Block() as block:

            @block.sync
            def _(sp):
                for n in range(CH):
                    m, h = n // 2, n % 2
                    sp.wait_ge(rl_ready, n + 1)
                    for part, r in ((0, rh), (1, rl)):
                        out = (q_scr[part, m * P:(m + 1) * P, h * HALF:(h + 1) * HALF] if m < QK - 1
                               else k_scr[part, :, h * HALF:(h + 1) * HALF])
                        sp.dma_start(out, r[:, n % 2, :].bitcast(F32)).then_inc(sent[n % 2], 16)
                for i in range(2):
                    sp.wait_ge(sent[i], 32 * (CH // 2))

            @block.scalar
            def _(act):
                for a, b in W_PIECES:
                    act.activation(wh[:, :, a:b], raw[:, :, a:b], ACT.Copy).then_inc(w_hi, 1)
                for h in range(2):
                    act.wait_ge(vt_done, h + 1)
                    act.activation(vt[:, h * HALF:(h + 1) * HALF], core.banks[2 + h][:, :], ACT.Copy).then_inc(vt_copied, 1)
                for n in range(CH):
                    act.wait_ge(rotated, n + 1)
                    if n >= 2:
                        act.wait_ge(sent[n % 2], 32 * (n // 2))
                    act.activation(rh[:, n % 2, :], rot[:, n % 2, :], ACT.Copy,
                                   scale=(-DH0 ** -0.5 if n // 2 < QK - 1 else 1.0)).then_inc(rh_ready, 1)
                act.wait_ge(v_proj, 1)
                for b in range(2):
                    act.activation(v0[:, 4 * b:4 * b + 4, :], core.banks[b][:, :].rearrange("p (b n) -> p b n", n=P),
                                   ACT.Copy).then_inc(v_hi, 1)

            @block.vector
            def _(dve):
                for n, (a, b) in enumerate(W_PIECES):
                    dve.wait_ge(w_hi, n + 1)
                    dve.tensor_tensor(wl[:, :, a:b], raw[:, :, a:b], wh[:, :, a:b].bitcast(F32),
                                      ALU.subtract).then_inc(w_split, 1)
                for n in range(CH):
                    m, h = n // 2, n % 2
                    cols = slice(h * HALF, (h + 1) * HALF)
                    scale = -DH0 ** -0.5 if m < QK - 1 else 1.0
                    dve.wait_ge(proj, n + 1)
                    dve.tensor_tensor(direct[:, n % 2, :], core.slots[n % 2][:, 0:HALF], cos[:, cols],
                                      ALU.mult).then_inc(prod, 1)
                    dve.tensor_tensor(swapped[:, n % 2, :], core.slots[n % 2][:, HALF:2 * HALF], sin[:, cols],
                                      ALU.mult).then_inc(prod, 1)
                    dve.wait_ge(prod, 2 * n + 2)
                    dve.tensor_tensor(rot[:, n % 2, :], direct[:, n % 2, :], swapped[:, n % 2, :],
                                      ALU.add).then_inc(rotated, 1)
                    dve.wait_ge(rh_ready, n + 1)
                    dve.scalar_tensor_tensor(rl[:, n % 2, :], rot[:, n % 2, :], scale, rh[:, n % 2, :].bitcast(F32),
                                             ALU.mult, ALU.subtract).then_inc(rl_ready, 1)
                for b in range(2):
                    dve.wait_ge(v_hi, b + 1)
                    dve.tensor_tensor(v0l[:, 4 * b:4 * b + 4, :], core.banks[b][:, :].rearrange("p (b n) -> p b n", n=P),
                                      v0[:, 4 * b:4 * b + 4, :].bitcast(F32), ALU.subtract).then_inc(v_lo, 1)

            @block.tensor
            def _(pe):
                pe.wait_ge(w_split, 1)
                for h in range(2):
                    cols, vc = slice(h * HALF, (h + 1) * HALF), slice(D + P, SW)
                    products(pe, core.banks[2 + h][:, :], [pr for k in range(KT) for pr in three(
                        wh[:, k, vc], wl[:, k, vc], xh[:, k, cols], xl[:, k, cols])]).then_inc(vt_done, 1)
                pe.wait_ge(vt_copied, 2)
                for b in range(TB):
                    mm = pe.transpose(core.banks[b // 4][:, (b % 4) * P:(b % 4 + 1) * P], vt[:, b * P:(b + 1) * P], ident[:, :])
                mm.then_inc(v_proj, 1)
                pe.wait_ge(w_split, 3)
                for n in range(CH):
                    m, h = n // 2, n % 2
                    cols = slice(h * HALF, (h + 1) * HALF)
                    if n >= 2:
                        pe.wait_ge(prod, 2 * (n - 1))
                    for s, base in ((0, 0), (1, SW)):
                        wc = slice(base + m * P, base + (m + 1) * P)
                        pairs = [pr for k in range(KT)
                                 for pr in three(wh[:, k, wc], wl[:, k, wc], xh[:, k, cols], xl[:, k, cols])]
                        mm = products(pe, core.slots[n % 2][:, s * HALF:(s + 1) * HALF], pairs)
                    mm.then_inc(proj, 1)


def attention(core, name, layer, consts, acc, xh, xl, io):
    nc = core.nc
    ident, mask, eps, ones = consts
    one = layer == 1
    UNITS = 2 * GH
    AHEAD = 2
    NB = 2 * AHEAD
    BLOCKS = ((0, 1, 6, 7), (2, 3, 4, 5))
    KBS = (8, 6)
    TURN = GH * sum(KBS)
    LAG = 2
    first_tile = [sum(KBS[v % 2] for v in range(u)) for u in range(UNITS + 3)]
    S_AT = ((1, 3, 5, 6), (0, 1, 3, 4)) if one else ((0, 2, 4, 6), (0, 1, 3, 4))
    INVERT_AT = (0, 0) if one else (2, 1)
    NORM_AHEAD = 1
    LONG = ("K", "Q", "W", "VT")

    def steps(u, has_next):
        v = u + AHEAD
        out = [[] for _ in range(KBS[u % 2])]
        if v < UNITS or has_next:
            for b, t in zip((3, 2, 1, 0), S_AT[u % 2]):
                out[t].append(("S", v, b))
        j = (u + 3) // 2
        if one and u % 2 and (j < GH or has_next):
            out[2].append(("Q", j))
        if one and u == UNITS - 3 and has_next:
            out[5].append(("K", GH))
        if one and u == UNITS - 2 and has_next:
            out[2].append(("VT", 0))
            out[4].append(("VT", 1))
        if one and u == UNITS:
            out[2].append(("V", GH))
        if one and u in (UNITS // 2, UNITS):
            for c, t in enumerate((3, 4, 6, 7)):
                out[t].append(("W", (4 if u == UNITS else 0) + c))
        if not one and u in (UNITS - 1, UNITS):
            out[2].append(("R", u - (UNITS - 1)))
        if not one and u == UNITS + 1:
            for c, t in enumerate((1, 2, 4, 5)):
                out[t].append(("W", 4 + c))
        return out

    def units_of(has_next):
        return range(2, UNITS + 2 if has_next else UNITS)

    def tail(has_next):
        return [] if has_next else ([] if one else [("R", 1)]) + [("W", 4 + c) for c in range(4)]

    def schedule(has_next):
        return [it for u in units_of(has_next) for tile in steps(u, has_next) for it in tile] + tail(has_next)

    start = [("K", 0), ("VT", 0), ("VT", 1), ("Q", 0), ("V", GH), ("Q", 1)] if one else []
    start += [("S", u, b) for u in range(AHEAD) for b in (3, 2, 1, 0)]
    first = list(start)
    start += [it for u in range(2) for tile in steps(u, True) for it in tile]
    N0, N = len(start), len(schedule(True))
    assert N % 2 == 0
    place_start = {it: n - N0 for n, it in enumerate(start)}
    place_turn = {it: n for n, it in enumerate(schedule(True))}
    place_last = {it: n for n, it in enumerate(schedule(False))}
    HI0 = sum(it[0] in ("K", "Q", "V") for it in start)

    with core.stage(name) as sb:
        probs = [sb(f"probs{i}", [P, 18 * P]) for i in range(NB)]
        pt_h = sb("pt_h", [P, 4, HALF], F32R)
        pt_l = sb("pt_l", [P, 4, HALF], F32R)
        low = sb("low", [P, NB, 4])
        sums = sb("sums", [P, NB, 4])
        rinv = sb("rinv", [P, NB, 4])
        AJ = 2 if one else 1
        at_h = sb("at_h", [P, AJ, T], F32R)
        at_l = sb("at_l", [P, AJ, T], F32R)
        wo_h = sb("wo_h", [P, AJ, D], F32R)
        wo_l = sb("wo_l", [P, AJ, D], F32R)
        wo_raw = sb("wo_raw", [P, 2, D])
        if one:
            qh, ql = sb("qh", [P, 2, T], F32R), sb("ql", [P, 2, T], F32R)
            kh, kl = sb("kh", [P, T], F32R), sb("kl", [P, T], F32R)
            vh, vl = sb("vh", [P, TB, P], F32R), sb("vl", [P, TB, P], F32R)
            wq_raw, wkv_raw = io["wq_raw"], io["wkv_raw"]
            wqh, wql = sb("wqh", [P, 2, KT, P], F32R), sb("wql", [P, 2, KT, P], F32R)
            vt = sb("vt", [P, T])
            wkvh, wkvl = sb("wkvh", [P, KT, 2 * P], F32R), sb("wkvl", [P, KT, 2 * P], F32R)
        else:
            DQ = 4 * DH0
            q_stack = sb("q_stack", [DQ, GH, T], F32R)
            k_stack = sb("k_stack", [DQ, KV, T], F32R)
            v_pad = sb("v_pad", [P, TB, GH, P], F32R)
            spread = sb("spread", [P, TB, 2, GH, DH0])
            scale_of = sb("scale_of", [P, 2, HALF])
            scaled = sb("scaled", [P, 2, HALF])
            inv_spread = core.sem(f"{name}_inv_spread")
            out_scaled = core.sem(f"{name}_out_scaled")
            SPREADS = 3 * GH
        tbank, obank = core.banks[0:2], core.banks[2:4]

        kv_loaded = core.sem(f"{name}_kv_loaded")
        q_loaded = [core.sem(f"{name}_q_loaded{i}") for i in range(2 if one else GH)]
        wo_loaded = [core.sem(f"{name}_wo_loaded{i}") for i in range(2)]
        kv_split = core.sem(f"{name}_kv_split")
        q_split = core.sem(f"{name}_q_split")
        wo_split = core.sem(f"{name}_wo_split")
        w_hi = core.sem(f"{name}_w_hi")
        slot_full = core.sem(f"{name}_slot_full")
        hi_done = core.sem(f"{name}_hi_done")
        slot_free = core.sem(f"{name}_slot_free")
        exp_done = core.sem(f"{name}_exp_done")
        inv_done = core.sem(f"{name}_inv_done")
        norm_done = core.sem(f"{name}_norm_done")
        turned = core.sem(f"{name}_turned")
        pt_hi = core.sem(f"{name}_pt_hi")
        pt_lo = core.sem(f"{name}_pt_lo")
        pv_done = core.sem(f"{name}_pv_done")
        out_hi = core.sem(f"{name}_out_hi")
        out_lo = core.sem(f"{name}_out_lo")
        acc_zero = core.sem(f"{name}_acc_zero")
        own_pe, own_dve, own_pool = (core.sem(f"{name}_own_{e}") for e in ("pe", "dve", "pool"))
        pad_zero = core.sem(f"{name}_pad_zero")
        OUTS = UNITS if one else 2
        HIS = 2 + GH
        W_FIRST = [("kv", 0), ("q", 0), ("q", 1), ("q", 2)]
        W_AT = {2: [("q", 3), ("q", GH)], 3: [("wo", 0), ("wo", 1)], 4: [("kv", 1)], 5: [("q", GH + 1)],
                6: [("wo", 2), ("wo", 3)], 7: [("q", GH + 2)]}
        W_TURN = [w for u in W_AT for w in W_AT[u]]
        W_LAST = [w for w in W_TURN if w[0] == "wo" or w[0] == "q" and w[1] < GH]
        NW = len(W_TURN)

        full = lambda g, n: (g + 1) * N + (N0 + n + 1)
        read = lambda g, n: g * N + (N0 + n + 1 + 2)
        vacant = lambda g, n: g * N + (N0 + n + 1)
        slot_of = lambda n: core.slots[(N0 + n) % 2]
        full_before = lambda g, it, first: g * N + max(N0 + place_turn[it] + 1, N + N0 + place_start[first] + 1)
        q_used = lambda g, j: (full(g, place_turn[("Q", j - 2)]) if ("Q", j - 2) in place_turn
                               else full_before(g, ("Q", j + 2), ("Q", j - 2)))
        read_before = lambda g, it, first: g * N + max(N0 + place_turn[it] + 3 - N, N0 + place_start[first] + 3)

        width = lambda u, b: (BLOCKS[u % 2][b] + 1) * P
        offset = lambda u, b: sum(width(u, a) for a in range(b))
        block_of = lambda u, b: probs[u % NB][:, offset(u, b):offset(u, b) + width(u, b)]
        tile_col = lambda u, kb: sum(q < kb for q in BLOCKS[u % 2]) * P

        def out_view(t, j, u):
            if u % 2:
                return t[:, j, 2 * P:6 * P]
            return t[:, j, :].rearrange("p (a c) -> p a c", a=4)[:, 0:4:3, :]

        def bank_view(t, s):
            return t[:, s, :] if s else t[:, s, :].rearrange("p (a c) -> p a c", a=2)

        def bank_out(u):
            return obank[u % 2][:, :] if u % 2 else obank[u % 2][:, :].rearrange("p (a c) -> p a c", a=2)

        def turns(eng, turn):
            with eng.Fori(0, KV - 1) as g:
                turn(g, place_turn, True)
            turn(KV - 1, place_last, False)

        with nc.Block() as block:

            @block.sync
            def _(sp):
                def load_q(g, j):
                    for rows in range(4):
                        sp.dma_start(q_stack[rows * DH0:(rows + 1) * DH0, j, :].bitcast(F32),
                                     io["q"][rows % 2][bass.ds(g * (GH * DH0) + j * DH0, DH0), :]).then_inc(q_loaded[j], 16)

                def load(g, what, j):
                    if what == "kv":
                        sp.wait_ge(kv_split, g + (j + 1))
                        for s, w in enumerate((io["wk"], io["wv"])):
                            sp.dma_start(wkv_raw[:, :, s * P:(s + 1) * P],
                                         w.rearrange("(k p) n -> p k n", p=P)[:, :, bass.ds(g * P + j * P, P)]).then_inc(kv_loaded, 16)
                    elif what == "q":
                        sp.wait_ge(q_split, g * GH + (j + 1))
                        sp.dma_start(wq_raw[:, j % 2, :, :], io["wq"].rearrange("(k p) n -> p k n", p=P)
                                     [:, :, bass.ds(g * (GH * P) + j * P, P)]).then_inc(q_loaded[j % 2], 16)
                    else:
                        sp.wait_ge(wo_split, g * GH + (j + 1))
                        sp.dma_start(wo_raw[:, j % 2, :],
                                     io["wo"][bass.ds(g * (GH * P) + j * P, P), :]).then_inc(wo_loaded[j % 2], 16)

                def turn(g, place, has_next):
                    if one:
                        for what, j in W_TURN if has_next else W_LAST:
                            load(g, what, j)
                        return
                    sp.wait_ge(wo_split, g + 1)
                    for s in range(2):
                        sp.dma_start(wo_raw[s * 64:(s + 1) * 64, 0, :], io["wo"][bass.ds(g * 64, 64), :]).then_inc(wo_loaded[0], 16)
                    for j in range(GH) if has_next else ():
                        sp.wait_ge(slot_full, full(g, place[("S", 2 * j + 1, 0)]) if j >= 2
                                   else full_before(g, ("S", 2 * j + 1 + UNITS, 0), ("S", 2 * j + 1, 0)))
                        load_q(g + 1, j)

                if one:
                    sp.sem_inc(kv_loaded, 32)
                    for i in range(2):
                        sp.sem_inc(q_loaded[i], 16)
                    load(0, "q", 2)
                else:
                    load_q(0, 0)
                    for part, rows in ((0, 0), (0, 1), (1, 2), (1, 3)):
                        sp.dma_start(k_stack[rows * DH0:(rows + 1) * DH0, :, :].bitcast(F32),
                                     io["k"][part].rearrange("(g i) t -> i g t", i=DH0)).then_inc(kv_loaded, 16)
                    for j in range(1, GH):
                        load_q(0, j)
                turns(sp, turn)

            @block.gpsimd
            def _(pool):
                pool.sem_inc(kv_split, 1)
                pool.sem_inc(q_split, 2)
                pool.sem_inc(wo_split, 2 if one else 1)

                def split(raw, hi, lo, count, done):
                    pool.sem_inc(own_pool, 1)
                    pool.tensor_copy(hi, raw).then_inc(w_hi, 1)
                    pool.wait_ge(w_hi, count)
                    pool.tensor_tensor(lo, raw, hi.bitcast(F32), ALU.subtract).then_inc(done, 1)

                def prepare(g, what, j, count, place):
                    if what == "kv":
                        pool.wait_ge(kv_loaded, g * 32 + (32 * j + 32))
                        if j:
                            pool.wait_ge(slot_full, full_before(g, ("VT", 1), ("VT", 1)))
                        split(wkv_raw[:, :, :], wkvh[:, :, :], wkvl[:, :, :], count, kv_split)
                    elif what == "q":
                        pool.wait_ge(q_loaded[j % 2], g * 32 + (j // 2) * 16 + 16)
                        if place is place_start and j == 2:
                            pool.wait_ge(slot_full, full(0, place_start[("Q", 0)]))
                        elif j > 2:
                            pool.wait_ge(slot_full, q_used(g, j))
                        split(wq_raw[:, j % 2, :, :], wqh[:, j % 2, :, :], wql[:, j % 2, :, :], count, q_split)
                    else:
                        pool.wait_ge(wo_loaded[j % 2], g * 32 + (j // 2) * 16 + 16)
                        pool.wait_ge(slot_full, full(g, place_turn[("W", 3)]) if j >= 2 else g * N + (N + N0))
                        split(wo_raw[:, j % 2, :], wo_h[:, j % 2, :], wo_l[:, j % 2, :], count, wo_split)

                def place_v(g, j):
                    pool.sem_inc(own_pool, 1)
                    for part, t in ((0, io["v0"]), (1, io["v0l"])):
                        c = part * 64 + j * DH0
                        pool.tensor_copy(v_pad[:, :, j, c:c + DH0], t[:, :, bass.ds(g * DH0, DH0)]).then_inc(kv_split, 1)

                def normalise(g, u):
                    pool.wait_ge(inv_done, g * UNITS + (u + 1))
                    for b in range(4):
                        pool.tensor_tensor(block_of(u, b), block_of(u, b), rinv[:, u % NB, b:b + 1].to_broadcast([P, width(u, b)]),
                                           ALU.mult).then_inc(norm_done, 1)

                def spread_inverses(g, u):
                    pool.wait_ge(inv_done, g * UNITS + (u + 1))
                    if u >= UNITS:
                        pool.wait_ge(slot_full, full(g, place_turn[("R", u - UNITS)]))
                    pool.sem_inc(own_pool, 1)
                    if u % 2:
                        blocks = ((2, 0, 4),)
                    else:
                        blocks = ((0, 0, 2), (6, 2, 2))
                    for first, b, n in blocks:
                        pool.tensor_copy(spread[:, first:first + n, :, u // 2 % GH, :],
                                         rinv[:, u % NB, b:b + n].unsqueeze(2).unsqueeze(3).to_broadcast([P, n, 2, DH0])
                                         ).then_inc(inv_spread, 1)

                def low_out(g, e):
                    pool.wait_ge(out_hi, g * OUTS + (e + 1))
                    pool.sem_inc(own_pool, 1)
                    pool.tensor_tensor(out_view(at_l, 0, e), bank_view(scaled, e), out_view(at_h, 0, e).bitcast(F32),
                                       ALU.subtract).then_inc(out_lo, 1)

                def turn(g, place, has_next):
                    if one:
                        n = len(W_FIRST)
                        for u in units_of(has_next):
                            if u + 1 < UNITS or has_next:
                                normalise(g, u + 1)
                            for what, j in W_TURN if has_next else W_LAST:
                                if (what, j) in W_AT.get(u, ()):
                                    n += 1
                                    prepare(g, what, j, g * NW + n, place)
                        return
                    for u in units_of(has_next):
                        if u >= UNITS:
                            low_out(g, u - UNITS)
                        spread_inverses(g, u)
                        if u == 4:
                            pool.wait_ge(wo_loaded[0], g * 32 + 32)
                            pool.wait_ge(slot_full, g * N + (N + N0))
                            split(wo_raw[:, 0, :], wo_h[:, 0, :], wo_l[:, 0, :], g + 1, wo_split)
                        if has_next and u % 2 == 0:
                            pool.wait_ge(pv_done, g * TURN + (first_tile[u] + 4))
                            place_v(g + 1, u // 2 - 1)
                    if not has_next:
                        low_out(g, 0)
                        low_out(g, 1)

                if one:
                    for n, (what, j) in enumerate(W_FIRST):
                        prepare(0, what, j, n + 1, place_start)
                    for u in range(3):
                        normalise(0, u)
                else:
                    pool.memset(v_pad[:, :, :, :].bitcast(F32), 0.0).then_inc(pad_zero, 1)
                    pool.wait_ge(pad_zero, 1)
                    for j in range(GH):
                        place_v(0, j)
                    for u in range(2):
                        spread_inverses(0, u)
                turns(pool, turn)

            @block.scalar
            def _(act):
                def high(g, n, count, dst, scale):
                    act.wait_ge(slot_full, full(g, n))
                    act.activation(dst, slot_of(n)[:, :], ACT.Copy, scale=scale).then_inc(hi_done, 1)

                def exp(g, n, u, b):
                    i = u % NB
                    act.wait_ge(slot_free, read(g, n))
                    act.activation(block_of(u, b), block_of(u, b), ACT.Exp, bias=low[:, i, b:b + 1],
                                   scale=-1.0, accum_out=sums[:, i, b:b + 1]).then_inc(exp_done, 1)

                def item(g, place, it):
                    n = place[it]
                    if it[0] == "S":
                        exp(g, n, it[1], it[2])
                    elif it[0] == "K":
                        high(g, n, 0, kh[:, :], 1.0)
                    elif it[0] == "V":
                        high(g, n, 1, vh[:, :, :].rearrange("p b n -> p (b n)"), 1.0)
                    elif it[0] == "Q":
                        high(g, n, 2, qh[:, it[1] % 2, :], -DH1 ** -0.5)
                    elif it[0] == "R":
                        s = it[1]
                        act.wait_ge(out_scaled, g * OUTS + (s + 1 + 2))
                        act.activation(out_view(at_h, 0, s), bank_view(scaled, s), ACT.Copy).then_inc(out_hi, 1)

                def high_out(g, place, u):
                    act.wait_ge(pv_done, g * TURN + (first_tile[u + 1] + 4))
                    if u >= 4:
                        act.wait_ge(slot_full, full(g, place[("W", 7 if u >= UNITS else 3)]))
                    act.activation(out_view(at_h, u // 2 % AJ, u), bank_out(u), ACT.Copy).then_inc(out_hi, 1)

                def unit(g, place, has_next, u):
                    late = []
                    for kb, its in enumerate(steps(u, has_next)):
                        for it in its:
                            if it[0] == "V":
                                item(g, place, it)
                        if any(it[0] in LONG for it in its):
                            for it in late:
                                item(g, place, it)
                            late = []
                        n, c = first_tile[u] + kb, tile_col(u, kb)
                        act.wait_ge(turned, g * TURN + (n + 1))
                        act.wait_ge(pv_done, g * TURN + (n + 1))
                        act.activation(pt_h[:, n % 4, c:HALF], tbank[n % 2][:, c:HALF], ACT.Copy).then_inc(pt_hi, 1)
                        if one and kb == LAG - 1 and u:
                            high_out(g, place, u - 1)
                        for it in [it for it in its if it[0] in "KQ"] + late:
                            item(g, place, it)
                        late = [it for it in its if it[0] in "SR"]
                    for it in late:
                        item(g, place, it)

                def turn(g, place, has_next):
                    for u in units_of(has_next):
                        unit(g, place, has_next, u)
                    if one and not has_next:
                        high_out(g, place, UNITS - 1)
                    for it in tail(has_next):
                        item(g, place, it)

                for it in first:
                    item(0, place_start, it)
                for u in range(2):
                    unit(0, place_start, True, u)
                turns(act, turn)

            @block.vector
            def _(dve):
                dve.sem_inc(slot_free, 2)
                dve.sem_inc(pt_lo, 2)
                dve.sem_inc(out_lo, 2)
                if not one:
                    dve.sem_inc(out_scaled, 2)
                dve.memset(acc[:, :, :], 0.0).then_inc(acc_zero, 1)
                dve.wait_ge(acc_zero, 1)

                def low_part(g, n, count, hi, lo, scale):
                    dve.wait_ge(hi_done, count)
                    dve.scalar_tensor_tensor(lo, slot_of(n)[:, :], scale, hi.bitcast(F32), ALU.mult,
                                             ALU.subtract).then_inc(slot_free, 1)

                def minimum(g, n, u, b):
                    i, w = u % NB, width(u, b)
                    dve.wait_ge(slot_full, full(g, n))
                    dve.sem_inc(own_dve, 1)
                    dve.tensor_tensor_reduce(block_of(u, b), slot_of(n)[:, 0:w], mask[:, T - w:T], 1.0, 3e38,
                                             ALU.add, ALU.min, low[:, i, b:b + 1]).then_inc(slot_free, 1)

                def item(g, place, it, his):
                    n = place[it]
                    if it[0] == "S":
                        minimum(g, n, it[1], it[2])
                    elif it[0] == "K":
                        low_part(g, n, his + 1, kh[:, :], kl[:, :], 1.0)
                    elif it[0] == "VT":
                        dve.wait_ge(slot_full, full(g, n))
                        dve.tensor_copy(vt[:, it[1] * HALF:(it[1] + 1) * HALF], slot_of(n)[:, 0:HALF]).then_inc(slot_free, 1)
                    elif it[0] == "V":
                        low_part(g, n, his + 1, vh[:, :, :].rearrange("p b n -> p (b n)"),
                                 vl[:, :, :].rearrange("p b n -> p (b n)"), 1.0)
                    elif it[0] == "Q":
                        low_part(g, n, his + 1, qh[:, it[1] % 2, :], ql[:, it[1] % 2, :], -DH1 ** -0.5)
                    elif it[0] == "R":
                        s = it[1]
                        dve.wait_ge(slot_full, full(g, n))
                        dve.tensor_copy(scale_of[:, s, :], slot_of(n)[:, 0:HALF]).then_inc(slot_free, 1)
                        dve.wait_ge(slot_free, read(g, n))
                        dve.wait_ge(pv_done, g * TURN + (first_tile[UNITS - 1 + s] + 4))
                        dve.wait_ge(out_lo, g * OUTS + (s + 1))
                        dve.tensor_tensor(scaled[:, s, :], obank[s][:, :], scale_of[:, s, :], ALU.mult).then_inc(out_scaled, 1)
                    else:
                        dve.wait_ge(slot_full, full(g, n))
                        c = it[1] % 4
                        part = acc[:, 2 * c:2 * c + 2, :].rearrange("p b n -> p (b n)")
                        dve.tensor_tensor(part, part, slot_of(n)[:, :], ALU.add).then_inc(slot_free, 1)

                def invert(g, u):
                    if not one and u >= NB:
                        w = u - NB
                        dve.wait_ge(inv_spread, g * SPREADS + (3 * (w // 2) + 2 + w % 2))
                    dve.wait_ge(exp_done, g * (4 * UNITS) + 4 * (u + 1))
                    dve.reciprocal(rinv[:, u % NB, :], sums[:, u % NB, :]).then_inc(inv_done, 1)

                def low_out(g, u):
                    dve.wait_ge(out_hi, g * OUTS + (u + 1))
                    j = u // 2 % AJ
                    dve.tensor_tensor(out_view(at_l, j, u), bank_out(u), out_view(at_h, j, u).bitcast(F32),
                                      ALU.subtract).then_inc(out_lo, 1)

                def unit(g, place, has_next, u, his):
                    for kb, its in enumerate(steps(u, has_next)):
                        for it in its:
                            if it[0] in "SV":
                                item(g, place, it, g * HIS + his)
                                his += it[0] == "V"
                        n, c = first_tile[u] + kb, tile_col(u, kb)
                        dve.wait_ge(pt_hi, g * TURN + (n + 1))
                        dve.tensor_tensor(pt_l[:, n % 4, c:HALF], tbank[n % 2][:, c:HALF],
                                          pt_h[:, n % 4, c:HALF].bitcast(F32), ALU.subtract).then_inc(pt_lo, 1)
                        if one and kb == LAG - 1 and u:
                            low_out(g, u - 1)
                        v = u + NORM_AHEAD
                        if kb == INVERT_AT[u % 2] and (v < UNITS or has_next):
                            invert(g, v)
                        for it in its:
                            if it[0] not in "SV":
                                item(g, place, it, g * HIS + his)
                                his += it[0] in ("K", "Q")
                    return his

                def turn(g, place, has_next):
                    his = HI0
                    for u in units_of(has_next):
                        his = unit(g, place, has_next, u, his)
                    if one and not has_next:
                        low_out(g, UNITS - 1)
                    for it in tail(has_next):
                        item(g, place, it, g * HIS + his)

                his = 0
                for it in first:
                    item(0, place_start, it, his)
                    his += it[0] in ("K", "Q", "V")
                for u in range(NORM_AHEAD):
                    invert(0, u)
                for u in range(2):
                    his = unit(0, place_start, True, u, his)
                turns(dve, turn)

            @block.tensor
            def _(pe):
                pe.sem_inc(pv_done, 4)
                pe.sem_inc(slot_full, N)

                def project(out, hi, lo):
                    for h in range(2):
                        cols = slice(h * HALF, (h + 1) * HALF)
                        pairs = [pr for k in range(KT) for pr in three(hi(k), lo(k), xh[:, k, cols], xl[:, k, cols])]
                        mm = products(pe, out[:, cols], pairs)
                    return mm

                def item(g, place, it):
                    n = place[it]
                    out = slot_of(n)
                    pe.wait_ge(slot_free, vacant(g, n))
                    if it[0] == "K":
                        pe.wait_ge(kv_split, g + (2 + (it[1] > 0)))
                        mm = project(out, lambda k: wkvh[:, k, 0:P], lambda k: wkvl[:, k, 0:P])
                    elif it[0] == "VT":
                        cols = slice(it[1] * HALF, (it[1] + 1) * HALF)
                        mm = products(pe, out[:, 0:HALF], [pr for k in range(KT) for pr in three(
                            wkvh[:, k, P:2 * P], wkvl[:, k, P:2 * P], xh[:, k, cols], xl[:, k, cols])])
                    elif it[0] == "R":
                        w = UNITS - 2 + it[1]
                        pe.wait_ge(inv_spread, g * SPREADS + (3 * (w // 2) + 2 + w % 2))
                        for i, b in enumerate(BLOCKS[it[1]]):
                            mm = pe.matmul(out[:, i * P:(i + 1) * P], spread[:, b, :, :, :].rearrange("p s j i -> p (s j i)"),
                                           ident[:, :], start=True, stop=True)
                    elif it[0] == "V":
                        pe.wait_ge(slot_free, read(g, place[("VT", 1)]))
                        for b in range(TB):
                            mm = pe.transpose(out[:, b * P:(b + 1) * P], vt[:, b * P:(b + 1) * P], ident[:, :])
                    elif it[0] == "Q":
                        j = it[1]
                        pe.wait_ge(q_split, g * GH + (j + 1 + 2))
                        mm = project(out, lambda k: wqh[:, j % 2, k, :], lambda k: wql[:, j % 2, k, :])
                    elif it[0] == "S":
                        u, b = it[1], it[2]
                        j, w = u // 2, width(u, b)
                        gs = g + (1 if u >= UNITS else 0)
                        if one and u % 2 == 0 and b == 3:
                            if ("Q", j) in place:
                                pe.wait_ge(slot_free, read(g, max(place[("Q", j)], place.get(("K", j), -N0))))
                            else:
                                pe.wait_ge(slot_free, read_before(g, ("Q", j + GH), ("Q", j)))
                        if not one and u % 2 == 0 and b == 3:
                            pe.wait_ge(q_loaded[j % GH], g * 64 + (64 if j < GH else 128))
                        if not one:
                            pe.sem_inc(own_pe, 1)
                        qc = slice(w - P, w)
                        for c0 in range(0, w, HALF):
                            c1 = min(c0 + HALF, w)
                            if one:
                                pairs = three(qh[:, j % 2, qc], ql[:, j % 2, qc], kh[:, c0:c1], kl[:, c0:c1])
                            else:
                                pairs = [(q_stack[:, j % GH, qc], k_stack[:, bass.ds(gs, 1), c0:c1]
                                          .rearrange("p g t -> p (g t)"))]
                            mm = products(pe, out[:, c0:c1], pairs)
                    else:
                        half, c = it[1] // 4, it[1] % 4
                        if c == 0 and one:
                            pe.wait_ge(wo_split, g * GH + (2 * half + 2 + 2))
                            pe.wait_ge(out_lo, g * OUTS + (4 * half + 4 + 2))
                        elif c == 0:
                            pe.wait_ge(wo_split, g + 2)
                            pe.wait_ge(out_lo, g * OUTS + (OUTS + 2))
                        for b in (2 * c, 2 * c + 1):
                            toks = slice(b * P, (b + 1) * P)
                            pairs = [pr for j in range(AJ) for pr in three(at_h[:, j, toks], at_l[:, j, toks],
                                                                           wo_h[:, j, :], wo_l[:, j, :])]
                            mm = products(pe, out[:, (b % 2) * HALF:(b % 2 + 1) * HALF], pairs)
                    mm.then_inc(slot_full, 1)

                def times_v(g, place, u, kb):
                    n, j, s, c = first_tile[u] + kb, u // 2 % GH, u % 2, tile_col(u, kb)
                    pe.wait_ge(pt_lo, g * TURN + (n + 1 + 2))
                    if kb == 0 and one and u == UNITS:
                        pe.wait_ge(slot_free, read(g, place_turn[("V", GH)]))
                    if kb == 0 and one and place is place_start:
                        pe.wait_ge(slot_free, read(g, place_start[("V", GH)]))
                    if kb == 0 and one:
                        pe.wait_ge(out_lo, g * OUTS + (u + 1))
                    if kb == 0 and not one:
                        pe.wait_ge(kv_split, g * 8 + (2 * (u // 2 + 1) + 1))
                        if j == 0:
                            pe.wait_ge(out_scaled, g * OUTS + (u % UNITS + 1 + (OUTS if u >= UNITS else 0)))
                    ph, pl = pt_h[:, n % 4, c:HALF], pt_l[:, n % 4, c:HALF]
                    if one:
                        pairs = three(vh[:, kb, :], vl[:, kb, :], ph, pl)
                    else:
                        pairs = [(v_pad[:, kb, j, :], ph), (v_pad[:, kb, j, :], pl)]
                    first = kb == 0 and (one or j == 0)
                    final = kb == KBS[s] - 1 and (one or j == GH - 1)
                    products(pe, obank[s][:, c:HALF], pairs, first, final).then_inc(pv_done, 1)

                def unit(g, place, has_next, u):
                    for kb, its in enumerate(steps(u, has_next)):
                        for it in its:
                            item(g, place, it)
                        n, c = first_tile[u] + kb, tile_col(u, kb)
                        if kb == 0:
                            pe.wait_ge(norm_done if one else exp_done, g * (4 * UNITS) + 4 * (u + 1))
                        pe.wait_ge(pt_lo, g * TURN + (n + 1))
                        for b in range(c // P, 4):
                            t = pe.transpose(tbank[n % 2][:, b * P:(b + 1) * P],
                                             block_of(u, b)[:, kb * P:(kb + 1) * P], ident[:, :])
                        t.then_inc(turned, 1)
                        if kb >= LAG:
                            times_v(g, place, u, kb - LAG)
                        elif u:
                            times_v(g, place, u - 1, KBS[(u - 1) % 2] + kb - LAG)

                def turn(g, place, has_next):
                    for u in units_of(has_next):
                        unit(g, place, has_next, u)
                    if not has_next:
                        for kb in range(KBS[1] - LAG, KBS[1]):
                            times_v(g, place, UNITS - 1, kb)
                    for it in tail(has_next):
                        item(g, place, it)

                if not one:
                    pe.wait_ge(kv_loaded, 64)
                else:
                    pe.wait_ge(kv_split, 2)
                for it in first:
                    item(0, place_start, it)
                for u in range(2):
                    unit(0, place_start, True, u)
                turns(pe, turn)


def swiglu_inputs(sb, io):
    G, GD, WIDE = GU_GROUPS, DN_GROUPS, 2 * INTER
    t = {"ids_gu": sb("f0_ids_gu", [G, D], I32), "ids_dn": sb("f0_ids_dn", [GD, INTER], I32),
         "group": sb("f0_group", [GD, 1]),
         "shift": sb("f0_shift", [P, 1], U32),
         "zq_gu": sb("f0_zq_gu", [G, WIDE // NIBBLES], U32), "zq_dn": sb("f0_zq_dn", [GD, D // NIBBLES], U32),
         "sc_gu": sb("f0_sc_gu", [G, WIDE]), "sc_dn": sb("f0_sc_dn", [GD, D])}
    loads = [(t["ids_gu"][:, :], io["L0_ffn_g_idx_gu"].rearrange("(a n) -> a n", a=1).to_broadcast([G, D])),
             (t["ids_dn"][:, :], io["L0_ffn_g_idx_down"].rearrange("(a n) -> a n", a=1).to_broadcast([GD, INTER])),
             (t["zq_gu"][:, :], io["L0_ffn_qzeros_gu"]), (t["zq_dn"][:, :], io["L0_ffn_qzeros_down"]),
             (t["sc_gu"][:, :], io["L0_ffn_scales_gu"]), (t["sc_dn"][:, :], io["L0_ffn_scales_down"]),
             (t["group"][:, :], io["group"]), (t["shift"][:, :], io["shift"])]
    return t, loads


def swiglu(core, consts, acc, xh, xl, inputs, io):
    nc = core.nc
    G, GD, WIDE = GU_GROUPS, DN_GROUPS, 2 * INTER
    CHUNKS = 3
    with core.stage("f0") as sb:
        zero_gu = sb("zero_gu", [G, 2, INTER], F32R)
        sch_gu, scl_gu = sb("sch_gu", [G, 2, INTER], F32R), sb("scl_gu", [G, 2, INTER], F32R)
        zero_dn = sb("zero_dn", [GD, D], F32R)
        sch_dn, scl_dn = sb("sch_dn", [GD, D], F32R), sb("scl_dn", [GD, D], F32R)
        hot_gu, hot_dn = sb("hot_gu", [G, D], F32R), sb("hot_dn", [GD, INTER], F32R)
        hot_tile = sb("hot_tile", [GD, 2, P], F32R)
        shift, group = inputs["shift"], inputs["group"]
        raw = sb("raw", [P, 2, 3 * HALF], U32)
        nibble = sb("nibble", [P, 2, 3 * HALF], U32)
        diff = sb("diff", [P, 2, HALF])
        weight = sb("weight", [P, 2, HALF])
        wh, wl = sb("wh", [P, 2, KT, 2, P], F32R), sb("wl", [P, 2, KT, 2, P], F32R)
        dh, dl = sb("dh", [P, 2, D], F32R), sb("dl", [P, 2, D], F32R)
        gate, hid = sb("gate", [P, 2, HALF]), sb("hid", [P, 2, HALF])
        hh, hl = sb("hh", [P, T], F32R), sb("hl", [P, T], F32R)
        ids, zq, sc = ({n: inputs[f"{kind}_{n}"] for n in ("gu", "dn")} for kind in ("ids", "zq", "sc"))
        idf = {"gu": sb("idf_gu", [G, D]), "dn": sb("idf_dn", [GD, INTER])}
        wrap = {n: t[:, :].bitcast(F32) for n, t in ids.items()}
        zi = {"gu": nibble[0:G, :, :].rearrange("p a n -> p (a n)")[:, 0:WIDE], "dn": sb("zi_dn", [GD, D], U32)[:, :]}
        S = {n: core.sem(f"f0_{n}") for n in (
            "acc_zero",
            "ids_done",
            "zero_bits",
            "zeros_done",
            "scale_hi",
            "scale_lo",
            "raw_loaded0", "raw_loaded1",
            "unpacked",
            "hot_copied",
            "selected",
            "diff_done",
            "weight_done",
            "w_hi", "w_lo",
            "gu",
            "gate", "hid",
            "h_hi", "h_lo",
            "dn",
            "added",
            "own_pool", "own_pe")}
        gu_bank, zero_bank, scale_bank = core.slots, core.banks[2], core.banks[3]
        LOADS = (2 * KT + 1) * 16
        IDS = 10

        def turns(eng, body):
            body(0, 0, P, P)
            with eng.Fori(0, (FT - 3) // 2) as i:
                for n in range(2):
                    body(2 * i + (n + 1), 1 - n, P, P)
            body(FT - 2, 1, P, F_LAST)
            body(FT - 1, 0, F_LAST, None)

        def first_tile(f):
            return isinstance(f, int) and f == 0

        def dn_bank(b):
            return core.slots[b // 4][:, (b % 4) * HALF:(b % 4 + 1) * HALF] if b % 4 < 2 else core.banks[b % 2][:, :]

        def chunk(t, par, c, F):
            if c == 2:
                return t[0:F, par, 2 * HALF:3 * HALF]
            return t[:, par, c * HALF:(c + 1) * HALF].rearrange("p (k s n) -> p k s n", k=2, s=2)[:, :, :, 0:F]

        def flat(t, c, F):
            return t[0:F, :] if c == 2 else t[:, :].rearrange("p (k s n) -> p k s n", k=2, s=2)[:, :, :, 0:F]

        def parts(par, c, F):
            return [t[0:F, par, :] for t in (dh, dl)] if c == 2 else [t[:, par, 2 * c:2 * c + 2, :, 0:F] for t in (wh, wl)]

        with nc.Block() as block:

            @block.sync
            def _(sp):
                def load(f, par, F):
                    def spread_rows(src, out, rows, cols):
                        sp.dma_start(out,
                                     src.unsqueeze(1).to_broadcast([rows // NIBBLES, NIBBLES, cols])).then_inc(S[f"raw_loaded{par}"], 16)

                    for k in range(KT):
                        for s in range(2):
                            spread_rows(io["qgu"][k * 16:(k + 1) * 16, bass.ds(f * P + s * INTER, F)],
                                        raw[:, par, (2 * k + s) * P:(2 * k + s) * P + F], P, F)
                    spread_rows(io["qdn"][bass.ds(f * (P // NIBBLES), F // NIBBLES), :], raw[0:F, par, 2 * HALF:3 * HALF], F, D)

                def body(f, par, F, F_next):
                    if F_next:
                        sp.wait_ge(S["unpacked"], f + 1)
                        load(f + 1, 1 - par, F_next)

                load(0, 0, P)
                turns(sp, body)

            @block.gpsimd
            def _(pool):
                pool.sem_inc(S["h_lo"], 2)
                pool.memset(acc[:, :, :], 0.0).then_inc(S["acc_zero"], 1)
                for n, (t, h, l) in enumerate(((sc["gu"], sch_gu, scl_gu), (sc["dn"], sch_dn, scl_dn))):
                    pool.wait_ge(S["scale_hi"], n + 1)
                    a, b = (h[:, :], l[:, :]) if n else (h[:, :, :].rearrange("g s n -> g (s n)"), l[:, :, :].rearrange("g s n -> g (s n)"))
                    pool.tensor_tensor(b, t[:, :], a.bitcast(F32), ALU.subtract).then_inc(S["scale_lo"], 1)

                def low(f, par, c, F):
                    h, l = parts(par, c, F)
                    pool.wait_ge(S["w_hi"], f * CHUNKS + (c + 1))
                    pool.sem_inc(S["own_pool"], 1)
                    pool.tensor_tensor(l, flat(weight[:, (par + c) % 2, :], c, F), h.bitcast(F32),
                                       ALU.subtract).then_inc(S["w_lo"], 1)

                def body(f, par, F, F_next):
                    for h in range(2):
                        if F_next:
                            low(f + 1, 1 - par, h, F_next)
                        cols = slice(h * HALF, (h + 1) * HALF)
                        pool.wait_ge(S["h_hi"], f * 2 + (h + 1))
                        pool.sem_inc(S["own_pool"], 1)
                        pool.tensor_tensor(hl[0:F, cols], hid[0:F, h, :], hh[0:F, cols].bitcast(F32),
                                           ALU.subtract).then_inc(S["h_lo"], 1)
                    if F_next:
                        low(f + 1, 1 - par, 2, F_next)

                for c in range(CHUNKS):
                    low(0, 0, c, P)
                turns(pool, body)

            @block.scalar
            def _(act):
                act.activation(sch_gu[:, :, :].rearrange("g s n -> g (s n)"), sc["gu"][:, :], ACT.Copy).then_inc(S["scale_hi"], 1)
                act.activation(sch_dn[:, :], sc["dn"][:, :], ACT.Copy).then_inc(S["scale_hi"], 1)

                def hot(f, par, F):
                    act.wait_ge(S["selected"], f * CHUNKS)
                    act.activation(hot_tile[:, par, 0:F], hot_dn[:, bass.ds(f * P, F)].bitcast(F32), ACT.Copy).then_inc(S["hot_copied"], 1)

                def high(f, par, c, F):
                    h, l = parts(par, c, F)
                    act.wait_ge(S["weight_done"], f * CHUNKS + (c + 1))
                    act.activation(h, flat(weight[:, (par + c) % 2, :], c, F), ACT.Copy).then_inc(S["w_hi"], 1)

                def body(f, par, F, F_next):
                    for h in range(2):
                        if F_next:
                            if h == 0:
                                hot(f + 1, 1 - par, F_next)
                            high(f + 1, 1 - par, h, F_next)
                        cols = slice(h * HALF, (h + 1) * HALF)
                        act.wait_ge(S["gu"], f * 2 + (h + 1))
                        act.activation(gate[0:F, h, :], gu_bank[h][0:F, 0:HALF], ACT.Silu).then_inc(S["gate"], 1)
                        act.wait_ge(S["hid"], f * 2 + (h + 1 + 2))
                        act.wait_ge(S["dn"], f * 8 + (4 * h + 4))
                        act.activation(hh[0:F, cols], hid[0:F, h, :], ACT.Copy).then_inc(S["h_hi"], 1)
                    if F_next:
                        high(f + 1, 1 - par, 2, F_next)

                act.wait_ge(S["ids_done"], IDS)
                act.activation(hot_tile[:, 0, :], hot_dn[:, 0:P].bitcast(F32), ACT.Copy).then_inc(S["hot_copied"], 1)
                for c in range(CHUNKS):
                    high(0, 0, c, P)
                turns(act, body)

            @block.vector
            def _(dve):
                dve.sem_inc(S["unpacked"], 1)
                dve.sem_inc(S["hid"], 2)
                dve.sem_inc(S["added"], 8)
                both = (("gu", G, hot_gu), ("dn", GD, hot_dn))
                steps = [0]

                def step(make):
                    for what in both:
                        make(*what).then_inc(S["ids_done"], 1)
                    steps[0] += 2
                    dve.wait_ge(S["ids_done"], steps[0])

                step(lambda n, g, t: dve.tensor_copy(idf[n][:, :], ids[n][:, :]))
                step(lambda n, g, t: dve.tensor_scalar(wrap[n], idf[n][:, :], 0.0, float(g), ALU.is_lt, ALU.mult))
                step(lambda n, g, t: dve.tensor_tensor(idf[n][:, :], idf[n][:, :], wrap[n], ALU.add))
                step(lambda n, g, t: dve.tensor_scalar(wrap[n], idf[n][:, :], 0.0, float(g - 1), ALU.max, ALU.min))
                step(lambda n, g, t: dve.tensor_scalar(t[:, :], wrap[n], group[0:g, 0:1], None, ALU.is_equal))
                assert steps[0] == IDS
                for n, g, t in both:
                    v = zi[n].rearrange("g (c s) -> g c s", s=NIBBLES)
                    for s in range(NIBBLES):
                        dve.tensor_scalar(v[:, :, s], zq[n][:, :], 4 * s, 15, ALU.logical_shift_right,
                                          ALU.bitwise_and).then_inc(S["zero_bits"], 1)
                dve.wait_ge(S["zero_bits"], 2 * NIBBLES)
                dve.tensor_scalar(zero_gu[:, :, :].rearrange("g s n -> g (s n)"), zi["gu"], 1.0, None, ALU.add).then_inc(S["zeros_done"], 1)
                dve.tensor_scalar(zero_dn[:, :], zi["dn"], 1.0, None, ALU.add).then_inc(S["zeros_done"], 1)
                dve.wait_ge(S["acc_zero"], 1)

                dve.wait_ge(S["zeros_done"], 2)

                def unpack(f, par, F):
                    dve.wait_ge(S[f"raw_loaded{par}"], (f + 2 - par) * (LOADS // 2))
                    if F == P:
                        dve.tensor_scalar(nibble[:, par, :], raw[:, par, :], shift[:, 0:1], 15, ALU.logical_shift_right,
                                          ALU.bitwise_and).then_inc(S["unpacked"], 1)
                        return
                    out, in_ = (t[:, par, 0:2 * HALF].rearrange("p (k n) -> p k n", n=P)[:, :, 0:F] for t in (nibble, raw))
                    dve.tensor_scalar(out, in_, shift[:, 0:1], 15, ALU.logical_shift_right,
                                      ALU.bitwise_and).then_inc(S["unpacked"], 1)
                    dve.tensor_scalar(nibble[0:F, par, 2 * HALF:], raw[0:F, par, 2 * HALF:], shift[0:F, 0:1], 15,
                                      ALU.logical_shift_right, ALU.bitwise_and).then_inc(S["unpacked"], 1)

                def weights(f, par, c, F):
                    n = (par + c) % 2
                    begin = first_tile(f)
                    dve.wait_ge(S["selected"], f * CHUNKS + (c + 1 + CHUNKS))
                    dve.wait_ge(S["unpacked"], f + (2 if F == P else 3))
                    if not begin or c:
                        dve.wait_ge(S["weight_done"], f * CHUNKS + c)
                    dve.tensor_tensor(flat(diff[:, n, :], c, F), chunk(nibble, par, c, F), flat(zero_bank, c, F),
                                      ALU.subtract).then_inc(S["diff_done"], 1)
                    dve.wait_ge(S["diff_done"], f * CHUNKS + (c + 1))
                    if not begin or c == 2:
                        dve.wait_ge(S["w_lo"], f * CHUNKS + (c - 1))
                    dve.tensor_tensor(flat(weight[:, n, :], c, F), flat(diff[:, n, :], c, F), flat(scale_bank, c, F),
                                      ALU.mult).then_inc(S["weight_done"], 1)

                def hidden(f, h, F):
                    dve.wait_ge(S["gate"], f * 2 + (h + 1))
                    dve.wait_ge(S["h_lo"], f * 2 + (h + 1))
                    dve.tensor_tensor(hid[0:F, h, :], gate[0:F, h, :], gu_bank[h][0:F, HALF:2 * HALF],
                                      ALU.mult).then_inc(S["hid"], 1)

                def add(f, b):
                    dve.wait_ge(S["dn"], f * 8 + (b + 1 + 8))
                    dve.tensor_tensor(acc[:, b, :], acc[:, b, :], dn_bank(b), ALU.add).then_inc(S["added"], 1)

                def body(f, par, F, F_next):
                    if F_next:
                        unpack(f + 1, 1 - par, F_next)
                    for h in range(2):
                        if F_next:
                            weights(f + 1, 1 - par, h, F_next)
                        hidden(f, h, F)
                        if h == 0 and not first_tile(f):
                            for b in range(4, 8):
                                add(f - 1, b)
                    if F_next:
                        weights(f + 1, 1 - par, 2, F_next)
                    for b in range(4):
                        add(f, b)

                unpack(0, 0, P)
                for c in range(CHUNKS):
                    weights(0, 0, c, P)
                turns(dve, body)
                for b in range(4, 8):
                    add(FT - 1, b)

            @block.tensor
            def _(pe):
                pe.sem_inc(S["selected"], CHUNKS)
                pe.sem_inc(S["dn"], 8)
                pe.wait_ge(S["ids_done"], IDS)
                pe.wait_ge(S["zeros_done"], 2)
                pe.wait_ge(S["scale_lo"], 2)

                def select(f, par, c, F):
                    if c or not first_tile(f):
                        pe.wait_ge(S["weight_done"], f * CHUNKS + c)
                    if c == 2:
                        pe.wait_ge(S["hot_copied"], f + 1)
                        hot = hot_tile[:, par, 0:F]
                        pe.matmul(zero_bank[0:F, :], hot, zero_dn[:, :], start=True, stop=True)
                        pe.matmul(scale_bank[0:F, :], hot, sch_dn[:, :], start=True, stop=False)
                        mm = pe.matmul(scale_bank[0:F, :], hot, scl_dn[:, :], start=False, stop=True)
                    else:
                        pe.sem_inc(S["own_pe"], 1)
                        for i in range(2):
                            hot = hot_gu[:, (2 * c + i) * P:(2 * c + i + 1) * P]
                            cols = bass.ds(f * P, F)
                            zo, so = (b[:, i * 2 * P:(i + 1) * 2 * P].rearrange("p (s n) -> p s n", s=2)[:, :, 0:F]
                                      for b in (zero_bank, scale_bank))
                            pe.matmul(zo, hot, zero_gu[:, :, cols], start=True, stop=True)
                            pe.matmul(so, hot, sch_gu[:, :, cols], start=True, stop=False)
                            mm = pe.matmul(so, hot, scl_gu[:, :, cols], start=False, stop=True)
                    mm.then_inc(S["selected"], 1)

                def down(f, par, half, F):
                    pe.wait_ge(S["w_lo"], f * CHUNKS + 3)
                    pe.wait_ge(S["h_lo"], f * 2 + (half + 1 + 2))
                    for b in range(4 * half, 4 * half + 4):
                        toks = slice(b * P, (b + 1) * P)
                        if b % 4 >= 2:
                            pe.wait_ge(S["added"], f * 8 + (b - 3 + 8))
                        mm = products(pe, dn_bank(b), three(hh[0:F, toks], hl[0:F, toks], dh[0:F, par, :], dl[0:F, par, :]))
                        mm.then_inc(S["dn"], 1)

                def body(f, par, F, F_next):
                    for h in range(2):
                        if F_next:
                            select(f + 1, 1 - par, h, F_next)
                        if h == 0:
                            pe.wait_ge(S["w_lo"], f * CHUNKS + 2)
                        pe.wait_ge(S["hid"], f * 2 + (h + 1))
                        pe.wait_ge(S["added"], f * 8 + (4 * h + 2))
                        cols = slice(h * HALF, (h + 1) * HALF)
                        for s in range(2):
                            pairs = [pr for k in range(KT) for pr in three(wh[:, par, k, s, 0:F], wl[:, par, k, s, 0:F],
                                                                           xh[:, k, cols], xl[:, k, cols])]
                            mm = products(pe, gu_bank[h][0:F, s * HALF:(s + 1) * HALF], pairs)
                        mm.then_inc(S["gu"], 1)
                        if h == 0 and not first_tile(f):
                            down(f - 1, 1 - par, 1, P)
                    if F_next:
                        select(f + 1, 1 - par, 2, F_next)
                    down(f, par, 0, F)

                for c in range(CHUNKS):
                    select(0, 0, c, P)
                turns(pe, body)
                down(FT - 1, 0, 1, F_LAST)


def lora_inputs(sb, io):
    t = {"wb": sb("m_wb", [P, KT, D]),
         "la": sb("m_la", [EXPERTS * RANK, D]),
         "wr": sb("m_wr", [EXPERTS, D]),
         "lb": sb("m_lb", [P, KT, EXPERTS, RANK]),
         "bias": sb("m_bias", [1, D]),
         "before": sb("m_before", [P, EXPERTS, EXPERTS])}
    loads = [(t["wb"][:, :, :], io["L1_ffn_W_base"].rearrange("(k p) d -> p k d", p=P)),
             (t["la"][:, :], io["L1_ffn_lora_A"].rearrange("e r d -> (e r) d")),
             (t["wr"][:, :], io["L1_ffn_W_router"]),
             (t["bias"][:, :], io["L1_ffn_b_base"].rearrange("(a n) -> a n", a=1)),
             (t["before"][:, :, :], io["before"])]
    loads += [(t["lb"][:, k, :, :], io["L1_ffn_lora_B"][:, k * P:(k + 1) * P, :].rearrange("e p r -> p e r")) for k in range(KT)]
    return t, loads


def lora_mixture(core, consts, acc, xh, xl, inputs):
    nc = core.nc
    ident, mask, eps, ones = consts
    ER = EXPERTS * RANK
    with core.stage("m") as sb:
        wb, la, wr, lb, bias, before = (inputs[n] for n in ("wb", "la", "wr", "lb", "bias", "before"))
        NW = D + ER + EXPERTS
        wth, wtl = sb("wth", [P, KT, NW], F32R), sb("wtl", [P, KT, NW], F32R)
        bth, btl = sb("bth", [ER, D], F32R), sb("btl", [ER, D], F32R)
        prob = sb("prob", [P, TB, EXPERTS])
        top = sb("top", [P, TB])
        tot = sb("tot", [P, TB])
        gt = sb("gt", [P, TB, EXPERTS, EXPERTS])
        eq = sb("eq", [P, TB, EXPERTS, EXPERTS])
        rank_of = sb("rank_of", [P, TB, EXPERTS])
        gated = sb("gated", [P, TB, EXPERTS])
        gates = sb("gates", [P, TB, EXPERTS, RANK])
        h = sb("h", [ER, T])
        hg = sb("hg", [ER, T])
        hth, htl = sb("hth", [ER, T], F32R), sb("htl", [ER, T], F32R)
        turned, hi, lo = core.sem("m_turned"), core.sem("m_hi"), core.sem("m_lo")
        route, r = core.sem("m_route"), core.sem("m_r")
        expd, spread = core.sem("m_expd"), core.sem("m_spread")
        logits = sb("logits", [EXPERTS, T])
        logits_done, logits_copied = core.sem("m_logits_done"), core.sem("m_logits_copied")
        h_done, h_copied, gates_turned = core.sem("m_h_done"), core.sem("m_h_copied"), core.sem("m_gates_turned")
        base, base_copied = core.sem("m_base"), core.sem("m_base_copied")
        ht, hth_ready, htl_ready = core.sem("m_ht"), core.sem("m_hth"), core.sem("m_htl")
        outs, copied = core.sem("m_outs"), core.sem("m_copied")
        with nc.Block() as block:

            pieces = [(k, slice(0, D), wth[:, k, 0:D], wtl[:, k, 0:D]) for k in range(KT)]
            pieces += [(KT, slice(0, HALF), wth[:, :, D:D + ER], wtl[:, :, D:D + ER])]
            pieces += [(KT + 1, slice(0, KT * EXPERTS), wth[:, :, D + ER:NW], wtl[:, :, D + ER:NW])]
            pieces += [(KT + 2, slice(0, D), bth[:, :], btl[:, :])]

            def lora_bank(b):
                return core.slots[b // 2 % 2][:, b % 2 * HALF:(b % 2 + 1) * HALF]

            def bank_view(n, cols):
                v = core.banks[n % 4][:, cols]
                if n == KT:
                    return v.rearrange("p (k c) -> p k c", k=KT)
                if n == KT + 1:
                    return v.rearrange("p (k c) -> p k c", k=KT)
                return v

            @block.scalar
            def _(act):
                for n, cols, h_, l_ in pieces:
                    act.wait_ge(turned, n + 1)
                    act.activation(h_, bank_view(n, cols), ACT.Copy).then_inc(hi, 1)
                act.wait_ge(logits_done, 1)
                act.activation(logits[:, :], core.slots[1][0:EXPERTS, :], ACT.Copy).then_inc(logits_copied, 1)
                act.wait_ge(r, 2)
                act.activation(prob[:, :, :], prob[:, :, :], ACT.Exp).then_inc(expd, 1)
                act.wait_ge(h_done, 1)
                act.activation(h[:, :], core.slots[0][:, :], ACT.Copy).then_inc(h_copied, 1)
                for b in range(TB):
                    if b == TB // 2:
                        act.wait_ge(ht, 1)
                        act.activation(hth[:, :], hg[:, :], ACT.Copy).then_inc(hth_ready, 1)
                    act.wait_ge(base, b + 1)
                    act.activation(acc[:, b, :], core.banks[b % 4][:, :], ACT.Copy).then_inc(base_copied, 1)

            @block.gpsimd
            def _(pool):
                pool.wait_ge(r, 14)
                pool.tensor_copy(gates[:, :, :, :], gated[:, :, :].unsqueeze(3).to_broadcast([P, TB, EXPERTS, RANK])).then_inc(spread, 1)

            @block.vector
            def _(dve):
                for n, cols, h_, l_ in pieces:
                    dve.wait_ge(hi, n + 1)
                    dve.tensor_tensor(l_, bank_view(n, cols), h_.bitcast(F32), ALU.subtract).then_inc(lo, 1)
                steps = [0]

                def step(ins):
                    steps[0] += 1
                    ins.then_inc(r, 1)
                    dve.wait_ge(r, steps[0])

                wide = lambda t: t[:, :, :].unsqueeze(3).to_broadcast([P, TB, EXPERTS, EXPERTS])
                across = lambda t: t[:, :, :].unsqueeze(2).to_broadcast([P, TB, EXPERTS, EXPERTS])
                dve.wait_ge(route, 1)
                step(dve.tensor_reduce(top[:, :], core.banks[3][:, 0:TB * EXPERTS].rearrange("p (b e) -> p b e", b=TB), AX.X, ALU.max))
                step(dve.tensor_tensor(prob[:, :, :], core.banks[3][:, 0:TB * EXPERTS].rearrange("p (b e) -> p b e", b=TB),
                                       top[:, :].unsqueeze(2).to_broadcast([P, TB, EXPERTS]), ALU.subtract))
                dve.wait_ge(expd, 1)
                step(dve.tensor_reduce(tot[:, :], prob[:, :, :], AX.X, ALU.add))
                step(dve.reciprocal(tot[:, :], tot[:, :]))
                step(dve.tensor_tensor(prob[:, :, :], prob[:, :, :], tot[:, :].unsqueeze(2).to_broadcast([P, TB, EXPERTS]), ALU.mult))
                step(dve.tensor_tensor(gt[:, :, :, :], across(prob), wide(prob), ALU.is_gt))
                step(dve.tensor_tensor(eq[:, :, :, :], across(prob), wide(prob), ALU.is_equal))
                step(dve.tensor_tensor(eq[:, :, :, :], eq[:, :, :, :],
                                       before[:, :, :].unsqueeze(1).to_broadcast([P, TB, EXPERTS, EXPERTS]), ALU.mult))
                step(dve.tensor_tensor(gt[:, :, :, :], gt[:, :, :, :], eq[:, :, :, :], ALU.add))
                step(dve.tensor_reduce(rank_of[:, :, :], gt[:, :, :, :], AX.X, ALU.add))
                step(dve.scalar_tensor_tensor(gated[:, :, :], rank_of[:, :, :], 2.0, prob[:, :, :], ALU.is_lt, ALU.mult))
                step(dve.tensor_reduce(tot[:, :], gated[:, :, :], AX.X, ALU.add))
                step(dve.reciprocal(tot[:, :], tot[:, :]))
                step(dve.scalar_tensor_tensor(gated[:, :, :], gated[:, :, :], LORA_SCALE,
                                              tot[:, :].unsqueeze(2).to_broadcast([P, TB, EXPERTS]), ALU.mult, ALU.mult))
                assert steps[0] == 14
                dve.wait_ge(h_copied, 1)
                dve.wait_ge(gates_turned, 1)
                dve.tensor_tensor(hg[:, :], h[:, :], core.slots[1][:, :], ALU.mult).then_inc(ht, 1)
                dve.wait_ge(hth_ready, 1)
                dve.tensor_tensor(htl[:, :], hg[:, :], hth[:, :].bitcast(F32), ALU.subtract).then_inc(htl_ready, 1)
                for b in range(TB):
                    dve.wait_ge(outs, b + 1)
                    dve.wait_ge(base_copied, b + 1)
                    dve.tensor_tensor(acc[:, b, :], acc[:, b, :], lora_bank(b), ALU.add).then_inc(copied, 1)

            @block.tensor
            def _(pe):
                for n in range(KT + 3):
                    if n >= 4:
                        pe.wait_ge(lo, n - 3)
                    bank = core.banks[n % 4]
                    for k in range(KT):
                        if n < KT:
                            t = pe.transpose(bank[:, k * P:(k + 1) * P], wb[:, k, n * P:(n + 1) * P], ident[:, :])
                        elif n == KT:
                            t = pe.transpose(bank[:, k * P:(k + 1) * P], la[:, k * P:(k + 1) * P], ident[:, :])
                        elif n == KT + 1:
                            t = pe.transpose(bank[:, k * EXPERTS:(k + 1) * EXPERTS], wr[:, k * P:(k + 1) * P],
                                             ident[0:EXPERTS, 0:EXPERTS])
                        else:
                            t = pe.transpose(bank[:, k * P:(k + 1) * P],
                                             lb[:, k, :, :].rearrange("p e r -> p (e r)"), ident[:, :])
                    t.then_inc(turned, 1)
                pe.wait_ge(lo, KT + 3)
                x_of = lambda k, toks: (xh[:, k, toks], xl[:, k, toks])
                def turned_product(out, c0, c1):
                    for n in range(2):
                        cols = slice(n * HALF, (n + 1) * HALF)
                        mm = products(pe, out[:, cols], [pr for k in range(KT) for pr in three(wth[:, k, c0:c1], wtl[:, k, c0:c1],
                                                                                             *x_of(k, cols))])
                    return mm

                turned_product(core.slots[1][0:EXPERTS, :], D + ER, NW).then_inc(logits_done, 1)
                turned_product(core.slots[0], D, D + ER).then_inc(h_done, 1)
                pe.wait_ge(logits_copied, 1)
                for b in range(TB):
                    t = pe.transpose(core.banks[3][:, b * EXPERTS:(b + 1) * EXPERTS], logits[:, b * P:(b + 1) * P],
                                     ident[0:EXPERTS, 0:EXPERTS])
                t.then_inc(route, 1)
                for b in range(TB):
                    toks = slice(b * P, (b + 1) * P)
                    if b >= 4:
                        pe.wait_ge(base_copied, b - 3)
                    if b == 3:
                        pe.wait_ge(r, 2)
                    if b == TB // 2:
                        pe.wait_ge(spread, 1)
                        for a in range(TB):
                            t = pe.transpose(core.slots[1][:, a * P:(a + 1) * P],
                                             gates[:, a, :, :].rearrange("p e r -> p (e r)"), ident[:, :])
                        t.then_inc(gates_turned, 1)
                    products(pe, core.banks[b % 4][:, :],
                             [pr for k in range(KT) for pr in three(*x_of(k, toks), wth[:, k, 0:D], wtl[:, k, 0:D])], True, False)
                    mm = pe.matmul(core.banks[b % 4][:, :], ones[0:1, :], bias[0:1, :], start=False, stop=True)
                    mm.then_inc(base, 1)
                pe.wait_ge(htl_ready, 1)
                for b in range(TB):
                    toks = slice(b * P, (b + 1) * P)
                    if b >= 4:
                        pe.wait_ge(copied, b - 3)
                    products(pe, lora_bank(b), three(hth[:, toks], htl[:, toks], bth[:, :], btl[:, :])).then_inc(outs, 1)


def program(nc, io, out):
    with ExitStack() as ctx:
        core = Core(nc, ctx)
        sb = lambda n, shape, dt=F32: ctx.enter_context(nc.sbuf_tensor(n, shape, dt))
        ident, mask, eps, ones = sb("ident", [P, P]), sb("mask", [P, T]), sb("eps", [P, 1]), sb("ones", [P, P])
        consts = (ident, mask, eps, ones)
        acc = sb("acc", [P, TB, D])
        x_scr = [nc.dram_tensor(f"x_after_{i}", (T, D), F32).ap() for i in range(3)]
        q_scr = nc.dram_tensor("q_parts", (2, D, T), F32).ap()
        k_scr = nc.dram_tensor("k_parts", (2, P, T), F32).ap()
        constants(core, consts, io["ident"], io["mask"])
        resid = io["L0_attn_resid"].rearrange("b t d -> (b t) d")
        with nc.sbuf_tensor("v0", [P, TB, P], F32R) as v0, nc.sbuf_tensor("v0l", [P, TB, P], F32R) as v0l:
            with nc.sbuf_tensor("xh0", [P, KT, T], F32R) as xh, nc.sbuf_tensor("xl0", [P, KT, T], F32R) as xl:
                with nc.sbuf_tensor("w0", [P, KT, Layer0Weights.NW], F32) as raw, nc.sbuf_tensor("cos", [P, T], F32) as cos, \
                        nc.sbuf_tensor("sin", [P, T], F32) as sin:
                    weights = Layer0Weights(raw, cos, sin, io)
                    seam(core, "s0", consts, acc, xh, xl, resid, None, False, False, weights.loads, weights.swap)
                    project_layer0(core, consts, xh, xl, weights, q_scr, k_scr, v0, v0l)
            attention(core, "a0", 0, consts, acc, None, None,
                      {"q": q_scr, "k": k_scr, "v0": v0, "v0l": v0l, "wo": io["L0_attn_Wo"]})
        xh, xl = sb("xh", [P, KT, T], F32R), sb("xl", [P, KT, T], F32R)
        with ExitStack() as ctx_f:
            inputs, loads = swiglu_inputs(lambda n, shape, dt=F32: ctx_f.enter_context(nc.sbuf_tensor(n, shape, dt)), io)
            seam(core, "s1", consts, acc, xh, xl, resid, x_scr[0], True, False, loads)
            swiglu(core, consts, acc, xh, xl, inputs,
                   {"qgu": io["L0_ffn_qweight_gu"], "qdn": io["L0_ffn_qweight_down"]})
        with nc.sbuf_tensor("wq_raw", [P, 2, KT, P], F32) as wq_raw, nc.sbuf_tensor("wkv_raw", [P, KT, 2 * P], F32) as wkv_raw:
            loads = [(wkv_raw[:, :, i * P:(i + 1) * P], io[f"L1_attn_w_{w}"].rearrange("(k p) n -> p k n", p=P)[:, :, 0:P])
                     for i, w in enumerate("kv")]
            loads += [(wq_raw[:, j, :, :], io["L1_attn_w_q"].rearrange("(k p) n -> p k n", p=P)[:, :, j * P:(j + 1) * P])
                      for j in range(2)]
            seam(core, "s2", consts, acc, xh, xl, x_scr[0], x_scr[1], True, False, loads)
            attention(core, "a1", 1, consts, acc, xh, xl,
                      {"wq": io["L1_attn_w_q"], "wk": io["L1_attn_w_k"], "wv": io["L1_attn_w_v"], "wo": io["L1_attn_w_o"],
                       "wq_raw": wq_raw, "wkv_raw": wkv_raw})
        inputs, loads = lora_inputs(sb, io)
        seam(core, "s3", consts, acc, xh, xl, x_scr[1], x_scr[2], True, False, loads)
        lora_mixture(core, consts, acc, xh, xl, inputs)
        seam(core, "s4", consts, acc, xh, xl, x_scr[2], out.rearrange("b t d -> (b t) d"), True, True)


def shape_constants():
    import math

    import numpy as np

    f32 = np.float32
    i = np.arange(0, DH0, 2, dtype=f32) / f32(DH0)
    freq = (f32(1.0 / (2.0 * math.pi)) * f32(500000.0) ** (-i)).astype(f32)
    factor, lo, hi, context = 32.0, 1.0, 4.0, 1024
    scaled = np.where(freq < f32(lo / context), freq / f32(factor), freq)
    smooth = np.clip((f32(context) * freq - f32(lo)) / f32(hi - lo), f32(0), f32(1))
    mixed = (f32(1) - smooth) * (freq / f32(factor)) + smooth * freq
    mid = (freq >= f32(lo / context)) & (freq <= f32(hi / context))
    freq = np.where(mid, mixed, scaled).astype(f32)
    phase = (f32(2.0 * math.pi) * np.arange(T).astype(f32)[:, None] * freq[None, :]).astype(f32)
    cos, sin = np.cos(phase).T, np.sin(phase).T
    return {
        "cos": np.ascontiguousarray(np.tile(np.concatenate([cos, cos]), (P // DH0, 1)), dtype=f32),
        "sin": np.ascontiguousarray(np.tile(np.concatenate([-sin, sin]), (P // DH0, 1)), dtype=f32),
        "ident": np.eye(P, dtype=f32),
        "mask": np.concatenate([np.zeros((P, T - P), f32), np.triu(np.full((P, P), MASKED, f32), 1)], axis=1),
        "shift": (4 * (np.arange(P) % NIBBLES)).astype(np.uint32)[:, None],
        "group": np.arange(DN_GROUPS, dtype=f32)[:, None],
        "before": np.ascontiguousarray(np.broadcast_to(np.tril(np.ones((EXPERTS, EXPERTS), f32), -1), (P, EXPERTS, EXPERTS))),
    }


_INS = ["L0_attn_resid", "L0_attn_Wq", "L0_attn_Wk", "L0_attn_Wv", "L0_attn_Wo", "L0_ffn_qweight_gu",
        "L0_ffn_qzeros_gu", "L0_ffn_scales_gu", "L0_ffn_g_idx_gu", "L0_ffn_qweight_down", "L0_ffn_qzeros_down",
        "L0_ffn_scales_down", "L0_ffn_g_idx_down", "L1_attn_w_q", "L1_attn_w_k", "L1_attn_w_v", "L1_attn_w_o",
        "L1_ffn_W_base", "L1_ffn_b_base", "L1_ffn_W_router", "L1_ffn_lora_A", "L1_ffn_lora_B"]


def kernel(**inputs):
    import numpy as np

    import concourse.bacc as bacc
    from concourse.bass_utils import run_bass_kernel_spmd

    nc = bacc.Bacc("TRN2", target_bir_lowering=False, num_devices=1)
    arrays = {name: np.ascontiguousarray(inputs[name]) for name in _INS}
    arrays.update(shape_constants())
    fed = {f"in_{name}": a for name, a in arrays.items()}
    io = {name: nc.dram_tensor(f"in_{name}", a.shape, mybir.dt.from_np(a.dtype), kind="ExternalInput").ap()
          for name, a in arrays.items()}
    out = nc.dram_tensor("out_x", (1, T, D), F32, kind="ExternalOutput").ap()
    program(nc, io, out)
    got = run_bass_kernel_spmd(nc, [fed], core_ids=[0])
    return got.results[0]["out_x"]
```
